# Optimizing a Trainium2 kernel written in Bass

```python
import numpy as np
import jax
import jax.numpy as jnp

def _softmax(x, axis=-1):
    return jax.nn.softmax(x, axis=axis)

def _gelu(x):
    return jax.nn.gelu(x, approximate=True)

def _silu(x):
    return jax.nn.silu(x)

def _sigmoid(x):
    return jax.nn.sigmoid(x)

def _layernorm(x, axis=-1, eps=1e-05):
    m = jnp.mean(x, axis=axis, keepdims=True)
    v = jnp.var(x, axis=axis, keepdims=True)
    return (x - m) / jnp.sqrt(v + eps)

def _scatter_add(tgt, idx, src, axis=0):
    return tgt.at[idx].add(src)

def _segment_sum(src, seg, n):
    return jax.ops.segment_sum(src, seg, n)
kernel_name = 'mk_adaln_attn_ffn_d1_seqx_r4_54a91e'

def setup_inputs(seed: int=0):
    np.random.seed(seed)
    _w = jnp.asarray

    def _rec_inputs():
        import jax
        import jax.numpy as jnp
        _rk = jax.random.key(seed)
        x = -0.000125 + 0.9999 * jax.random.normal(jax.random.fold_in(_rk, 1), (32, 256, 256), jnp.float32)
        _lenS = 256 - jax.random.randint(jax.random.fold_in(_rk, 7), (32,), 0, max(1, 256 // 4) + 1, jnp.int32)
        _lenS2 = 256 - jax.random.randint(jax.random.fold_in(_rk, 8), (32,), 0, max(1, 256 // 4) + 1, jnp.int32)
        cond_1024 = 0.00782532 + 1.00527 * jax.random.normal(jax.random.fold_in(_rk, 11), (32, 256), jnp.float32)
        return (x, cond_1024)
    x, cond_1024 = _rec_inputs()

    def _L0_cond_setup():
        import jax, jax.numpy as jnp
        import numpy as np
        INV_SQRT2 = 0.7071067811865476
        key = jax.random.key(seed)
        k1, k2, k3, k4 = jax.random.split(key, 4)
        B, N, d = (8, 1024, 256)
        scale = 1.0 / np.sqrt(d)
        return {'v': jax.random.normal(k1, (B, N, d), dtype=jnp.float32), 'q_pool': jax.random.normal(k2, (B, d), dtype=jnp.float32), 'W1': jax.random.normal(k3, (d, d), dtype=jnp.float32) * scale, 'b1': jnp.zeros((d,), dtype=jnp.float32), 'W2': jax.random.normal(k4, (d, d), dtype=jnp.float32) * scale, 'b2': jnp.zeros((d,), dtype=jnp.float32)}
    _L0_cond_all = _L0_cond_setup()
    _L0_cond_in = {k: v for k, v in _L0_cond_all.items() if k in ('W1', 'b1', 'W2', 'b2')}
    del _L0_cond_all

    def _L0_attn_setup():
        import jax, jax.numpy as jnp
        import numpy as np
        import math
        B, S, D = (8, 512, 256)

        def _trunc_normal(key, shape, fan_in, fan_out):
            std = math.sqrt(2.0 / (fan_in + fan_out))
            return jax.random.truncated_normal(key, -3.0, 3.0, shape, jnp.float32) * std
        key = jax.random.key(seed)
        kx, kq, kk, kv, ko = jax.random.split(key, 5)
        return {'in_features': jax.random.normal(kx, (B, S, D), jnp.float32), 'Wq': _trunc_normal(kq, (D, D), D, D), 'Wk': _trunc_normal(kk, (D, D), D, D), 'Wv': _trunc_normal(kv, (D, D), D, D), 'Wo': _trunc_normal(ko, (D, D), D, D)}
    _L0_attn_all = _L0_attn_setup()
    _L0_attn_in = {k: v for k, v in _L0_attn_all.items() if k in ('Wq', 'Wk', 'Wv', 'Wo')}
    del _L0_attn_all

    def _L0_cond2_setup():
        import jax, jax.numpy as jnp
        import numpy as np
        B, T, D = (128, 32, 256)
        ADA, INTER, RANK = (256, 256, 8)
        LN_EPS = 1e-05

        def _layernorm(x, g, b):
            mu = jnp.mean(x, axis=-1, keepdims=True)
            var = jnp.var(x, axis=-1, keepdims=True)
            return (x - mu) * jax.lax.rsqrt(var + LN_EPS) * g + b
        key = jax.random.key(seed)
        ks = jax.random.split(key, 9)
        return {'x': jax.random.normal(ks[0], (B, T, D), dtype=jnp.float32), 'ada_emb': jax.random.normal(ks[1], (B, ADA), dtype=jnp.float32), 'base_layer': jax.random.normal(ks[2], (D, D), dtype=jnp.float32), 'w1': jax.random.normal(ks[3], (ADA, INTER), dtype=jnp.float32) * 0.02, 'b1': jnp.zeros((INTER,), dtype=jnp.float32), 'w2': jax.random.normal(ks[4], (INTER, 2 * D * RANK), dtype=jnp.float32) * 0.02, 'b2': jnp.zeros((2 * D * RANK,), dtype=jnp.float32), 'ln_g': jnp.ones((ADA,), dtype=jnp.float32), 'ln_b': jnp.zeros((ADA,), dtype=jnp.float32)}
    _L0_cond2_all = _L0_cond2_setup()
    _L0_cond2_in = {k: v for k, v in _L0_cond2_all.items() if k in ('base_layer', 'w1', 'b1', 'w2', 'b2', 'ln_g', 'ln_b')}
    del _L0_cond2_all

    def _L0_ffn_setup():
        import jax, jax.numpy as jnp
        import numpy as np
        NH, NKV, E, K = (16, 4, 8, 2)
        CAP_FACTOR = 1.25
        LN_EPS = 1e-05

        def _layer_norm(x, w, b):
            mu = jnp.mean(x, axis=-1, keepdims=True)
            var = jnp.mean(jnp.square(x - mu), axis=-1, keepdims=True)
            return (x - mu) * jax.lax.rsqrt(var + LN_EPS) * w + b
        key = jax.random.key(seed)
        ks = jax.random.split(key, 6)
        S, B, H, F = (512, 1, 256, 512)
        HD = H // NH
        qkv_out = NKV * (NH // NKV + 2) * HD
        f32 = jnp.float32
        return {'hidden_states': jax.random.normal(ks[0], (S, B, H), f32), 'ln1_weight': jnp.ones((H,), f32), 'ln1_bias': jnp.zeros((H,), f32), 'ln2_weight': jnp.ones((H,), f32), 'ln2_bias': jnp.zeros((H,), f32), 'qkv_weight': jax.random.normal(ks[1], (qkv_out, H), f32) * 0.02, 'proj_weight': jax.random.normal(ks[2], (H, H), f32) * 0.02, 'router_weight': jax.random.normal(ks[3], (H, E), f32) * 0.02, 'moe_w1': jax.random.normal(ks[4], (E, H, F), f32) * 0.02, 'moe_w2': jax.random.normal(ks[5], (F and E, F, H), f32)[:E] * 0.02 if False else jax.random.normal(ks[5], (E, F, H), f32) * 0.02}
    _L0_ffn_all = _L0_ffn_setup()
    _L0_ffn_in = {k: v for k, v in _L0_ffn_all.items() if k in ('ln1_weight', 'ln1_bias', 'ln2_weight', 'ln2_bias', 'qkv_weight', 'proj_weight', 'router_weight', 'moe_w1', 'moe_w2')}
    del _L0_ffn_all
    return {'x': x, 'cond_1024': cond_1024, 'L0_cond_W1': _L0_cond_in['W1'], 'L0_cond_b1': _L0_cond_in['b1'], 'L0_cond_W2': _L0_cond_in['W2'], 'L0_cond_b2': _L0_cond_in['b2'], 'L0_attn_Wq': _L0_attn_in['Wq'], 'L0_attn_Wk': _L0_attn_in['Wk'], 'L0_attn_Wv': _L0_attn_in['Wv'], 'L0_attn_Wo': _L0_attn_in['Wo'], 'L0_cond2_base_layer': _L0_cond2_in['base_layer'], 'L0_cond2_w1': _L0_cond2_in['w1'], 'L0_cond2_b1': _L0_cond2_in['b1'], 'L0_cond2_w2': _L0_cond2_in['w2'], 'L0_cond2_b2': _L0_cond2_in['b2'], 'L0_cond2_ln_g': _L0_cond2_in['ln_g'], 'L0_cond2_ln_b': _L0_cond2_in['ln_b'], 'L0_ffn_ln1_weight': _L0_ffn_in['ln1_weight'], 'L0_ffn_ln1_bias': _L0_ffn_in['ln1_bias'], 'L0_ffn_ln2_weight': _L0_ffn_in['ln2_weight'], 'L0_ffn_ln2_bias': _L0_ffn_in['ln2_bias'], 'L0_ffn_qkv_weight': _L0_ffn_in['qkv_weight'], 'L0_ffn_proj_weight': _L0_ffn_in['proj_weight'], 'L0_ffn_router_weight': _L0_ffn_in['router_weight'], 'L0_ffn_moe_w1': _L0_ffn_in['moe_w1'], 'L0_ffn_moe_w2': _L0_ffn_in['moe_w2']}

def reference(x, cond_1024, L0_cond_W1, L0_cond_b1, L0_cond_W2, L0_cond_b2, L0_attn_Wq, L0_attn_Wk, L0_attn_Wv, L0_attn_Wo, L0_cond2_base_layer, L0_cond2_w1, L0_cond2_b1, L0_cond2_w2, L0_cond2_b2, L0_cond2_ln_g, L0_cond2_ln_b, L0_ffn_ln1_weight, L0_ffn_ln1_bias, L0_ffn_ln2_weight, L0_ffn_ln2_bias, L0_ffn_qkv_weight, L0_ffn_proj_weight, L0_ffn_router_weight, L0_ffn_moe_w1, L0_ffn_moe_w2):
    import jax
    import jax.numpy as jnp

    def _L0_cond_ref(v, q_pool, W1, b1, W2, b2):
        import jax, jax.numpy as jnp
        import numpy as np
        INV_SQRT2 = 0.7071067811865476
        B, N, d = v.shape
        h = jax.nn.silu(q_pool @ W1.T + b1)
        gate = jax.nn.sigmoid(h @ W2.T + b2)[:, None, :]
        levels = int(np.log2(N))
        a = v
        details = []
        for _ in range(levels):
            e, o = (a[:, 0::2], a[:, 1::2])
            details.append((e - o) * INV_SQRT2)
            a = (e + o) * INV_SQRT2
        a = a * gate
        for dc in reversed(details):
            dc = dc * gate
            e = (a + dc) * INV_SQRT2
            o = (a - dc) * INV_SQRT2
            n = e.shape[1]
            a = jnp.stack([e, o], axis=2).reshape(B, 2 * n, d)
        return v + a

    def _L0_attn_ref(in_features, Wq, Wk, Wv, Wo):
        import jax, jax.numpy as jnp
        import numpy as np
        import math
        B, S, D = (8, 512, 256)

        def _trunc_normal(key, shape, fan_in, fan_out):
            std = math.sqrt(2.0 / (fan_in + fan_out))
            return jax.random.truncated_normal(key, -3.0, 3.0, shape, jnp.float32) * std
        d_k = Wq.shape[0]
        scale = 1.0 / math.sqrt(d_k)
        x = in_features
        Q = x @ Wq.T
        K = x @ Wk.T
        V = x @ Wv.T
        scores = jnp.einsum('bqd,bkd->bqk', Q, K) * scale
        seq_len = x.shape[-2]
        causal = jnp.tril(jnp.ones((seq_len, seq_len), dtype=bool))
        scores = jnp.where(causal, scores, -jnp.inf)
        attn = jax.nn.softmax(scores, axis=-1)
        out = jnp.einsum('bqk,bkd->bqd', attn, V)
        return out @ Wo.T

    def _L0_cond2_ref(x, ada_emb, base_layer, w1, b1, w2, b2, ln_g, ln_b):
        import jax, jax.numpy as jnp
        import numpy as np
        B, T, D = (128, 32, 256)
        ADA, INTER, RANK = (256, 256, 8)
        LN_EPS = 1e-05

        def _layernorm(x, g, b):
            mu = jnp.mean(x, axis=-1, keepdims=True)
            var = jnp.var(x, axis=-1, keepdims=True)
            return (x - mu) * jax.lax.rsqrt(var + LN_EPS) * g + b
        b, t, d = x.shape
        ae = _layernorm(ada_emb, ln_g, ln_b)
        h = jax.nn.gelu(ae @ w1 + b1, approximate=False)
        xw = h @ w2 + b2
        x_a, x_b = jnp.split(xw, 2, axis=-1)
        x_a = x_a.reshape(b, d, RANK)
        x_b = x_b.reshape(b, d, RANK)
        layer = base_layer[None, :, :] + jnp.einsum('bdr,bkr->bdk', x_a, x_b)
        out = jnp.einsum('btc,bco->bto', x, layer)
        return x + out

    def _L0_ffn_ref(hidden_states, ln1_weight, ln1_bias, ln2_weight, ln2_bias, qkv_weight, proj_weight, router_weight, moe_w1, moe_w2):
        import jax, jax.numpy as jnp
        import numpy as np
        NH, NKV, E, K = (16, 4, 8, 2)
        CAP_FACTOR = 1.25
        LN_EPS = 1e-05

        def _layer_norm(x, w, b):
            mu = jnp.mean(x, axis=-1, keepdims=True)
            var = jnp.mean(jnp.square(x - mu), axis=-1, keepdims=True)
            return (x - mu) * jax.lax.rsqrt(var + LN_EPS) * w + b
        S, B, H = hidden_states.shape
        HD = H // NH
        q_per_kv = NH // NKV
        ln1 = _layer_norm(hidden_states, ln1_weight, ln1_bias)
        qkv = jnp.einsum('sbh,oh->sbo', ln1, qkv_weight)
        qkv = qkv.reshape(S, B, NKV, (q_per_kv + 2) * HD)
        q = qkv[..., :q_per_kv * HD].reshape(S, B, NH, HD)
        k = qkv[..., q_per_kv * HD:(q_per_kv + 1) * HD]
        v = qkv[..., (q_per_kv + 1) * HD:]
        qb = jnp.transpose(q, (1, 2, 0, 3)).reshape(B, NKV, q_per_kv, S, HD)
        kb = jnp.transpose(k, (1, 2, 0, 3))
        vb = jnp.transpose(v, (1, 2, 0, 3))
        scale = 1.0 / np.sqrt(HD).astype(np.float32)
        scores = jnp.einsum('bgqsd,bgtd->bgqst', qb, kb) * scale
        causal = jnp.tril(jnp.ones((S, S), bool))
        scores = jnp.where(causal, scores, jnp.finfo(scores.dtype).min)
        attn = jax.nn.softmax(scores, axis=-1)
        ao = jnp.einsum('bgqst,bgtd->bgqsd', attn, vb)
        ao = ao.reshape(B, NH, S, HD)
        ao = jnp.transpose(ao, (2, 0, 1, 3)).reshape(S, B, H)
        proj = jnp.einsum('sbh,oh->sbo', ao, proj_weight)
        h1 = hidden_states + proj
        ln2 = _layer_norm(h1, ln2_weight, ln2_bias)
        x = ln2.reshape(-1, H)
        N = x.shape[0]
        logits = x @ router_weight
        probs = jax.nn.softmax(logits, axis=-1)
        top_p, top_i = jax.lax.top_k(probs, K)
        top_p = top_p / jnp.sum(top_p, axis=-1, keepdims=True)
        exp_idx = top_i.reshape(-1)
        exp_p = top_p.reshape(-1)
        order = jnp.argsort(exp_idx, stable=True)
        sorted_exp = exp_idx[order]
        counts = jnp.bincount(exp_idx, length=E)
        offsets = jnp.concatenate([jnp.zeros((1,), counts.dtype), jnp.cumsum(counts)[:-1]])
        within = jnp.arange(N * K) - offsets[sorted_exp]
        cap = int(np.ceil(N * K / E * CAP_FACTOR))
        T = E * cap
        valid = within < cap
        dst = jnp.where(valid, sorted_exp * cap + within, T)
        padded_tokens = jnp.zeros((T, H), x.dtype).at[dst].set(x[order // K], mode='drop')
        padded_probs = jnp.zeros((T,), exp_p.dtype).at[dst].set(exp_p[order], mode='drop')
        padded_tid = jnp.zeros((T,), jnp.int32).at[dst].set((order // K).astype(jnp.int32), mode='drop')
        xt = padded_tokens.reshape(E, cap, H)
        fc1 = jax.nn.gelu(jnp.einsum('ech,ehf->ecf', xt, moe_w1))
        fc2 = jnp.einsum('ecf,efh->ech', fc1, moe_w2).reshape(T, H)
        weighted = fc2 * padded_probs[:, None]
        moe_out = jnp.zeros((N, H), hidden_states.dtype).at[padded_tid].add(weighted)
        return h1 + moe_out.reshape(S, B, H)
    x = x + _L0_attn_ref(_L0_cond_ref(x, cond_1024, L0_cond_W1, L0_cond_b1, L0_cond_W2, L0_cond_b2), L0_attn_Wq, L0_attn_Wk, L0_attn_Wv, L0_attn_Wo)
    x = x + _L0_ffn_ref(_L0_cond2_ref(x, cond_1024, L0_cond2_base_layer, L0_cond2_w1, L0_cond2_b1, L0_cond2_w2, L0_cond2_b2, L0_cond2_ln_g, L0_cond2_ln_b), L0_ffn_ln1_weight, L0_ffn_ln1_bias, L0_ffn_ln2_weight, L0_ffn_ln2_bias, L0_ffn_qkv_weight, L0_ffn_proj_weight, L0_ffn_router_weight, L0_ffn_moe_w1, L0_ffn_moe_w2)
    return x

_drawn_inputs = setup_inputs


def setup_inputs(seed=0):
    import zlib

    import numpy as np

    out = dict(_drawn_inputs(seed))
    spreads = {'L0_cond_b1': (0.0, 0.627),
     'L0_cond_b2': (0.0, 0.461),
     'L0_cond2_b1': (0.0, 0.8),
     'L0_cond2_b2': (0.0, 0.1),
     'L0_cond2_ln_g': (1.0, 0.6),
     'L0_cond2_ln_b': (0.0, 0.8),
     'L0_ffn_ln1_weight': (1.0, 0.6),
     'L0_ffn_ln1_bias': (0.0, 0.8),
     'L0_ffn_ln2_weight': (1.0, 0.6),
     'L0_ffn_ln2_bias': (0.0, 0.8)}
    factors = {'L0_ffn_qkv_weight': 8.0,
     'L0_ffn_proj_weight': 8.0,
     'L0_ffn_router_weight': 8.0,
     'L0_ffn_moe_w1': 8.0,
     'L0_ffn_moe_w2': 8.0}
    for name, (base, spread) in spreads.items():
        noise = np.random.default_rng([zlib.crc32(name.encode()), seed]).standard_normal(out[name].shape)
        drawn = base * np.exp(spread * noise) if base else spread * noise
        out[name] = jnp.asarray(drawn.astype(out[name].dtype))
    for name, factor in factors.items():
        out[name] = (out[name] * factor).astype(out[name].dtype)
    return out
```

```python
from contextlib import ExitStack

import numpy as np
import concourse.bass as bass
from concourse import mybir

F32 = mybir.dt.float32
BF16 = mybir.dt.bfloat16
I32 = mybir.dt.int32
ALU = mybir.AluOpType
ACT = mybir.ActivationFunctionType
AX = mybir.AxisListType

P = 128
S, T, D = 32, 256, 256
DC = D // P
TC = T // P
RANK = 8
NH, NKV, HD = 16, 4, 16
JQ = NH // NKV
QKV = NKV * (JQ + 2) * HD
E, K, F = 8, 2, 512
FC = F // P
N = S * T
CAP = -(-N * K * 5 // (E * 4))
U1 = 4
I1 = S // U1
TG = P // S
G = T // TG
U2 = 4
I2 = G // U2
BT = 512
NB = CAP // BT
ROW = D + 1 + E
LN_EPS = 1e-5
NEG = -1e30
NO_ROW = 1 << 20
RSQRT_MAGIC = float(0x5F3759DF)
NEWTON = 3
EMPTYING = 4

C_ID, C_TRI, C_ORDER, C_SAME, C_WITHIN = 0, P, 2 * P, 3 * P, 4 * P
C_CAUSAL = 5 * P
C_HEAD = C_CAUSAL + S
C_SEL = C_HEAD + NKV
C_TIE = C_SEL + P // RANK
C_BASE = C_TIE + E
C_RESET = C_BASE + E
C_N = C_RESET + E * G


def constants():
    p = np.arange(P)
    s, t = p % S, p // S
    c = np.zeros((P, C_N), np.float32)
    c[:, C_ID:C_ID + P] = np.eye(P)
    c[:, C_TRI:C_TRI + P] = np.where(p[None, :] > p[:, None], NEG, 0)
    c[:, C_ORDER:C_ORDER + P] = s[:, None] < s[None, :]
    c[:, C_SAME:C_SAME + P] = s[:, None] == s[None, :]
    c[:, C_WITHIN:C_WITHIN + P] = (s[:, None] == s[None, :]) & (t[:, None] < t[None, :])
    c[:, C_CAUSAL:C_CAUSAL + S] = np.where(np.arange(S)[None, :] > s[:, None], NEG, 0)
    c[:, C_HEAD:C_HEAD + NKV] = (p[:, None] % (NKV * HD)) // HD == np.arange(NKV)
    c[:, C_SEL:C_SEL + P // RANK] = p[:, None] // RANK == np.arange(P // RANK)
    c[:, C_TIE:C_TIE + E] = E - np.arange(E)
    c[:, C_BASE:C_BASE + E] = np.arange(E) * CAP
    c[:, C_RESET:C_RESET + E * G] = np.tile(np.arange(G) > 0, E)
    tok = (p[:, None] + np.arange(G)[None, :] * P).astype(np.int32)
    return c, tok


class Chain:

    def __init__(self, eng, sem, base=0):
        self.eng, self.sem, self.base, self.n = eng, sem, base, 0

    def step(self, ins):
        ins.then_inc(self.sem, 1)
        self.n += 1

    def wait(self):
        self.eng.wait_ge(self.sem, self.base + self.n)

    def link(self, ins):
        self.step(ins)
        self.wait()


def inverse_root(nc, chain, var, tmp, seed):
    v, a, y0, y1 = (tmp[:, k] for k in range(4))
    chain.link(nc.vector.tensor_scalar(v, var, LN_EPS, None, ALU.add))
    chain.link(nc.vector.tensor_single_scalar(seed, v.bitcast(I32), 1, ALU.logical_shift_right))
    chain.link(nc.vector.tensor_scalar(y1.bitcast(I32), seed, -1.0, RSQRT_MAGIC, ALU.mult, ALU.add))
    old, new = y1, y0
    for _ in range(NEWTON):
        chain.link(nc.vector.tensor_tensor(a, old, old, ALU.mult))
        chain.link(nc.vector.scalar_tensor_tensor(a, a, -0.5, v, ALU.mult, ALU.mult))
        chain.link(nc.vector.scalar_tensor_tensor(new, a, 1.5, old, ALU.add, ALU.mult))
        old, new = new, old
    return old


class Program:

    def __init__(self, nc, ctx, dram):
        self.nc, self.ctx, self.d = nc, ctx, dram
        sb = lambda name, shape, dt=F32: ctx.enter_context(nc.sbuf_tensor(name, shape, dt))
        self.cst = sb("cst", [P, C_N])
        self.ident = self.cst[:, C_ID:C_ID + P]
        self.identb = sb("identb", [P, P], BF16)
        self.trib = sb("trib", [P, P], BF16)
        self.causalb = sb("causalb", [P, TG, NKV, S], BF16)
        self.gate = sb("gate", [P, DC, S])
        self.Wa = sb("Wa", [P, DC, D])
        self.Wc = sb("Wc", [P, DC, D])
        self.base = sb("base", [P, DC, D])
        self.xa = sb("xa", [P, DC, 2, P])
        self.xb = sb("xb", [P, 2, D])
        self.wqkv = sb("wqkv", [P, DC, QKV])
        self.wproj = sb("wproj", [P, DC, D])
        self.wroute = sb("wroute", [P, DC, E])
        self.ln1 = sb("ln1", [P, 2, DC])
        self.ln2 = sb("ln2", [P, 2, DC])
        self.tok = sb("tok", [P, G], I32)
        self.empty = sb("empty", [P, ROW])
        self.sem = lambda name: ctx.enter_context(nc.semaphore(name))
        self.passed = self.sem("passed")
        self.emptied = self.sem("emptied")
        self.x12 = nc.dram_tensor("x12_rows", (T, S, 2, D), F32, kind="Internal").ap()
        self.slots = nc.dram_tensor("slot_rows", (E * CAP + BT, ROW), F32, kind="Internal").ap()


def setup(pr):
    nc, d = pr.nc, pr.d
    with ExitStack() as ctx:
        sb = lambda name, shape, dt=F32: ctx.enter_context(nc.sbuf_tensor(name, shape, dt))
        sem = pr.sem
        ps = [ctx.enter_context(nc.psum_tensor(f"setup_ps{k}", [P, 512], F32)) for k in range(8)]
        cond = sb("cond", [S, D])
        condn = sb("condn", [S, D])
        w = {k: sb(f"s_{k}", [P, DC, D]) for k in ("Wq", "Wk", "Wv", "w1")}
        W1T, W2T, WoT = (sb(n, [P, DC, D]) for n in ("W1T", "W2T", "WoT"))
        w2 = sb("w2", [P, DC, 2 * D * RANK])
        vec = {k: sb(f"s_{k}", [P, DC]) for k in ("b1", "b2", "c2b1", "lng", "lnb")}
        b2c = sb("b2c", [P, 2, DC, RANK])
        condT, aeT, z, ez, hs, h2 = (sb(n, [P, DC, S]) for n in ("condT", "aeT", "z", "ez", "hs", "h2"))
        xbT = sb("xbT", [P, DC, 2, P])
        stats = sb("stats", [S, 6])
        mv = sb("mv", [S, 2])
        tmp = sb("tmp", [S, 4, 1])
        seed = sb("seed", [S, 1], I32)
        loaded, dve = sem("loaded"), sem("setup_dve")
        events = {}

        def event(name):
            if name not in events:
                events[name] = sem(f"done_{name}")
            return events[name]

        chunked = lambda a: a.rearrange("(c p) n -> p c n", p=P)
        block = ctx.enter_context(nc.Block())

        loads = [
            (cond[:], d["cond_1024"]), (pr.cst[:], d["cst"]), (pr.tok[:], d["tok"]),
            (W1T[:], d["L0_cond_W1"]), (W2T[:], d["L0_cond_W2"]), (WoT[:], d["L0_attn_Wo"]),
            (condT[:], d["condT"]), (pr.wproj[:], d["L0_ffn_proj_weight"]), (pr.wqkv[:], d["L0_ffn_qkv_weight"]),
            (w["Wq"][:], chunked(d["L0_attn_Wq"])), (w["Wk"][:], chunked(d["L0_attn_Wk"])),
            (w["Wv"][:], chunked(d["L0_attn_Wv"])), (w["w1"][:], chunked(d["L0_cond2_w1"])),
            (w2[:], chunked(d["L0_cond2_w2"])), (pr.base[:], chunked(d["L0_cond2_base_layer"])),
            (pr.wroute[:], chunked(d["L0_ffn_router_weight"])),
            (vec["b1"][:], d["L0_cond_b1"]), (vec["b2"][:], d["L0_cond_b2"]),
            (vec["c2b1"][:], d["L0_cond2_b1"]),
            (vec["lng"][:], d["L0_cond2_ln_g"]), (vec["lnb"][:], d["L0_cond2_ln_b"]),
            (b2c[:], d["L0_cond2_b2"]),
            (pr.ln1[:, 0, :], d["L0_ffn_ln1_weight"]), (pr.ln1[:, 1, :], d["L0_ffn_ln1_bias"]),
            (pr.ln2[:, 0, :], d["L0_ffn_ln2_weight"]), (pr.ln2[:, 1, :], d["L0_ffn_ln2_bias"]),
        ]
        all_loaded = 16 * len(loads)

        @block.sync
        def _(sp):
            for dst, src in loads:
                sp.dma_start(dst, src).then_inc(loaded, 16)
            sp.wait_ge(event("empty"), 1)
            rows = pr.slots.rearrange("(p a) c -> p a c", p=P)
            per = rows.shape[1] // EMPTYING
            for k in range(EMPTYING):
                sp.dma_start(rows[:, k * per:(k + 1) * per, :],
                             pr.empty[:, None, :].broadcast_to([P, per, ROW])).then_inc(pr.emptied, 16)

        @block.vector
        def _(dve_eng):
            ch = Chain(dve_eng, dve)
            v = nc.vector
            ch.link(v.memset(pr.empty[:], 0.0))
            v.memset(pr.empty[:, D:D + 1].bitcast(I32), NO_ROW).then_inc(event("empty"), 1)
            dve_eng.wait_ge(loaded, all_loaded)
            ch.step(v.tensor_copy(pr.identb[:], pr.ident))
            ch.step(v.tensor_copy(pr.trib[:], pr.cst[:, C_TRI:C_TRI + P]))
            ch.step(v.tensor_copy(pr.causalb[:].rearrange("p t g s -> p (t g) s"),
                                  pr.cst[:, None, C_CAUSAL:C_CAUSAL + S].broadcast_to([P, TG * NKV, S])))
            ch.link(v.bn_stats(stats[:], cond[:]))
            ch.link(v.bn_aggr(mv[:], stats[:]))
            rstd = inverse_root(nc, ch, mv[:, 1:2], tmp, seed[:])
            v.tensor_scalar(condn[:], cond[:], mv[:, 0:1], rstd, ALU.subtract, ALU.mult).then_inc(event("condn"), 1)
            ch.step(v.tensor_scalar(pr.wqkv[:, :, 0:D], pr.wqkv[:, :, 0:D], HD ** -0.5, None, ALU.mult))
            dve_eng.wait_ge(event("ps_condnT"), 1)
            for c in range(DC):
                ins = (v.tensor_scalar(aeT[:, c, :], ps[1][:, c * S:(c + 1) * S], vec["lng"][:, c:c + 1],
                                        vec["lnb"][:, c:c + 1], ALU.mult, ALU.add))
            ins.then_inc(event("aeT"), 1)
            dve_eng.wait_ge(event("ps_Wa"), 1)
            ch.step(v.tensor_scalar(pr.Wa[:].rearrange("p c n -> p (c n)"), ps[2][:], D ** -0.5, None, ALU.mult))
            dve_eng.wait_ge(event("ps_Wc"), 1)
            v.tensor_copy(pr.Wc[:].rearrange("p c n -> p (c n)"), ps[3][:]).then_inc(event("Wc"), 1)
            dve_eng.wait_ge(event("ps_h"), 1)
            for c in range(DC):
                ins = (v.tensor_scalar(z[:, c, :], ps[4][:, c * S:(c + 1) * S], vec["b1"][:, c:c + 1],
                                        None, ALU.add))
            ins.then_inc(event("z1"), 1)
            dve_eng.wait_ge(event("exp1"), 1)
            ch.link(v.tensor_scalar(ez[:], ez[:], 1.0, None, ALU.add))
            ch.link(v.reciprocal(ez[:], ez[:]))
            v.tensor_tensor(hs[:], z[:], ez[:], ALU.mult).then_inc(event("hs"), 1)
            dve_eng.wait_ge(event("ps_gate"), 1)
            for c in range(DC):
                ins = (v.tensor_scalar(z[:, c, :], ps[5][:, c * S:(c + 1) * S], vec["b2"][:, c:c + 1],
                                        None, ALU.add))
            ins.then_inc(event("z2"), 1)
            dve_eng.wait_ge(event("exp2"), 1)
            ch.link(v.tensor_scalar(ez[:], ez[:], 1.0, None, ALU.add))
            ch.link(v.reciprocal(ez[:], ez[:]))
            ch.step(v.tensor_scalar(pr.gate[:], ez[:], 1.0, None, ALU.add))
            for a, dst in ((0, pr.xa), (1, xbT)):
                dve_eng.wait_ge(event(f"ps_x{a}"), 1)
                for c in range(DC):
                    src = ps[a][:, c * RANK * S:(c + 1) * RANK * S].rearrange("p (r b) -> p b r", r=RANK)
                    ins = (v.tensor_tensor(
                        dst[:, c].rearrange("p h n -> p (h n)").rearrange("p (b r) -> p b r", r=RANK),
                        src, b2c[:, a, c, :].unsqueeze(1).broadcast_to([P, S, RANK]), ALU.add))
            ins.then_inc(event("xbT"), 1)
            dve_eng.wait_ge(event("ps_xb"), 1)
            ch.link(v.tensor_copy(pr.xb[:].rearrange("p h n -> p (h n)"), ps[2][:]))

        @block.tensor
        def _(pe):
            t = nc.tensor
            pe.wait_ge(loaded, all_loaded)
            pe.wait_ge(event("condn"), 1)
            for c in range(DC):
                ins = t.transpose(ps[1][:, c * S:(c + 1) * S], condn[:, c * P:(c + 1) * P], pr.ident[0:S, 0:S])
            ins.then_inc(event("ps_condnT"), 1)

            def product(name, out, lhs, rhs, after=None):
                if after:
                    pe.wait_ge(event(after), 1)
                width = rhs.shape[2]
                for mc in range(DC):
                    for kc in range(DC):
                        ins = t.matmul(out[:, mc * width:(mc + 1) * width], lhs[:, kc, mc * P:(mc + 1) * P],
                                       rhs[:, kc, :], start=(kc == 0), stop=(kc == DC - 1))
                ins.then_inc(event(f"ps_{name}"), 1)

            product("Wa", ps[2], w["Wq"], w["Wk"])
            product("Wc", ps[3], w["Wv"], WoT)
            product("h", ps[4], W1T, condT)
            product("h2", ps[6], w["w1"], aeT, after="aeT")
            product("gate", ps[5], W2T, hs, after="hs")
            pe.wait_ge(event("gelu"), 1)
            for a in range(2):
                for c in range(DC):
                    for r in range(RANK):
                        at = (c * RANK + r) * S
                        for ic in range(DC):
                            cols = w2[:, ic, a * D * RANK:(a + 1) * D * RANK].rearrange("p (k r) -> p r k", r=RANK)
                            ins = t.matmul(ps[a][:, at:at + S], cols[:, r, c * P:(c + 1) * P], h2[:, ic, :],
                                           start=(ic == 0), stop=(ic == DC - 1))
                ins.then_inc(event(f"ps_x{a}"), 1)
            pe.wait_ge(event("xbT"), 1)
            for h in range(2):
                for c in range(DC):
                    ins = t.transpose(ps[2][:, h * D + c * P:h * D + (c + 1) * P], xbT[:, c, h, :], pr.ident)
            ins.then_inc(event("ps_xb"), 1)

        @block.scalar
        def _(act):
            act.wait_ge(event("z1"), 1)
            nc.scalar.activation(ez[:], z[:], ACT.Exp, scale=-1.0).then_inc(event("exp1"), 1)
            act.wait_ge(event("z2"), 1)
            nc.scalar.activation(ez[:], z[:], ACT.Exp, scale=-1.0).then_inc(event("exp2"), 1)
            act.wait_ge(event("ps_h2"), 1)
            for c in range(DC):
                ins = nc.scalar.activation(h2[:, c, :], ps[6][:, c * S:(c + 1) * S], ACT.Gelu,
                                           bias=vec["c2b1"][:, c:c + 1])
            ins.then_inc(event("gelu"), 1)


def sequences(pr):
    nc, d = pr.nc, pr.d
    with ExitStack() as ctx:
        sb = lambda name, shape, dt=F32: ctx.enter_context(nc.sbuf_tensor(name, shape, dt))
        sem = pr.sem
        sems = lambda name: [sem(f"{name}{u}") for u in range(U1)]
        pa = [ctx.enter_context(nc.psum_tensor(f"pa{u}", [P, 512], F32)) for u in range(U1)]
        pb = [ctx.enter_context(nc.psum_tensor(f"pb{u}", [P, 512], F32)) for u in range(U1)]
        bufs = lambda name, shape: [sb(f"{name}{u}", shape) for u in range(U1)]
        x = bufs("x", [P, TC, D])
        xT = bufs("xT", [P, DC, T])
        uT = bufs("uT", [P, DC, T])
        qT = bufs("qT", [P, DC, T])
        pz = bufs("pz", [P, 512])
        pT = bufs("pT", [P, T + P])
        x1T = bufs("x1T", [P, DC, T])
        lr = bufs("lr", [P, T])
        x2T = bufs("x2T", [P, DC, T])
        x12 = bufs("x12_", [P, TC, 2, D])
        nmax, den, rden = (sb(n, [P, U1, TC]) for n in ("nmax", "den", "rden"))
        col = sb("col", [P, U1, DC + 1])
        stats = sb("stats1", [P, U1, TC, 6])
        mv = sb("mv1", [P, U1, TC, 2])
        tmp = sb("tmp1", [P, 4, U1 * TC])
        seed = sb("seed1", [P, U1 * TC], I32)
        flat = lambda a: a[:].rearrange("p c n -> p (c n)")

        x_in, xT_in = sems("x_in"), sems("xT_in")
        names_pe = "qT score pT z y low out x1 x2 nT kv".split()
        pe_did = {n: sem(f"pe_{n}_") for n in names_pe}
        names_dve = "u soft pT x1T x2T stat nrm kv".split()
        dve_did = {n: sem(f"dve_{n}_") for n in names_dve}
        names_act = "qT exp z lr x12 nT q".split()
        act_did = {n: sem(f"act_{n}_") for n in names_act}
        max_did = sem("max_found")
        stored = sems("stored")
        x1_rows, links = sem("x1_rows"), sem("links1")
        LINKS = U1 * (3 + 2 * TC) + 3 + 3 * NEWTON

        block = ctx.enter_context(nc.Block())

        @block.sync
        def _(sp):
            src = d["x"].rearrange("s (c p) n -> s p c n", p=P)
            dst = pr.x12.rearrange("(c p) s k n -> s p c (k n)", p=P)
            for u in range(U1):
                sp.sem_inc(stored[u], 16)
            with sp.Fori(0, I1) as i:
                for u in range(U1):
                    sp.wait_ge(pe_did["z"], U1 * i + u + 1)
                    sp.sem_inc(pr.passed, 1)
                    sp.dma_start(x[u][:], src[bass.ds(i + I1 * u, 1)].rearrange("a p c n -> p (a c) n")
                                 ).then_inc(x_in[u], 16)
                for u in range(U1):
                    sp.wait_ge(dve_did["x1T"], U1 * i + u + 1)
                    sp.sem_inc(pr.passed, 1)
                    sp.dma_start(xT[u][:], d["xT"][bass.ds(i + I1 * u, 1)].rearrange("a p c n -> p (a c) n")
                                 ).then_inc(xT_in[u], 16)
                for u in range(U1):
                    sp.wait_ge(act_did["x12"], U1 * i + u + 1)
                    sp.sem_inc(pr.passed, 1)
                    sp.dma_start(dst[bass.ds(i + I1 * u, 1)].rearrange("a p c n -> p (a c) n"),
                                 x12[u][:].rearrange("p c k n -> p c (k n)")).then_inc(stored[u], 16)
            for u in range(U1):
                sp.wait_ge(stored[u], 16 * (I1 + 1))

        @block.tensor
        def _(pe):
            t = nc.tensor

            def product(out, lhs, rhs, cols=T, start=True, stop=True):
                for mc in range(DC):
                    for kc in range(DC):
                        ins = t.matmul(out[:, mc * cols:(mc + 1) * cols], lhs[:, kc, mc * P:(mc + 1) * P],
                                       rhs[:, kc, :], start=start and mc == 0 and kc == 0,
                                       stop=stop and kc == DC - 1, skip_group_check=True)
                return ins

            def transposes(out, src):
                for c in range(DC):
                    for r in range(TC):
                        ins = t.transpose(out[:, c * 256 + r * P:c * 256 + (r + 1) * P],
                                          src[:, r, c * P:(c + 1) * P], pr.ident)
                return ins

            for u in range(U1):
                pe.sem_inc(pe_did["z"], 1)
                pe.sem_inc(act_did["q"], 1)
                pe.sem_inc(dve_did["kv"], 1)
                pe.sem_inc(dve_did["x1T"], 1)
            with pe.Fori(0, I1) as i:
                for u in range(U1):
                    pe.wait_ge(dve_did["kv"], U1 * i + u + 1)
                    pe.wait_ge(dve_did["u"], U1 * i + u + 1)
                    product(pb[u], pr.Wa, uT[u]).then_inc(pe_did["qT"], 1)
                for u in range(U1):
                    pe.wait_ge(act_did["q"], U1 * i + u + 1)
                    pe.wait_ge(act_did["qT"], U1 * i + u + 1)
                    for r in range(TC):
                        out = pa[u][:, r * P:r * P + (r + 1) * P]
                        for c in range(DC):
                            t.matmul(out, qT[u][:, c, r * P:(r + 1) * P], uT[u][:, c, 0:(r + 1) * P],
                                     start=(c == 0), stop=False, skip_group_check=True)
                        ins = t.matmul(out[:, r * P:(r + 1) * P], pr.identb[:], pr.trib[:],
                                       start=False, stop=True, skip_group_check=True)
                    ins.then_inc(pe_did["score"], 1)
                for u in range(U1):
                    pe.wait_ge(dve_did["soft"], U1 * i + u + 1)
                    for k in range(3):
                        ins = t.transpose(pb[u][:, k * P:(k + 1) * P], pz[u][:, k * P:(k + 1) * P], pr.ident)
                    ins.then_inc(pe_did["pT"], 1)
                for u in range(U1):
                    pe.wait_ge(dve_did["pT"], U1 * i + u + 1)
                    pe.wait_ge(x_in[u], 16 * i + 16)
                    for c in range(DC):
                        t.matmul(pa[u][:, c * T:(c + 1) * T], x[u][:, 0, c * P:(c + 1) * P], pT[u][:, 0:T],
                                 start=(c == 0), stop=False, skip_group_check=True)
                        ins = t.matmul(pa[u][:, c * T + P:(c + 1) * T], x[u][:, 1, c * P:(c + 1) * P],
                                       pT[u][:, T:T + P], start=False, stop=True, skip_group_check=True)
                    ins.then_inc(pe_did["z"], 1)
                for u in range(U1):
                    pe.wait_ge(act_did["z"], U1 * i + u + 1)
                    product(pb[u], pr.Wc, pz[u][:].rearrange("p (c n) -> p c n", c=DC)
                            ).then_inc(pe_did["y"], 1)
                for u in range(U1):
                    pe.wait_ge(dve_did["x1T"], U1 * (i + 1) + u + 1)
                    for c in range(DC):
                        ins = t.matmul(pb[u][:, 0:T], pr.xa[:, c, u // 2, :], x1T[u][:, c, :],
                                       start=(c == 0), stop=(c == DC - 1))
                    ins.then_inc(pe_did["low"], 1)
                for u in range(U1):
                    product(pa[u], pr.base, x1T[u], stop=False)
                    pe.wait_ge(act_did["lr"], U1 * i + u + 1)
                    for c in range(DC):
                        ins = t.matmul(pa[u][:, c * T:(c + 1) * T], pr.xb[:, u // 2, c * P:(c + 1) * P],
                                       lr[u][:], start=False, stop=True, skip_group_check=True)
                    ins.then_inc(pe_did["out"], 1)
                    transposes(pb[u], x1T[u]).then_inc(pe_did["x1"], 1)
                for u in range(U1):
                    pe.wait_ge(dve_did["x2T"], U1 * i + u + 1)
                    transposes(pa[u], x2T[u]).then_inc(pe_did["x2"], 1)
                for u in range(U1):
                    pe.wait_ge(dve_did["nrm"], U1 * i + u + 1)
                    transposes(pb[u], uT[u]).then_inc(pe_did["nT"], 1)
                for u in range(U1):
                    pe.wait_ge(act_did["nT"], U1 * i + u + 1)
                    for dst, c0, n in ((pb, 2 * P, 1), (pa, 0, 2)):
                        for m in range(n):
                            for c in range(DC):
                                ins = t.matmul(dst[u][:, m * T:(m + 1) * T],
                                               pr.wqkv[:, c, c0 + m * P:c0 + (m + 1) * P], qT[u][:, c, :],
                                               start=(c == 0), stop=(c == DC - 1))
                    ins.then_inc(pe_did["kv"], 1)

        @block.scalar
        def _(act):
            a = nc.scalar
            with act.Fori(0, I1) as i:
                for u in range(U1):
                    act.wait_ge(pe_did["qT"], U1 * i + u + 1)
                    a.copy(flat(qT[u]), pb[u][:]).then_inc(act_did["qT"], 1)
                for u in range(U1):
                    act.wait_ge(max_did, U1 * i + u + 1)
                    for r in range(TC):
                        cols = slice(r * P, r * P + (r + 1) * P)
                        ins = a.activation(pz[u][:, cols], pa[u][:, cols], ACT.Exp, bias=nmax[:, u, r:r + 1],
                                           accum_out=den[:, u, r:r + 1])
                    ins.then_inc(act_did["exp"], 1)
                for u in range(U1):
                    act.wait_ge(pe_did["z"], U1 * (i + 1) + u + 1)
                    for c in range(DC):
                        ins = a.activation(pz[u][:, c * T:(c + 1) * T], pa[u][:, c * T:(c + 1) * T], ACT.Copy,
                                           scale=col[:, u, c:c + 1])
                    ins.then_inc(act_did["z"], 1)
                for u in range(U1):
                    act.wait_ge(pe_did["low"], U1 * i + u + 1)
                    a.activation(lr[u][:], pb[u][:, 0:T], ACT.Copy, scale=col[:, u, DC:DC + 1]
                                 ).then_inc(act_did["lr"], 1)
                for u in range(U1):
                    act.wait_ge(pe_did["x1"], U1 * i + u + 1)
                    act.wait_ge(stored[u], 16 * i + 16)
                    a.copy(x12[u][:, :, 0, :], pb[u][:].rearrange("p (c n) -> p c n", c=TC)
                           ).then_inc(x1_rows, 1)
                for u in range(U1):
                    act.wait_ge(pe_did["x2"], U1 * i + u + 1)
                    a.copy(x12[u][:, :, 1, :], pa[u][:].rearrange("p (c n) -> p c n", c=TC)
                           ).then_inc(act_did["x12"], 1)
                for u in range(U1):
                    act.wait_ge(pe_did["nT"], U1 * i + u + 1)
                    for c in range(DC):
                        ins = a.activation(qT[u][:, c, :], pb[u][:, c * T:(c + 1) * T], ACT.Identity,
                                           scale=pr.ln1[:, 0, c:c + 1], bias=pr.ln1[:, 1, c:c + 1])
                    ins.then_inc(act_did["nT"], 1)
                for u in range(U1):
                    act.wait_ge(pe_did["kv"], U1 * i + u + 1)
                    act.sem_inc(pr.passed, 1)
                    a.copy(pr.q[:, :, :, :, bass.ds(i + I1 * u, 1)].rearrange("p c g t a -> p c g (t a)"),
                           pa[u][:].rearrange("p (c g t) -> p c g t", c=DC, g=G)).then_inc(act_did["q"], 1)

        @block.vector
        def _(dve):
            v = nc.vector
            with dve.Fori(0, I1) as i:
                ch = Chain(dve, links, i * LINKS)
                for u in range(U1):
                    ch.step(v.tensor_scalar(col[:, u, 0:DC], pr.gate[:, :, bass.ds(i + I1 * u, 1)]
                                            .rearrange("p c a -> p (c a)"), 1.0, None, ALU.mult))
                    ch.step(v.tensor_scalar(col[:, u, DC:DC + 1],
                                            pr.cst[:, bass.ds(C_SEL + i + I1 * (u % 2), 1)], 1.0, None, ALU.mult))
                ch.wait()
                for u in range(U1):
                    dve.wait_ge(xT_in[u], 16 * i + 16)
                    for c in range(DC):
                        ins = v.tensor_scalar(uT[u][:, c, :], xT[u][:, c, :], col[:, u, c:c + 1], None, ALU.mult)
                    ins.then_inc(dve_did["u"], 1)
                for u in range(U1):
                    dve.wait_ge(pe_did["score"], U1 * i + u + 1)
                    for r in range(TC):
                        ins = v.tensor_reduce(nmax[:, u, r:r + 1], pa[u][:, r * P:r * P + (r + 1) * P],
                                              AX.X, ALU.max, negate=True)
                    ins.then_inc(max_did, 1)
                for u in range(U1):
                    dve.wait_ge(act_did["exp"], U1 * i + u + 1)
                    ch.link(v.reciprocal(rden[:, u, :], den[:, u, :]))
                    for r in range(TC):
                        cols = slice(r * P, r * P + (r + 1) * P)
                        ins = v.tensor_scalar(pz[u][:, cols], pz[u][:, cols], rden[:, u, r:r + 1], None, ALU.mult)
                    ins.then_inc(dve_did["soft"], 1)
                for u in range(U1):
                    dve.wait_ge(pe_did["pT"], U1 * i + u + 1)
                    v.tensor_copy(pT[u][:], pb[u][:, 0:T + P]).then_inc(dve_did["pT"], 1)
                for u in range(U1):
                    dve.wait_ge(pe_did["y"], U1 * i + u + 1)
                    v.tensor_tensor(flat(x1T[u]), pb[u][:], flat(xT[u]), ALU.add).then_inc(dve_did["x1T"], 1)
                for u in range(U1):
                    dve.wait_ge(pe_did["out"], U1 * i + u + 1)
                    v.tensor_tensor(flat(x2T[u]), pa[u][:], flat(x1T[u]), ALU.add).then_inc(dve_did["x2T"], 1)
                for u in range(U1):
                    dve.wait_ge(act_did["x12"], U1 * i + u + 1)
                    for c in range(TC):
                        ch.step(v.bn_stats(stats[:, u, c, :], x12[u][:, c, 1, :]))
                ch.wait()
                dve.sem_inc(pr.passed, 1)
                for u in range(U1):
                    for c in range(TC):
                        ch.step(v.bn_aggr(mv[:, u, c, :], stats[:, u, c, :]))
                ch.wait()
                rstd = inverse_root(nc, ch, mv[:].rearrange("p u c k -> p (u c) k")[:, :, 1], tmp, seed[:])
                for u in range(U1):
                    for c in range(TC):
                        k = u * TC + c
                        ins = v.tensor_scalar(uT[u][:, c, :], x12[u][:, c, 1, :], mv[:, u, c, 0:1],
                                              rstd[:, k:k + 1], ALU.subtract, ALU.mult)
                    ins.then_inc(dve_did["nrm"], 1)
                for u in range(U1):
                    dve.wait_ge(pe_did["kv"], U1 * i + u + 1)
                    dve.sem_inc(pr.passed, 1)
                    v.tensor_copy(pr.kv[:, :, :, bass.ds(i + I1 * u, 1)].rearrange("p g t a -> p g (t a)"),
                                  pb[u][:, 0:T].rearrange("p (g t) -> p g t", g=G)).then_inc(dve_did["kv"], 1)
                assert ch.n == LINKS, ch.n


def positions(pr):
    nc, d = pr.nc, pr.d
    with ExitStack() as ctx:
        sb = lambda name, shape, dt=F32: ctx.enter_context(nc.sbuf_tensor(name, shape, dt))
        sem = pr.sem
        sems = lambda name: [sem(f"{name}{u}") for u in range(U2)]
        pa = [ctx.enter_context(nc.psum_tensor(f"ga{u}", [P, 512], F32)) for u in range(U2)]
        pb = [ctx.enter_context(nc.psum_tensor(f"gb{u}", [P, 512], F32)) for u in range(U2)]
        bufs = lambda name, shape: [sb(f"{name}{u}", shape) for u in range(U2)]
        KV1 = NKV * HD
        qg = bufs("qg", [KV1, TG, JQ, S])
        kvd = bufs("kvd", [P, TG, NKV, S])
        pw = bufs("pw", [P, TG * NKV, S])
        pwT = bufs("pwT", [P, TG, JQ, S])
        vb = bufs("vb", [P, TG, KV1])
        aoT = bufs("aoT", [P, 2, TG, S])
        x12 = bufs("xg", [P, 2, D])
        h1 = bufs("h1", [P, D])
        res = bufs("res", [P, D])
        nrm = bufs("nrm", [P, D])
        nT = bufs("nT", [P, DC, P])
        nmax, den = (sb(n, [P, U2, TG * NKV]) for n in ("gmax", "gden"))
        stats = sb("stats2", [P, U2, 6])
        mv = sb("mv2", [P, U2, 2])
        tmp = sb("tmp2", [P, 4, U2])
        seed = sb("seed2", [P, U2], I32)

        x_in, stored = sems("g_x_in"), sems("g_stored")
        pe_did = {n: sem(f"gpe_{n}_") for n in "score wT av h nT logit".split()}
        dve_did = {n: sem(f"gdve_{n}_") for n in "q sub rden h1 nrm logit".split()}
        act_did = {n: sem(f"gact_{n}_") for n in "exp wT v ao nT".split()}
        pool_did = {n: sem(f"gpool_{n}_") for n in "kv soft res".split()}
        links = sem("links2")
        LINKS = U2 * 5 + 3 + 3 * NEWTON
        group = lambda i, u: i * U2 + u

        block = ctx.enter_context(nc.Block())

        @block.sync
        def _(sp):
            src = pr.x12.rearrange("(g t) s k n -> g (t s) (k n)", t=TG)
            dst = pr.d["out"].rearrange("(g t) s n -> g (t s) n", t=TG)
            for u in range(U2):
                sp.sem_inc(stored[u], 16)
            with sp.Fori(0, I2) as i:
                for u in range(U2):
                    sp.wait_ge(pool_did["res"], U2 * i + u + 1)
                    sp.sem_inc(pr.passed, 1)
                    sp.dma_start(x12[u][:].rearrange("p k n -> p (k n)"),
                                 src[bass.ds(group(i, u), 1)].rearrange("a p n -> (a p) n")
                                 ).then_inc(x_in[u], 16)
                for u in range(U2):
                    sp.wait_ge(pool_did["res"], U2 * (i + 1) + u + 1)
                    sp.sem_inc(pr.passed, 1)
                    sp.dma_start(dst[bass.ds(group(i, u), 1)].rearrange("a p n -> (a p) n"), res[u][:]
                                 ).then_inc(stored[u], 16)
            for u in range(U2):
                sp.wait_ge(stored[u], 16 * (I2 + 1))

        @block.gpsimd
        def _(pool):
            g = nc.gpsimd
            for u in range(U2):
                pool.sem_inc(pool_did["res"], 1)
            with pool.Fori(0, I2) as i:
                for u in range(U2):
                    pool.wait_ge(pe_did["av"], U2 * i + u + 1)
                    g.tensor_tensor(kvd[u][:],
                                    pr.kv[:, bass.ds(group(i, u), 1)].rearrange("p a t s -> p (a t) s").unsqueeze(2)
                                    .broadcast_to([P, TG, NKV, S]),
                                    pr.cst[:, C_HEAD:C_HEAD + NKV].unsqueeze(1).unsqueeze(3)
                                    .broadcast_to([P, TG, NKV, S]), ALU.mult).then_inc(pool_did["kv"], 1)
                for u in range(U2):
                    pool.wait_ge(dve_did["rden"], U2 * i + u + 1)
                    g.tensor_tensor(pw[u][:], pw[u][:], den[:, u, :].unsqueeze(2)
                                    .broadcast_to([P, TG * NKV, S]), ALU.mult).then_inc(pool_did["soft"], 1)
                for u in range(U2):
                    pool.wait_ge(dve_did["h1"], U2 * i + u + 1)
                    pool.wait_ge(stored[u], 16 * i + 16)
                    g.tensor_tensor(res[u][:], x12[u][:, 0, :], h1[u][:], ALU.add
                                    ).then_inc(pool_did["res"], 1)

        @block.tensor
        def _(pe):
            t_ = nc.tensor
            for u in range(U2):
                pe.sem_inc(pe_did["av"], 1)
                pe.sem_inc(act_did["nT"], 1)
                pe.sem_inc(dve_did["logit"], 1)
            with pe.Fori(0, I2) as i:
                for u in range(U2):
                    pe.wait_ge(act_did["nT"], U2 * i + u + 1)
                    t_.matmul(pa[u][:], pr.identb[:], pr.causalb[:].rearrange("p t g s -> p (t g s)"),
                              start=True, stop=False, skip_group_check=True)
                    pe.wait_ge(dve_did["q"], U2 * i + u + 1)
                    pe.wait_ge(pool_did["kv"], U2 * i + u + 1)
                    for t in range(TG):
                        ins = t_.matmul(pa[u][:, t * P:(t + 1) * P], qg[u][:, t].rearrange("p j s -> p (j s)"),
                                        kvd[u][0:KV1, t].rearrange("p g s -> p (g s)"),
                                        start=False, stop=True, skip_group_check=True)
                    ins.then_inc(pe_did["score"], 1)
                for u in range(U2):
                    pe.wait_ge(dve_did["logit"], U2 * i + u + 1)
                    pe.wait_ge(dve_did["sub"], U2 * i + u + 1)
                    pe.sem_inc(pr.passed, 1)
                    for t in range(TG):
                        t_.transpose(pa[u][:, t * KV1:(t + 1) * KV1],
                                     kvd[u][KV1:P, t].rearrange("p g s -> p (g s)"),
                                     pr.cst[KV1:P, C_ID + KV1:C_ID + P])
                    pe.wait_ge(pool_did["soft"], U2 * i + u + 1)
                    for t in range(TG):
                        ins = t_.transpose(pb[u][:, t * P:(t + 1) * P],
                                           pw[u][:, t * NKV:(t + 1) * NKV, :].rearrange("p g s -> p (g s)"),
                                           pr.ident)
                    ins.then_inc(pe_did["wT"], 1)
                for u in range(U2):
                    pe.wait_ge(act_did["wT"], U2 * i + u + 1)
                    pe.wait_ge(act_did["v"], U2 * i + u + 1)
                    for jp in range(2):
                        for t in range(TG):
                            out = pa[u][jp * KV1:(jp + 1) * KV1, 256:512].rearrange("p (h t s) -> p h t s", h=2, t=TG)
                            ins = t_.matmul(out[:, :, t, :], vb[u][:, t, :], pwT[u][:, t, jp::2, :],
                                            start=True, stop=True, skip_group_check=True)
                    ins.then_inc(pe_did["av"], 1)
                for u in range(U2):
                    pe.wait_ge(act_did["ao"], U2 * i + u + 1)
                    for h in range(2):
                        ins = t_.matmul(pb[u][:, 0:D], aoT[u][:, h].rearrange("p t s -> p (t s)"),
                                        pr.wproj[:, h, :], start=(h == 0), stop=(h == 1))
                    ins.then_inc(pe_did["h"], 1)
                for u in range(U2):
                    pe.wait_ge(dve_did["nrm"], U2 * i + u + 1)
                    for c in range(DC):
                        ins = t_.transpose(pa[u][:, c * P:(c + 1) * P], nrm[u][:, c * P:(c + 1) * P], pr.ident)
                    ins.then_inc(pe_did["nT"], 1)
                for u in range(U2):
                    pe.wait_ge(act_did["nT"], U2 * (i + 1) + u + 1)
                    for c in range(DC):
                        ins = t_.matmul(pb[u][:, 256:256 + E], nT[u][:, c, :], pr.wroute[:, c, :],
                                        start=(c == 0), stop=(c == DC - 1))
                    ins.then_inc(pe_did["logit"], 1)

        @block.scalar
        def _(act):
            a = nc.scalar
            a.activation(tmp[:, 0, 0:1], pr.cst[:, 0:1], ACT.Exp).then_inc(links, 1)
            with act.Fori(0, I2) as i:
                for u in range(U2):
                    act.wait_ge(dve_did["sub"], U2 * i + u + 1)
                    a.activation(pw[u][:], pw[u][:], ACT.Exp).then_inc(act_did["exp"], 1)
                for u in range(U2):
                    act.wait_ge(pe_did["wT"], U2 * i + u + 1)
                    a.copy(vb[u][:].rearrange("p t n -> p (t n)"), pa[u][:, 0:TG * KV1]).then_inc(act_did["v"], 1)
                    a.copy(pwT[u][:].rearrange("p t j s -> p (t j s)"), pb[u][:]).then_inc(act_did["wT"], 1)
                for u in range(U2):
                    act.wait_ge(pe_did["av"], U2 * (i + 1) + u + 1)
                    a.copy(aoT[u][:].rearrange("p h t s -> p (h t s)"), pa[u][:, 256:512]
                           ).then_inc(act_did["ao"], 1)
                for u in range(U2):
                    act.wait_ge(pe_did["nT"], U2 * i + u + 1)
                    for c in range(DC):
                        ins = a.activation(nT[u][:, c, :], pa[u][:, c * P:(c + 1) * P], ACT.Identity,
                                           scale=pr.ln2[:, 0, c:c + 1], bias=pr.ln2[:, 1, c:c + 1])
                    ins.then_inc(act_did["nT"], 1)

        @block.vector
        def _(dve):
            v = nc.vector
            dve.wait_ge(links, 1)
            with dve.Fori(0, I2) as i:
                ch = Chain(dve, links, i * LINKS + 1)
                for u in range(U2):
                    for jp in range(2):
                        ins = v.tensor_scalar(
                            qg[u][:].rearrange("p t j s -> p j t s")[:, jp::2],
                            pr.q[jp * KV1:(jp + 1) * KV1, :, bass.ds(group(i, u), 1)]
                            .rearrange("p c a t s -> p c (a t) s"),
                            1.0, None, ALU.mult)
                    ins.then_inc(dve_did["q"], 1)
                for u in range(U2):
                    dve.wait_ge(pe_did["score"], U2 * i + u + 1)
                    ch.link(v.tensor_reduce(nmax[:, u, :], pa[u][:].rearrange("p (n s) -> p n s", s=S),
                                            AX.X, ALU.max))
                    v.tensor_tensor(pw[u][:], pa[u][:].rearrange("p (n s) -> p n s", s=S),
                                    nmax[:, u, :].unsqueeze(2).broadcast_to([P, TG * NKV, S]),
                                    ALU.subtract).then_inc(dve_did["sub"], 1)
                for u in range(U2):
                    dve.wait_ge(act_did["exp"], U2 * i + u + 1)
                    ch.link(v.tensor_reduce(den[:, u, :], pw[u][:], AX.X, ALU.add))
                    v.reciprocal(den[:, u, :], den[:, u, :]).then_inc(dve_did["rden"], 1)
                for u in range(U2):
                    dve.wait_ge(pe_did["h"], U2 * i + u + 1)
                    dve.wait_ge(x_in[u], 16 * i + 16)
                    v.tensor_tensor(h1[u][:], pb[u][:, 0:D], x12[u][:, 1, :], ALU.add
                                    ).then_inc(dve_did["h1"], 1)
                    dve.wait_ge(dve_did["h1"], U2 * i + u + 1)
                    ch.link(v.bn_stats(stats[:, u, :], h1[u][:]))
                    dve.sem_inc(pr.passed, 1)
                    ch.step(v.bn_aggr(mv[:, u, :], stats[:, u, :]))
                ch.wait()
                rstd = inverse_root(nc, ch, mv[:, :, 1], tmp, seed[:])
                for u in range(U2):
                    v.tensor_scalar(nrm[u][:], h1[u][:], mv[:, u, 0:1], rstd[:, u:u + 1],
                                    ALU.subtract, ALU.mult).then_inc(dve_did["nrm"], 1)
                for u in range(U2):
                    ch.step(v.tensor_scalar(pr.rows[:, bass.ds(group(i, u), 1), 0:D].rearrange("p a n -> p (a n)"),
                                            h1[u][:], mv[:, u, 0:1],
                                            rstd[:, u:u + 1], ALU.subtract, ALU.mult))
                for u in range(U2):
                    dve.wait_ge(pe_did["logit"], U2 * i + u + 1)
                    v.tensor_scalar(pr.logits[:, bass.ds(group(i, u), 1), :].rearrange("p a n -> p (a n)"),
                                    pb[u][:, 256:256 + E], 1.0, None, ALU.mult
                                    ).then_inc(dve_did["logit"], 1)
                assert ch.n == LINKS, ch.n


def experts(pr):
    nc, d = pr.nc, pr.d
    with ExitStack() as ctx:
        sb = lambda name, shape, dt=F32: ctx.enter_context(nc.sbuf_tensor(name, shape, dt))
        sem = pr.sem
        TB = BT // P
        ph = [ctx.enter_context(nc.psum_tensor(f"ph{f}", [P, BT], F32)) for f in range(FC)]
        pt = [ctx.enter_context(nc.psum_tensor(f"pt{c}", [P, BT], F32)) for c in range(DC)]
        py = [ctx.enter_context(nc.psum_tensor(f"py{c}", [P, 2, D], F32)) for c in range(TB // 2)]
        L2, eq, S1, excl = (sb(n, [P, G, E]) for n in ("L2", "eq", "S1", "excl"))
        hot = sb("hot", [P, K, G, E])
        best, top = sb("best", [P, K, G]), sb("top", [P, G])
        ratio, prob = sb("ratio", [P, G]), sb("prob", [P, K, G])
        slotf, slot = sb("slotf", [P, K, G]), sb("slot", [P, K, G], I32)
        chosen = sb("chosen", [P, G, E], BF16)
        total, totalb = sb("total", [P, E]), sb("totalb", [P, E], BF16)
        order = sb("order", [P, 3, P], BF16)
        tiles = sb("tiles", [P, E, G])
        scan = sb("scan", [P, E, G])
        w1 = [sb(f"w1_{k}", [P, DC, F]) for k in range(2)]
        w2 = [sb(f"w2_{k}", [P, FC, D]) for k in range(2)]
        xr = [sb(f"xr{k}", [P, TB, ROW]) for k in range(2)]
        y = [sb(f"y{k}", [P, TB, D]) for k in range(2)]
        xT = sb("xTe", [P, DC, BT])
        h = sb("h", [P, FC, BT])

        links, ratio_in, ratio_did, ranked = sem("links3"), sem("ratio_in"), sem("ratio_did"), sem("ranked")
        chosen_did, routed, dispatched = sem("chosen_did"), sem("routed"), sem("dispatched")
        w_in = [sem(f"w_in{k}") for k in range(2)]
        x_in = [sem(f"xr_in{k}") for k in range(2)]
        added, settled = sem("added"), sem("settled")
        t_did, xT_did, fc1_did, gelu_did = sem("t_did"), sem("xT_did"), sem("fc1_did"), sem("gelu_did")
        fc2_did, y_did = sem("fc2_did"), sem("y_did")
        FC2_0, GELU_0 = 2 * NB + 1, FC
        PAIRS = E // 2
        number = lambda ep, n: ep * 2 * NB + n
        uses = lambda ep, n: ep * NB + n // 2
        grow = lambda a: a.unsqueeze(2).broadcast_to([P, G, E])
        row_e = lambda c0: pr.cst[:, c0:c0 + E].unsqueeze(1).broadcast_to([P, G, E])

        block = ctx.enter_context(nc.Block())

        @block.sync
        def _(sp):
            src = pr.slots.rearrange("(n t p) c -> n p t c", t=TB, p=P)
            w1_d = d["L0_ffn_moe_w1"].rearrange("e (c p) f -> e p c f", p=P)
            w2_d = d["L0_ffn_moe_w2"].rearrange("e (c p) n -> e p c n", p=P)

            def load_x(ep, n):
                sp.wait_ge(settled, number(ep, n) + 1)
                sp.sem_inc(pr.passed, 1)
                sp.dma_start(xr[n % 2][:], src[bass.ds(number(ep, n), 1)].rearrange("a p t c -> p (a t) c")
                             ).then_inc(x_in[n % 2], 16)

            sp.sem_inc(settled, 2)
            with sp.Fori(0, PAIRS) as ep:
                for par in range(2):
                    sp.wait_ge(fc2_did, (ep * 2 + par - 1) * 2 * NB + FC2_0)
                    sp.sem_inc(pr.passed, 1)
                    sp.dma_start(w1[par][:], w1_d[bass.ds(ep * 2 + par, 1)].rearrange("a p c f -> p (a c) f")
                                 ).then_inc(w_in[par], 16)
                    sp.dma_start(w2[par][:], w2_d[bass.ds(ep * 2 + par, 1)].rearrange("a p c f -> p (a c) f")
                                 ).then_inc(w_in[par], 16)
                    for b in range(NB):
                        if par == 0 and b == 0:
                            sp.wait_ge(dispatched, 16 * K * G)
                        load_x(ep, par * NB + b)
            sp.wait_ge(settled, PAIRS * 2 * NB + 1)
            sp.dma_start(xr[0][:], src[PAIRS * 2 * NB]).then_inc(x_in[0], 16)
            sp.wait_ge(x_in[0], 16 * (PAIRS * NB + 1))

        @block.gpsimd
        def _(pool):
            g = nc.gpsimd
            out = d["out"].rearrange("t s n -> (t s) n")
            pool.wait_ge(pr.emptied, 16 * EMPTYING)
            pool.wait_ge(routed, 1)
            for j in range(G):
                for k in range(K):
                    g.indirect_dma_start(
                        out=pr.slots, out_offset=bass.IndirectOffsetOnAxis(ap=slot[:, k, j:j + 1], axis=0),
                        in_=pr.rows[:, j, :], in_offset=None, bounds_check=E * CAP - 1, oob_is_err=False,
                    ).then_inc(dispatched, 16)
            with pool.Fori(0, PAIRS) as ep:
                for n in range(2 * NB):
                    pool.wait_ge(y_did, number(ep, n) + 2)
                    pool.sem_inc(pr.passed, 1)
                    for t in range(TB):
                        g.indirect_dma_start(
                            out=out, out_offset=bass.IndirectOffsetOnAxis(
                                ap=xr[n % 2][:, t, D:D + 1].bitcast(I32), axis=0),
                            in_=y[n % 2][:, t, :], in_offset=None, bounds_check=N - 1, oob_is_err=False,
                            compute_op=ALU.add).then_inc(added, 16)
                    pool.wait_ge(added, 16 * TB * (number(ep, n) + 1))
                    pool.sem_inc(settled, 1)

        @block.tensor
        def _(pe):
            t_ = nc.tensor
            pe.sem_inc(fc2_did, FC2_0)
            pe.sem_inc(gelu_did, GELU_0)
            pe.sem_inc(y_did, 1)
            flat = lambda a: a.rearrange("p g e -> p (g e)")
            pe.wait_ge(chosen_did, 1)
            t_.matmul(ph[0][:], order[:, 2, :], flat(chosen[:]), start=True, stop=False)
            t_.matmul(ph[0][:], order[:, 0, :], totalb[:].unsqueeze(1).broadcast_to([P, G, E]),
                      start=False, stop=True)
            t_.matmul(ph[1][:], order[:, 1, :], flat(chosen[:]), start=True, stop=True).then_inc(ranked, 1)

            def turn(q):
                for c in range(DC):
                    for t in range(TB):
                        ins = t_.transpose(pt[c][:, t * P:(t + 1) * P], xr[q][:, t, c * P:(c + 1) * P], pr.ident)
                ins.then_inc(t_did, 1)

            pe.wait_ge(routed, 1)
            pe.wait_ge(x_in[0], 16)
            turn(0)
            with pe.Fori(0, PAIRS) as ep:
                for n in range(2 * NB):
                    par = n // NB
                    pe.wait_ge(xT_did, number(ep, n) + 1)
                    if n % NB == 0:
                        pe.wait_ge(w_in[par], 32 * ep + 32)
                    for f in range(FC):
                        pe.wait_ge(gelu_did, number(ep, n) * FC + f + 1 - FC + GELU_0)
                        for c in range(DC):
                            ins = t_.matmul(ph[f][:], w1[par][:, c, f * P:(f + 1) * P], xT[:, c, :],
                                            start=(c == 0), stop=(c == DC - 1))
                        ins.then_inc(fc1_did, 1)
                    pe.wait_ge(x_in[(n + 1) % 2], 16 * (uses(ep, n + 1) + 1))
                    turn((n + 1) % 2)
                    pe.wait_ge(gelu_did, (number(ep, n) + 1) * FC + GELU_0)
                    pe.wait_ge(y_did, number(ep, n) + 1)
                    for t in range(TB):
                        for f in range(FC):
                            ins = t_.matmul(py[t // 2][:, t % 2, :], h[:, f, t * P:(t + 1) * P], w2[par][:, f, :],
                                            start=(f == 0), stop=(f == FC - 1))
                        if t % 2:
                            ins.then_inc(fc2_did, 1)

        @block.scalar
        def _(act):
            a = nc.scalar
            act.wait_ge(ratio_in, 1)
            a.activation(ratio[:], ratio[:], ACT.Exp).then_inc(ratio_did, 1)

            def features(first):
                act.wait_ge(t_did, first)
                for c in range(DC):
                    ins = a.activation(xT[:, c, :], pt[c][:], ACT.Identity,
                                       scale=pr.ln2[:, 0, c:c + 1], bias=pr.ln2[:, 1, c:c + 1])
                ins.then_inc(xT_did, 1)

            features(1)
            act.wait_ge(chosen_did, 1)
            a.activation(top[:, 0:1], pr.cst[:, 0:1], ACT.Gelu_apprx_tanh).then_inc(ratio_did, 1)
            with act.Fori(0, PAIRS) as ep:
                for n in range(2 * NB):
                    for f in range(FC):
                        act.wait_ge(fc1_did, number(ep, n) * FC + f + 1)
                        a.activation(h[:, f, :], ph[f][:], ACT.Gelu_apprx_tanh).then_inc(gelu_did, 1)
                    features(number(ep, n) + 2)

        @block.vector
        def _(dve):
            v = nc.vector
            ch = Chain(dve, links)
            ch.step(v.tensor_copy(order[:].rearrange("p k n -> p (k n)"), pr.cst[:, C_ORDER:C_ORDER + 3 * P]))
            source = pr.logits
            for k in range(K):
                ch.link(v.tensor_reduce(best[:, k, :], source[:], AX.X, ALU.max))
                ch.link(v.tensor_tensor(eq[:], source[:], grow(best[:, k, :]), ALU.is_equal))
                ch.link(v.tensor_tensor(eq[:], eq[:], row_e(C_TIE), ALU.mult))
                ch.link(v.tensor_reduce(top[:], eq[:], AX.X, ALU.max))
                ch.link(v.tensor_tensor(hot[:, k], eq[:], grow(top[:]), ALU.is_equal))
                if k == 0:
                    ch.link(v.scalar_tensor_tensor(L2[:].rearrange("p g e -> p (g e)"),
                                                   hot[:, 0].rearrange("p g e -> p (g e)"), NEG,
                                                   pr.logits[:].rearrange("p g e -> p (g e)"),
                                                   ALU.mult, ALU.add))
                    source = L2
            v.tensor_tensor(ratio[:], best[:, 1, :], best[:, 0, :], ALU.subtract).then_inc(ratio_in, 1)
            ch.link(v.tensor_tensor(chosen[:], hot[:, 0], hot[:, 1], ALU.add))
            ch.link(v.tensor_reduce(total[:], chosen[:].rearrange("p g e -> p e g"), AX.X, ALU.add))
            v.tensor_copy(totalb[:], total[:]).then_inc(chosen_did, 1)
            dve.wait_ge(ratio_did, 1)
            ch.link(v.tensor_scalar(prob[:, 1, :], ratio[:], 1.0, None, ALU.add))
            ch.link(v.reciprocal(prob[:, 0, :], prob[:, 1, :]))
            ch.link(v.tensor_tensor(prob[:, 1, :], ratio[:], prob[:, 0, :], ALU.mult))
            for k, out in ((0, eq), (1, L2)):
                ch.link(v.tensor_tensor(out[:], hot[:, k], grow(prob[:, k, :]), ALU.mult))
            ch.step(v.tensor_tensor(pr.rows[:, :, D + 1:ROW], eq[:], L2[:], ALU.add))
            ch.step(v.tensor_copy(pr.rows[:, :, D:D + 1].bitcast(I32), pr.tok[:].unsqueeze(2)))
            dve.wait_ge(ranked, 1)
            ch.link(v.tensor_copy(tiles[:], ph[1][:].rearrange("p (g e) -> p e g", e=E)))
            ch.link(v.tensor_tensor_scan(scan[:].rearrange("p e g -> p (e g)"),
                                         pr.cst[:, C_RESET:C_RESET + E * G],
                                         tiles[:].rearrange("p e g -> p (e g)"), 0.0, ALU.mult, ALU.add))
            ch.link(v.tensor_tensor(excl[:].rearrange("p g e -> p e g"), scan[:], tiles[:], ALU.subtract))
            ch.link(v.tensor_tensor(excl[:], ph[0][:].rearrange("p (g e) -> p g e", e=E), excl[:], ALU.add))
            ch.link(v.tensor_tensor(S1[:], excl[:], row_e(C_BASE), ALU.add))
            ch.link(v.tensor_scalar(excl[:], excl[:], float(CAP), float(NO_ROW), ALU.is_ge, ALU.mult))
            ch.link(v.tensor_tensor(S1[:], S1[:], excl[:], ALU.add))
            for k in range(K):
                ch.link(v.tensor_tensor(eq[:], hot[:, k], S1[:], ALU.mult))
                ch.link(v.tensor_reduce(slotf[:, k, :], eq[:], AX.X, ALU.add))
            v.tensor_copy(slot[:], slotf[:]).then_inc(routed, 1)
            with dve.Fori(0, PAIRS) as ep:
                for n in range(2 * NB):
                    for half in range(TB // 2):
                        dve.wait_ge(fc2_did, number(ep, n) * 2 + half + 1 + FC2_0)
                        dve.sem_inc(pr.passed, 1)
                        for t in (2 * half, 2 * half + 1):
                            ins = v.tensor_scalar(
                                y[n % 2][:, t, :], py[half][:, t % 2, :],
                                xr[n % 2][:, t, bass.ds(ep * 2 + (D + 1 + n // NB), 1)], None, ALU.mult)
                    ins.then_inc(y_did, 1)


_INS = ["x", "cond_1024", "L0_cond_W1", "L0_cond_b1", "L0_cond_W2", "L0_cond_b2", "L0_attn_Wq", "L0_attn_Wk",
        "L0_attn_Wv", "L0_attn_Wo", "L0_cond2_base_layer", "L0_cond2_w1", "L0_cond2_b1", "L0_cond2_w2",
        "L0_cond2_b2", "L0_cond2_ln_g", "L0_cond2_ln_b", "L0_ffn_ln1_weight", "L0_ffn_ln1_bias",
        "L0_ffn_ln2_weight", "L0_ffn_ln2_bias", "L0_ffn_qkv_weight", "L0_ffn_proj_weight",
        "L0_ffn_router_weight", "L0_ffn_moe_w1", "L0_ffn_moe_w2"]


def program(nc, dram):
    with ExitStack() as ctx:
        pr = Program(nc, ctx, dram)
        setup(pr)
        kept = ctx.enter_context(nc.sbuf_tensor("kept", [P, G, (DC + 1) * P], F32))
        pr.q = kept[:, :, 0:DC * P].rearrange("p g (c t s) -> p c g t s", c=DC, t=TG)
        pr.kv = kept[:, :, DC * P:].rearrange("p g (t s) -> p g t s", t=TG)
        pr.rows = kept[:, :, 0:ROW]
        pr.logits = ctx.enter_context(nc.sbuf_tensor("logits", [P, G, E], F32))
        sequences(pr)
        positions(pr)
        experts(pr)


def kernel(**inputs):
    import concourse.bacc as bacc
    from concourse.bass_utils import run_bass_kernel_spmd

    nc = bacc.Bacc("TRN2", target_bir_lowering=False, num_devices=1)
    table, tok = constants()
    arrays = {name: np.ascontiguousarray(inputs[name]) for name in _INS}
    for name, a in arrays.items():
        if a.shape == (D,):
            arrays[name] = np.ascontiguousarray(a.reshape(DC, P).transpose(1, 0))
    by_rows = lambda a: np.ascontiguousarray(a.reshape(DC, P, -1).transpose(1, 0, 2))
    for name in ("L0_cond_W1", "L0_cond_W2", "L0_attn_Wo"):
        arrays[name] = by_rows(arrays[name].T)
    arrays["condT"] = by_rows(arrays["cond_1024"].T)
    arrays["xT"] = np.ascontiguousarray(arrays["x"].transpose(0, 2, 1).reshape(S, DC, P, T).transpose(0, 2, 1, 3))
    proj = arrays["L0_ffn_proj_weight"].reshape(D, NKV, JQ // 2, 2, HD)
    arrays["L0_ffn_proj_weight"] = np.ascontiguousarray(proj.transpose(3, 1, 4, 2, 0).reshape(P, DC, D))
    qkv = arrays["L0_ffn_qkv_weight"].reshape(NKV, JQ + 2, HD, DC, P)
    arrays["L0_ffn_qkv_weight"] = np.ascontiguousarray(qkv.transpose(4, 3, 1, 0, 2).reshape(P, DC, QKV))
    b2 = arrays["L0_cond2_b2"].reshape(2, DC, P, RANK)
    arrays["L0_cond2_b2"] = np.ascontiguousarray(b2.transpose(2, 0, 1, 3))
    arrays["cst"], arrays["tok"] = table, tok
    dram = {name: nc.dram_tensor(f"in_{name}", a.shape, mybir.dt.from_np(a.dtype), kind="ExternalInput").ap()
            for name, a in arrays.items()}
    dram["out"] = nc.dram_tensor("out_rows", (T, S, D), F32, kind="ExternalOutput").ap()
    program(nc, dram)
    arrays = {f"in_{name}": a for name, a in arrays.items()}
    r = run_bass_kernel_spmd(nc, [arrays], core_ids=[0])
    return np.ascontiguousarray(r.results[0]["out_rows"].transpose(1, 0, 2))
```

```python
from contextlib import ExitStack

import numpy as np
import concourse.bass as bass
from concourse import mybir

F32 = mybir.dt.float32
F32R = mybir.dt.float32r
BF16 = mybir.dt.bfloat16
I32 = mybir.dt.int32
ALU = mybir.AluOpType
ACT = mybir.ActivationFunctionType
AX = mybir.AxisListType

P = 128
S, T, D = 32, 256, 256
DC = D // P
TC = T // P
RANK = 8
NH, NKV, HD = 16, 4, 16
JQ = NH // NKV
QKV = NKV * (JQ + 2) * HD
E, K, F = 8, 2, 512
FC = F // P
N = S * T
CAP = -(-N * K * 5 // (E * 4))
U1 = 4
I1 = S // U1
TG = P // S
G = T // TG
U2 = 2
I2 = G // U2
DEPTH = 3
BT = 512
NB = CAP // BT
TB = BT // P
NX = 5
AHEAD = 2
W_AT = 3
ROW = D + 1 + E
LN_EPS = 1e-5
NEG = -1e30
NO_ROW = 1 << 20
RSQRT_MAGIC = float(0x5F3759DF)
NEWTON = 3
EMPTYING = 4

C_ID, C_TRI, C_ORDER, C_SAME, C_WITHIN = 0, P, 2 * P, 3 * P, 4 * P
C_CAUSAL = 5 * P
C_HEAD = C_CAUSAL + S
C_SEL = C_HEAD + NKV
C_TIE = C_SEL + P // RANK
C_BASE = C_TIE + E
C_RESET = C_BASE + E
C_N = C_RESET + E * G


def constants():
    p = np.arange(P)
    s, t = p % S, p // S
    c = np.zeros((P, C_N), np.float32)
    c[:, C_ID:C_ID + P] = np.eye(P)
    c[:, C_TRI:C_TRI + P] = np.where(p[None, :] > p[:, None], NEG, 0)
    c[:, C_ORDER:C_ORDER + P] = s[:, None] < s[None, :]
    c[:, C_SAME:C_SAME + P] = s[:, None] == s[None, :]
    c[:, C_WITHIN:C_WITHIN + P] = (s[:, None] == s[None, :]) & (t[:, None] < t[None, :])
    c[:, C_CAUSAL:C_CAUSAL + S] = np.where(np.arange(S)[None, :] > s[:, None], NEG, 0)
    c[:, C_HEAD:C_HEAD + NKV] = (p[:, None] % (NKV * HD)) // HD == np.arange(NKV)
    c[:, C_SEL:C_SEL + P // RANK] = p[:, None] // RANK == np.arange(P // RANK)
    c[:, C_TIE:C_TIE + E] = E - np.arange(E)
    c[:, C_BASE:C_BASE + E] = np.arange(E) * CAP
    c[:, C_RESET:C_RESET + E * G] = np.tile(np.arange(G) > 0, E)
    tok = (p[:, None] + np.arange(G)[None, :] * P).astype(np.int32)
    return c, tok


class Chain:

    def __init__(self, eng, sem, base=0):
        self.eng, self.sem, self.base, self.n = eng, sem, base, 0

    def step(self, ins):
        ins.then_inc(self.sem, 1)
        self.n += 1

    def wait(self):
        self.eng.wait_ge(self.sem, self.base + self.n)

    def link(self, ins):
        self.step(ins)
        self.wait()


def inverse_root_steps(nc, chain, var, tmp, seed):
    v, a, y0, y1 = (tmp[:, k] for k in range(4))
    chain.wait()
    chain.step(nc.vector.tensor_scalar(v, var, LN_EPS, None, ALU.add))
    yield
    chain.wait()
    chain.step(nc.vector.tensor_single_scalar(seed, v.bitcast(I32), 1, ALU.logical_shift_right))
    yield
    chain.wait()
    chain.step(nc.vector.tensor_scalar(y1.bitcast(I32), seed, -1.0, RSQRT_MAGIC, ALU.mult, ALU.add))
    yield
    old, new = y1, y0
    for _ in range(NEWTON):
        chain.wait()
        chain.step(nc.vector.tensor_tensor(a, old, old, ALU.mult))
        yield
        chain.wait()
        chain.step(nc.vector.scalar_tensor_tensor(a, a, -0.5, v, ALU.mult, ALU.mult))
        yield
        chain.wait()
        chain.step(nc.vector.scalar_tensor_tensor(new, a, 1.5, old, ALU.add, ALU.mult))
        yield
        old, new = new, old


def inverse_root(nc, chain, var, tmp, seed):
    for _ in inverse_root_steps(nc, chain, var, tmp, seed):
        pass
    chain.wait()
    return tmp[:, 3 - NEWTON % 2]


class Program:

    def __init__(self, nc, ctx, dram):
        self.nc, self.ctx, self.d = nc, ctx, dram
        sb = lambda name, shape, dt=F32: ctx.enter_context(nc.sbuf_tensor(name, shape, dt))
        self.cst = sb("cst", [P, C_N])
        self.ident = self.cst[:, C_ID:C_ID + P]
        self.identb = sb("identb", [P, P], BF16)
        self.identr = sb("identr", [P, P], F32R)
        self.trib = sb("trib", [P, P], BF16)
        self.causalb = sb("causalb", [P, TG, NKV, S], BF16)
        self.gate = sb("gate", [P, DC, S])
        self.Wa = sb("Wa", [P, DC, D])
        self.Wc = sb("Wc", [P, DC, D])
        self.base = sb("base", [P, DC, D])
        self.xa = sb("xa", [P, DC, 2, P])
        self.xb = sb("xb", [P, 2, D])
        self.wqkv = sb("wqkv", [P, DC, QKV])
        self.wproj = sb("wproj", [P, DC, D])
        self.wroute = sb("wroute", [P, DC, E])
        self.ln1 = sb("ln1", [P, 2, DC])
        self.ln2 = sb("ln2", [P, 2, DC])
        self.tok = sb("tok", [P, G], I32)
        self.empty = sb("empty", [P, ROW])
        self.sem = lambda name: ctx.enter_context(nc.semaphore(name))
        self.passed = self.sem("passed")
        self.emptied = self.sem("emptied")
        self.x12 = nc.dram_tensor("x12_rows", (T, S, 2, D), F32, kind="Internal").ap()
        self.slots = nc.dram_tensor("slot_rows", (E * CAP + AHEAD * BT, ROW), F32, kind="Internal").ap()


def setup(pr):
    nc, d = pr.nc, pr.d
    with ExitStack() as ctx:
        sb = lambda name, shape, dt=F32: ctx.enter_context(nc.sbuf_tensor(name, shape, dt))
        sem = pr.sem
        ps = [ctx.enter_context(nc.psum_tensor(f"setup_ps{k}", [P, 512], F32)) for k in range(8)]
        cond = sb("cond", [S, D])
        condn = sb("condn", [S, D])
        w = {k: sb(f"s_{k}", [P, DC, D]) for k in ("Wq", "Wk", "Wv", "w1")}
        W1T, W2T, WoT = (sb(n, [P, DC, D]) for n in ("W1T", "W2T", "WoT"))
        w2 = sb("w2", [P, DC, 2 * D * RANK])
        vec = {k: sb(f"s_{k}", [P, DC]) for k in ("b1", "b2", "c2b1", "lng", "lnb")}
        b2c = sb("b2c", [P, 2, DC, RANK])
        condT, aeT, z, ez, hs, h2 = (sb(n, [P, DC, S]) for n in ("condT", "aeT", "z", "ez", "hs", "h2"))
        xbT = sb("xbT", [P, DC, 2, P])
        stats = sb("stats", [S, 6])
        mv = sb("mv", [S, 2])
        tmp = sb("tmp", [S, 4, 1])
        seed = sb("seed", [S, 1], I32)
        loaded, dve = sem("loaded"), sem("setup_dve")
        events = {}

        def event(name):
            if name not in events:
                events[name] = sem(f"done_{name}")
            return events[name]

        chunked = lambda a: a.rearrange("(c p) n -> p c n", p=P)
        block = ctx.enter_context(nc.Block())

        loads = [
            (cond[:], d["cond_1024"]), (pr.cst[:], d["cst"]), (pr.tok[:], d["tok"]),
            (W1T[:], d["L0_cond_W1"]), (W2T[:], d["L0_cond_W2"]), (WoT[:], d["L0_attn_Wo"]),
            (condT[:], d["condT"]), (pr.wproj[:], d["L0_ffn_proj_weight"]), (pr.wqkv[:], d["L0_ffn_qkv_weight"]),
            (w["Wq"][:], chunked(d["L0_attn_Wq"])), (w["Wk"][:], chunked(d["L0_attn_Wk"])),
            (w["Wv"][:], chunked(d["L0_attn_Wv"])), (w["w1"][:], chunked(d["L0_cond2_w1"])),
            (w2[:], chunked(d["L0_cond2_w2"])), (pr.base[:], chunked(d["L0_cond2_base_layer"])),
            (pr.wroute[:], chunked(d["L0_ffn_router_weight"])),
            (vec["b1"][:], d["L0_cond_b1"]), (vec["b2"][:], d["L0_cond_b2"]),
            (vec["c2b1"][:], d["L0_cond2_b1"]),
            (vec["lng"][:], d["L0_cond2_ln_g"]), (vec["lnb"][:], d["L0_cond2_ln_b"]),
            (b2c[:], d["L0_cond2_b2"]),
            (pr.ln1[:, 0, :], d["L0_ffn_ln1_weight"]), (pr.ln1[:, 1, :], d["L0_ffn_ln1_bias"]),
            (pr.ln2[:, 0, :], d["L0_ffn_ln2_weight"]), (pr.ln2[:, 1, :], d["L0_ffn_ln2_bias"]),
        ]
        all_loaded = 16 * len(loads)

        @block.sync
        def _(sp):
            for dst, src in loads:
                sp.dma_start(dst, src).then_inc(loaded, 16)
            sp.wait_ge(event("empty"), 1)
            rows = pr.slots.rearrange("(p a) c -> p a c", p=P)
            per = rows.shape[1] // EMPTYING
            for k in range(EMPTYING):
                sp.dma_start(rows[:, k * per:(k + 1) * per, :],
                             pr.empty[:, None, :].broadcast_to([P, per, ROW])).then_inc(pr.emptied, 16)

        @block.vector
        def _(dve_eng):
            ch = Chain(dve_eng, dve)
            v = nc.vector
            ch.link(v.memset(pr.empty[:], 0.0))
            v.memset(pr.empty[:, D:D + 1].bitcast(I32), NO_ROW).then_inc(event("empty"), 1)
            dve_eng.wait_ge(loaded, all_loaded)
            ch.step(v.tensor_copy(pr.identb[:], pr.ident))
            ch.step(v.tensor_copy(pr.identr[:], pr.ident))
            ch.step(v.tensor_copy(pr.trib[:], pr.cst[:, C_TRI:C_TRI + P]))
            ch.step(v.tensor_copy(pr.causalb[:].rearrange("p t g s -> p (t g) s"),
                                  pr.cst[:, None, C_CAUSAL:C_CAUSAL + S].broadcast_to([P, TG * NKV, S])))
            ch.link(v.bn_stats(stats[:], cond[:]))
            ch.link(v.bn_aggr(mv[:], stats[:]))
            rstd = inverse_root(nc, ch, mv[:, 1:2], tmp, seed[:])
            v.tensor_scalar(condn[:], cond[:], mv[:, 0:1], rstd, ALU.subtract, ALU.mult).then_inc(event("condn"), 1)
            ch.step(v.tensor_scalar(pr.wqkv[:, :, 0:D], pr.wqkv[:, :, 0:D], HD ** -0.5, None, ALU.mult))
            dve_eng.wait_ge(event("ps_condnT"), 1)
            for c in range(DC):
                ins = (v.tensor_scalar(aeT[:, c, :], ps[1][:, c * S:(c + 1) * S], vec["lng"][:, c:c + 1],
                                        vec["lnb"][:, c:c + 1], ALU.mult, ALU.add))
            ins.then_inc(event("aeT"), 1)
            dve_eng.wait_ge(event("ps_Wa"), 1)
            ch.step(v.tensor_scalar(pr.Wa[:].rearrange("p c n -> p (c n)"), ps[2][:], D ** -0.5, None, ALU.mult))
            dve_eng.wait_ge(event("ps_Wc"), 1)
            v.tensor_copy(pr.Wc[:].rearrange("p c n -> p (c n)"), ps[3][:]).then_inc(event("Wc"), 1)
            dve_eng.wait_ge(event("ps_h"), 1)
            for c in range(DC):
                ins = (v.tensor_scalar(z[:, c, :], ps[4][:, c * S:(c + 1) * S], vec["b1"][:, c:c + 1],
                                        None, ALU.add))
            ins.then_inc(event("z1"), 1)
            dve_eng.wait_ge(event("exp1"), 1)
            ch.link(v.tensor_scalar(ez[:], ez[:], 1.0, None, ALU.add))
            ch.link(v.reciprocal(ez[:], ez[:]))
            v.tensor_tensor(hs[:], z[:], ez[:], ALU.mult).then_inc(event("hs"), 1)
            dve_eng.wait_ge(event("ps_gate"), 1)
            for c in range(DC):
                ins = (v.tensor_scalar(z[:, c, :], ps[5][:, c * S:(c + 1) * S], vec["b2"][:, c:c + 1],
                                        None, ALU.add))
            ins.then_inc(event("z2"), 1)
            dve_eng.wait_ge(event("exp2"), 1)
            ch.link(v.tensor_scalar(ez[:], ez[:], 1.0, None, ALU.add))
            ch.link(v.reciprocal(ez[:], ez[:]))
            ch.step(v.tensor_scalar(pr.gate[:], ez[:], 1.0, None, ALU.add))
            for a, dst in ((0, pr.xa), (1, xbT)):
                dve_eng.wait_ge(event(f"ps_x{a}"), 1)
                for c in range(DC):
                    src = ps[a][:, c * RANK * S:(c + 1) * RANK * S].rearrange("p (r b) -> p b r", r=RANK)
                    ins = (v.tensor_tensor(
                        dst[:, c].rearrange("p h n -> p (h n)").rearrange("p (b r) -> p b r", r=RANK),
                        src, b2c[:, a, c, :].unsqueeze(1).broadcast_to([P, S, RANK]), ALU.add))
            ins.then_inc(event("xbT"), 1)
            dve_eng.wait_ge(event("ps_xb"), 1)
            ch.link(v.tensor_copy(pr.xb[:].rearrange("p h n -> p (h n)"), ps[2][:]))

        @block.tensor
        def _(pe):
            t = nc.tensor
            pe.wait_ge(loaded, all_loaded)
            pe.wait_ge(event("condn"), 1)
            for c in range(DC):
                ins = t.transpose(ps[1][:, c * S:(c + 1) * S], condn[:, c * P:(c + 1) * P], pr.ident[0:S, 0:S])
            ins.then_inc(event("ps_condnT"), 1)

            def product(name, out, lhs, rhs, after=None):
                if after:
                    pe.wait_ge(event(after), 1)
                width = rhs.shape[2]
                for mc in range(DC):
                    for kc in range(DC):
                        ins = t.matmul(out[:, mc * width:(mc + 1) * width], lhs[:, kc, mc * P:(mc + 1) * P],
                                       rhs[:, kc, :], start=(kc == 0), stop=(kc == DC - 1))
                ins.then_inc(event(f"ps_{name}"), 1)

            product("Wa", ps[2], w["Wq"], w["Wk"])
            product("Wc", ps[3], w["Wv"], WoT)
            product("h", ps[4], W1T, condT)
            product("h2", ps[6], w["w1"], aeT, after="aeT")
            product("gate", ps[5], W2T, hs, after="hs")
            pe.wait_ge(event("gelu"), 1)
            for a in range(2):
                for c in range(DC):
                    for r in range(RANK):
                        at = (c * RANK + r) * S
                        for ic in range(DC):
                            cols = w2[:, ic, a * D * RANK:(a + 1) * D * RANK].rearrange("p (k r) -> p r k", r=RANK)
                            ins = t.matmul(ps[a][:, at:at + S], cols[:, r, c * P:(c + 1) * P], h2[:, ic, :],
                                           start=(ic == 0), stop=(ic == DC - 1))
                ins.then_inc(event(f"ps_x{a}"), 1)
            pe.wait_ge(event("xbT"), 1)
            for h in range(2):
                for c in range(DC):
                    ins = t.transpose(ps[2][:, h * D + c * P:h * D + (c + 1) * P], xbT[:, c, h, :], pr.ident)
            ins.then_inc(event("ps_xb"), 1)

        @block.scalar
        def _(act):
            act.wait_ge(event("z1"), 1)
            nc.scalar.activation(ez[:], z[:], ACT.Exp, scale=-1.0).then_inc(event("exp1"), 1)
            act.wait_ge(event("z2"), 1)
            nc.scalar.activation(ez[:], z[:], ACT.Exp, scale=-1.0).then_inc(event("exp2"), 1)
            act.wait_ge(event("ps_h2"), 1)
            for c in range(DC):
                ins = nc.scalar.activation(h2[:, c, :], ps[6][:, c * S:(c + 1) * S], ACT.Gelu,
                                           bias=vec["c2b1"][:, c:c + 1])
            ins.then_inc(event("gelu"), 1)


def sequences(pr):
    nc, d = pr.nc, pr.d
    with ExitStack() as ctx:
        sb = lambda name, shape, dt=F32: ctx.enter_context(nc.sbuf_tensor(name, shape, dt))
        sem = pr.sem
        sems = lambda name: [sem(f"{name}{u}") for u in range(U1)]
        pa = [ctx.enter_context(nc.psum_tensor(f"pa{u}", [P, 512], F32)) for u in range(U1)]
        pb = [ctx.enter_context(nc.psum_tensor(f"pb{u}", [P, 512], F32)) for u in range(U1)]
        bufs = lambda name, shape: [sb(f"{name}{u}", shape) for u in range(U1)]
        x = bufs("x", [P, TC, D])
        xT = bufs("xT", [P, DC, T])
        uT = bufs("uT", [P, DC, T])
        qT = bufs("qT", [P, DC, T])
        pz = bufs("pz", [P, 512])
        pT = bufs("pT", [P, T + P])
        x1T = bufs("x1T", [P, DC, T])
        lr = bufs("lr", [P, T])
        x2T = bufs("x2T", [P, DC, T])
        x12 = bufs("x12_", [P, TC, 2, D])
        nmax, den, rden = (sb(n, [P, U1, TC]) for n in ("nmax", "den", "rden"))
        col = sb("col", [P, U1, DC + 1])
        stats = sb("stats1", [P, U1, TC, 6])
        mv = sb("mv1", [P, U1, TC, 2])
        tmp = sb("tmp1", [P, 4, U1 * TC])
        seed = sb("seed1", [P, U1 * TC], I32)
        flat = lambda a: a[:].rearrange("p c n -> p (c n)")

        x_in, xT_in = sems("x_in"), sems("xT_in")
        names_pe = "qT score pT z y low out x1 x2 nT kv".split()
        pe_did = {n: sem(f"pe_{n}_") for n in names_pe}
        names_dve = "u soft pT x1T x2T stat nrm kv".split()
        dve_did = {n: sem(f"dve_{n}_") for n in names_dve}
        names_act = "qT exp z lr x12 nT q".split()
        act_did = {n: sem(f"act_{n}_") for n in names_act}
        max_did = sem("max_found")
        stored = sems("stored")
        x1_rows, links = sem("x1_rows"), sem("links1")
        LINKS = U1 * (3 + 2 * TC) + 3 + 3 * NEWTON

        block = ctx.enter_context(nc.Block())

        @block.sync
        def _(sp):
            src = d["x"].rearrange("s (c p) n -> s p c n", p=P)
            dst = pr.x12.rearrange("(c p) s k n -> s p c (k n)", p=P)
            for u in range(U1):
                sp.sem_inc(stored[u], 16)
            with sp.Fori(0, I1) as i:
                for u in range(U1):
                    sp.wait_ge(pe_did["z"], U1 * i + u + 1)
                    sp.sem_inc(pr.passed, 1)
                    sp.dma_start(x[u][:], src[bass.ds(i + I1 * u, 1)].rearrange("a p c n -> p (a c) n")
                                 ).then_inc(x_in[u], 16)
                for u in range(U1):
                    sp.wait_ge(dve_did["x1T"], U1 * i + u + 1)
                    sp.sem_inc(pr.passed, 1)
                    sp.dma_start(xT[u][:], d["xT"][bass.ds(i + I1 * u, 1)].rearrange("a p c n -> p (a c) n")
                                 ).then_inc(xT_in[u], 16)
                for u in range(U1):
                    sp.wait_ge(act_did["x12"], U1 * i + u + 1)
                    sp.sem_inc(pr.passed, 1)
                    sp.dma_start(dst[bass.ds(i + I1 * u, 1)].rearrange("a p c n -> p (a c) n"),
                                 x12[u][:].rearrange("p c k n -> p c (k n)")).then_inc(stored[u], 16)
            for u in range(U1):
                sp.wait_ge(stored[u], 16 * (I1 + 1))

        @block.tensor
        def _(pe):
            t = nc.tensor

            def product(out, lhs, rhs, cols=T, start=True, stop=True):
                for mc in range(DC):
                    for kc in range(DC):
                        ins = t.matmul(out[:, mc * cols:(mc + 1) * cols], lhs[:, kc, mc * P:(mc + 1) * P],
                                       rhs[:, kc, :], start=start and mc == 0 and kc == 0,
                                       stop=stop and kc == DC - 1, skip_group_check=True)
                return ins

            def transposes(out, src):
                for c in range(DC):
                    for r in range(TC):
                        ins = t.transpose(out[:, c * 256 + r * P:c * 256 + (r + 1) * P],
                                          src[:, r, c * P:(c + 1) * P], pr.ident)
                return ins

            for u in range(U1):
                pe.sem_inc(pe_did["z"], 1)
                pe.sem_inc(act_did["q"], 1)
                pe.sem_inc(dve_did["kv"], 1)
                pe.sem_inc(dve_did["x1T"], 1)
            with pe.Fori(0, I1) as i:
                for u in range(U1):
                    pe.wait_ge(dve_did["kv"], U1 * i + u + 1)
                    pe.wait_ge(dve_did["u"], U1 * i + u + 1)
                    product(pb[u], pr.Wa, uT[u]).then_inc(pe_did["qT"], 1)
                for u in range(U1):
                    pe.wait_ge(act_did["q"], U1 * i + u + 1)
                    pe.wait_ge(act_did["qT"], U1 * i + u + 1)
                    for r in range(TC):
                        out = pa[u][:, r * P:r * P + (r + 1) * P]
                        for c in range(DC):
                            t.matmul(out, qT[u][:, c, r * P:(r + 1) * P], uT[u][:, c, 0:(r + 1) * P],
                                     start=(c == 0), stop=False, skip_group_check=True)
                        ins = t.matmul(out[:, r * P:(r + 1) * P], pr.identb[:], pr.trib[:],
                                       start=False, stop=True, skip_group_check=True)
                    ins.then_inc(pe_did["score"], 1)
                for u in range(U1):
                    pe.wait_ge(dve_did["soft"], U1 * i + u + 1)
                    for k in range(3):
                        ins = t.transpose(pb[u][:, k * P:(k + 1) * P], pz[u][:, k * P:(k + 1) * P], pr.ident)
                    ins.then_inc(pe_did["pT"], 1)
                for u in range(U1):
                    pe.wait_ge(dve_did["pT"], U1 * i + u + 1)
                    pe.wait_ge(x_in[u], 16 * i + 16)
                    for c in range(DC):
                        t.matmul(pa[u][:, c * T:(c + 1) * T], x[u][:, 0, c * P:(c + 1) * P], pT[u][:, 0:T],
                                 start=(c == 0), stop=False, skip_group_check=True)
                        ins = t.matmul(pa[u][:, c * T + P:(c + 1) * T], x[u][:, 1, c * P:(c + 1) * P],
                                       pT[u][:, T:T + P], start=False, stop=True, skip_group_check=True)
                    ins.then_inc(pe_did["z"], 1)
                for u in range(U1):
                    pe.wait_ge(act_did["z"], U1 * i + u + 1)
                    product(pb[u], pr.Wc, pz[u][:].rearrange("p (c n) -> p c n", c=DC)
                            ).then_inc(pe_did["y"], 1)
                for u in range(U1):
                    pe.wait_ge(dve_did["x1T"], U1 * (i + 1) + u + 1)
                    for c in range(DC):
                        ins = t.matmul(pb[u][:, 0:T], pr.xa[:, c, u // 2, :], x1T[u][:, c, :],
                                       start=(c == 0), stop=(c == DC - 1))
                    ins.then_inc(pe_did["low"], 1)
                for u in range(U1):
                    product(pa[u], pr.base, x1T[u], stop=False)
                    pe.wait_ge(act_did["lr"], U1 * i + u + 1)
                    for c in range(DC):
                        ins = t.matmul(pa[u][:, c * T:(c + 1) * T], pr.xb[:, u // 2, c * P:(c + 1) * P],
                                       lr[u][:], start=False, stop=True, skip_group_check=True)
                    ins.then_inc(pe_did["out"], 1)
                    transposes(pb[u], x1T[u]).then_inc(pe_did["x1"], 1)
                for u in range(U1):
                    pe.wait_ge(dve_did["x2T"], U1 * i + u + 1)
                    transposes(pa[u], x2T[u]).then_inc(pe_did["x2"], 1)
                for u in range(U1):
                    pe.wait_ge(dve_did["nrm"], U1 * i + u + 1)
                    transposes(pb[u], uT[u]).then_inc(pe_did["nT"], 1)
                for u in range(U1):
                    pe.wait_ge(act_did["nT"], U1 * i + u + 1)
                    for dst, c0, n in ((pb, 2 * P, 1), (pa, 0, 2)):
                        for m in range(n):
                            for c in range(DC):
                                ins = t.matmul(dst[u][:, m * T:(m + 1) * T],
                                               pr.wqkv[:, c, c0 + m * P:c0 + (m + 1) * P], qT[u][:, c, :],
                                               start=(c == 0), stop=(c == DC - 1))
                    ins.then_inc(pe_did["kv"], 1)

        @block.scalar
        def _(act):
            a = nc.scalar
            with act.Fori(0, I1) as i:
                for u in range(U1):
                    act.wait_ge(pe_did["qT"], U1 * i + u + 1)
                    a.copy(flat(qT[u]), pb[u][:]).then_inc(act_did["qT"], 1)
                for u in range(U1):
                    act.wait_ge(max_did, U1 * i + u + 1)
                    for r in range(TC):
                        cols = slice(r * P, r * P + (r + 1) * P)
                        ins = a.activation(pz[u][:, cols], pa[u][:, cols], ACT.Exp, bias=nmax[:, u, r:r + 1],
                                           accum_out=den[:, u, r:r + 1])
                    ins.then_inc(act_did["exp"], 1)
                for u in range(U1):
                    act.wait_ge(pe_did["z"], U1 * (i + 1) + u + 1)
                    for c in range(DC):
                        ins = a.activation(pz[u][:, c * T:(c + 1) * T], pa[u][:, c * T:(c + 1) * T], ACT.Copy,
                                           scale=col[:, u, c:c + 1])
                    ins.then_inc(act_did["z"], 1)
                for u in range(U1):
                    act.wait_ge(pe_did["low"], U1 * i + u + 1)
                    a.activation(lr[u][:], pb[u][:, 0:T], ACT.Copy, scale=col[:, u, DC:DC + 1]
                                 ).then_inc(act_did["lr"], 1)
                for u in range(U1):
                    act.wait_ge(pe_did["x1"], U1 * i + u + 1)
                    act.wait_ge(stored[u], 16 * i + 16)
                    a.copy(x12[u][:, :, 0, :], pb[u][:].rearrange("p (c n) -> p c n", c=TC)
                           ).then_inc(x1_rows, 1)
                for u in range(U1):
                    act.wait_ge(pe_did["x2"], U1 * i + u + 1)
                    a.copy(x12[u][:, :, 1, :], pa[u][:].rearrange("p (c n) -> p c n", c=TC)
                           ).then_inc(act_did["x12"], 1)
                for u in range(U1):
                    act.wait_ge(pe_did["nT"], U1 * i + u + 1)
                    for c in range(DC):
                        ins = a.activation(qT[u][:, c, :], pb[u][:, c * T:(c + 1) * T], ACT.Identity,
                                           scale=pr.ln1[:, 0, c:c + 1], bias=pr.ln1[:, 1, c:c + 1])
                    ins.then_inc(act_did["nT"], 1)
                for u in range(U1):
                    act.wait_ge(pe_did["kv"], U1 * i + u + 1)
                    act.sem_inc(pr.passed, 1)
                    a.copy(pr.q[:, :, :, :, bass.ds(i + I1 * u, 1)].rearrange("p c g t a -> p c g (t a)"),
                           pa[u][:].rearrange("p (c g t) -> p c g t", c=DC, g=G)).then_inc(act_did["q"], 1)

        @block.vector
        def _(dve):
            v = nc.vector
            with dve.Fori(0, I1) as i:
                ch = Chain(dve, links, i * LINKS)
                for u in range(U1):
                    ch.step(v.tensor_scalar(col[:, u, 0:DC], pr.gate[:, :, bass.ds(i + I1 * u, 1)]
                                            .rearrange("p c a -> p (c a)"), 1.0, None, ALU.mult))
                    ch.step(v.tensor_scalar(col[:, u, DC:DC + 1],
                                            pr.cst[:, bass.ds(C_SEL + i + I1 * (u % 2), 1)], 1.0, None, ALU.mult))
                ch.wait()
                for u in range(U1):
                    dve.wait_ge(xT_in[u], 16 * i + 16)
                    for c in range(DC):
                        ins = v.tensor_scalar(uT[u][:, c, :], xT[u][:, c, :], col[:, u, c:c + 1], None, ALU.mult)
                    ins.then_inc(dve_did["u"], 1)
                for u in range(U1):
                    dve.wait_ge(pe_did["score"], U1 * i + u + 1)
                    for r in range(TC):
                        ins = v.tensor_reduce(nmax[:, u, r:r + 1], pa[u][:, r * P:r * P + (r + 1) * P],
                                              AX.X, ALU.max, negate=True)
                    ins.then_inc(max_did, 1)
                for u in range(U1):
                    dve.wait_ge(act_did["exp"], U1 * i + u + 1)
                    ch.link(v.reciprocal(rden[:, u, :], den[:, u, :]))
                    for r in range(TC):
                        cols = slice(r * P, r * P + (r + 1) * P)
                        ins = v.tensor_scalar(pz[u][:, cols], pz[u][:, cols], rden[:, u, r:r + 1], None, ALU.mult)
                    ins.then_inc(dve_did["soft"], 1)
                for u in range(U1):
                    dve.wait_ge(pe_did["pT"], U1 * i + u + 1)
                    v.tensor_copy(pT[u][:], pb[u][:, 0:T + P]).then_inc(dve_did["pT"], 1)
                for u in range(U1):
                    dve.wait_ge(pe_did["y"], U1 * i + u + 1)
                    v.tensor_tensor(flat(x1T[u]), pb[u][:], flat(xT[u]), ALU.add).then_inc(dve_did["x1T"], 1)
                for u in range(U1):
                    dve.wait_ge(pe_did["out"], U1 * i + u + 1)
                    v.tensor_tensor(flat(x2T[u]), pa[u][:], flat(x1T[u]), ALU.add).then_inc(dve_did["x2T"], 1)
                for u in range(U1):
                    dve.wait_ge(act_did["x12"], U1 * i + u + 1)
                    for c in range(TC):
                        ch.step(v.bn_stats(stats[:, u, c, :], x12[u][:, c, 1, :]))
                ch.wait()
                dve.sem_inc(pr.passed, 1)
                for u in range(U1):
                    for c in range(TC):
                        ch.step(v.bn_aggr(mv[:, u, c, :], stats[:, u, c, :]))
                ch.wait()
                rstd = inverse_root(nc, ch, mv[:].rearrange("p u c k -> p (u c) k")[:, :, 1], tmp, seed[:])
                for u in range(U1):
                    for c in range(TC):
                        k = u * TC + c
                        ins = v.tensor_scalar(uT[u][:, c, :], x12[u][:, c, 1, :], mv[:, u, c, 0:1],
                                              rstd[:, k:k + 1], ALU.subtract, ALU.mult)
                    ins.then_inc(dve_did["nrm"], 1)
                for u in range(U1):
                    dve.wait_ge(pe_did["kv"], U1 * i + u + 1)
                    dve.sem_inc(pr.passed, 1)
                    v.tensor_copy(pr.kv[:, :, :, bass.ds(i + I1 * u, 1)].rearrange("p g t a -> p g (t a)"),
                                  pb[u][:, 0:T].rearrange("p (g t) -> p g t", g=G)).then_inc(dve_did["kv"], 1)
                assert ch.n == LINKS, ch.n


def positions(pr):
    nc, d = pr.nc, pr.d
    with ExitStack() as ctx:
        sb = lambda name, shape, dt=F32: ctx.enter_context(nc.sbuf_tensor(name, shape, dt))
        sem = pr.sem
        sems = lambda name: [sem(f"{name}{u}") for u in range(U2)]
        bank = lambda name: [ctx.enter_context(nc.psum_tensor(f"{name}{u}", [P, 512], F32)) for u in range(U2)]
        ps_s, ps_w, ps_v, ps_h = (bank(n) for n in ("gs", "gw", "gv", "gh"))
        bufs = lambda name, shape: [sb(f"{name}{u}", shape) for u in range(U2)]
        KV1 = NKV * HD
        qg = bufs("qg", [KV1, TG, JQ, S])
        kvd = bufs("kvd", [P, TG, NKV, S])
        pw = bufs("pw", [P, TG * NKV, S])
        pwT = bufs("pwT", [P, TG, JQ, S])
        vb = bufs("vb", [P, TG, KV1])
        aoT = bufs("aoT", [P, 2, TG, S])
        x12 = bufs("xg", [P, 2, D])
        h1 = bufs("h1", [P, D])
        res = bufs("res", [P, D])
        nrm = bufs("nrm", [P, D])
        nT = bufs("nT", [P, DC, P])
        nmax, den = (sb(n, [P, U2, TG * NKV]) for n in ("gmax", "gden"))
        stats = sb("stats2", [P, U2, 6])
        mv = sb("mv2", [P, U2, 2])
        tmp = sb("tmp2", [P, 4, U2])
        seed = sb("seed2", [P, U2], I32)

        x_in, stored = sems("g_x_in"), sems("g_stored")
        pe_did = {n: sem(f"gpe_{n}_") for n in "score vT wT av h nT logit".split()}
        dve_did = {n: sem(f"gdve_{n}_") for n in "max sub sum rden h1 nrm logit".split()}
        act_did = {n: sem(f"gact_{n}_") for n in "q exp wT v ao nT rows".split()}
        pool_did = {n: sem(f"gpool_{n}_") for n in "kv soft res".split()}
        links = sem("links2")
        LINKS = U2 * 2 + 3 + 3 * NEWTON
        group = lambda j, u: j * U2 + u
        places = range(U2)

        def after(eng, sem, j, u):
            if not (isinstance(j, int) and j < 0):
                eng.wait_ge(sem, j * U2 + (u + 1))

        def pipeline(eng, step):
            has = lambda j: 0 <= j < I2
            for k in range(-1, DEPTH + 1):
                step(k, has)
            with eng.Fori(0, I2 - 2 - DEPTH) as i:
                step(i + (DEPTH + 1), lambda j: True)
            for k in range(I2 - 1, I2 + DEPTH):
                step(k, has)

        block = ctx.enter_context(nc.Block())

        @block.sync
        def _(sp):
            src = pr.x12.rearrange("(g t) s k n -> g (t s) (k n)", t=TG)
            dst = pr.d["out"].rearrange("(g t) s n -> g (t s) n", t=TG)

            def load(j, u):
                sp.dma_start(x12[u][:].rearrange("p k n -> p (k n)"),
                             src[bass.ds(group(j, u), 1)].rearrange("a p n -> (a p) n")).then_inc(x_in[u], 16)

            def store(j, u):
                after(sp, pool_did["res"], j, u)
                sp.sem_inc(pr.passed, 1)
                sp.dma_start(dst[bass.ds(group(j, u), 1)].rearrange("a p n -> (a p) n"), res[u][:]
                             ).then_inc(stored[u], 16)

            for u in places:
                load(0, u)
            with sp.Fori(0, I2 - 1) as j:
                for u in places:
                    store(j, u)
                    load(j + 1, u)
            for u in places:
                store(I2 - 1, u)
            for u in places:
                sp.wait_ge(stored[u], 16 * I2)

        @block.gpsimd
        def _(pool):
            g = nc.gpsimd

            def step(k, has):
                if has(k - 2):
                    for u in places:
                        after(pool, dve_did["h1"], k - 2, u)
                        if not isinstance(k, int) or k > 2:
                            pool.wait_ge(stored[u], 16 * (k - 2))
                        g.tensor_tensor(res[u][:], x12[u][:, 0, :], h1[u][:], ALU.add
                                        ).then_inc(pool_did["res"], 1)
                if has(k):
                    for u in places:
                        after(pool, dve_did["rden"], k, u)
                        g.tensor_tensor(pw[u][:], pw[u][:], den[:, u, :].unsqueeze(2)
                                        .broadcast_to([P, TG * NKV, S]), ALU.mult).then_inc(pool_did["soft"], 1)
                if has(k + 1):
                    for u in places:
                        after(pool, pe_did["vT"], k, u)
                        g.tensor_tensor(kvd[u][:],
                                        pr.kv[:, bass.ds(group(k + 1, u), 1)].rearrange("p a t s -> p (a t) s")
                                        .unsqueeze(2).broadcast_to([P, TG, NKV, S]),
                                        pr.cst[:, C_HEAD:C_HEAD + NKV].unsqueeze(1).unsqueeze(3)
                                        .broadcast_to([P, TG, NKV, S]), ALU.mult).then_inc(pool_did["kv"], 1)

            pipeline(pool, step)

        @block.tensor
        def _(pe):
            t_ = nc.tensor

            def step(k, has):
                if has(k - 2):
                    for u in places:
                        after(pe, dve_did["logit"], k - 4, u)
                        after(pe, act_did["ao"], k - 2, u)
                        for h in range(2):
                            ins = t_.matmul(ps_h[u][:, 0:D], aoT[u][:, h].rearrange("p t s -> p (t s)"),
                                            pr.wproj[:, h, :], start=(h == 0), stop=(h == 1))
                        ins.then_inc(pe_did["h"], 1)
                if has(k - 1):
                    for u in places:
                        after(pe, pool_did["soft"], k - 1, u)
                        for t in range(TG):
                            ins = t_.transpose(ps_w[u][:, t * P:(t + 1) * P],
                                       pw[u][:, t * NKV:(t + 1) * NKV, :].rearrange("p g s -> p (g s)"), pr.ident)
                        ins.then_inc(pe_did["wT"], 1)
                if has(k - 3):
                    for u in places:
                        if has(k - 2):
                            after(pe, dve_did["h1"], k - 2, u)
                        after(pe, dve_did["nrm"], k - 3, u)
                        for c in range(DC):
                            ins = t_.transpose(ps_h[u][:, 256 + c * P:256 + (c + 1) * P],
                                       nrm[u][:, c * P:(c + 1) * P], pr.ident)
                        ins.then_inc(pe_did["nT"], 1)
                if has(k):
                    for u in places:
                        t_.matmul(ps_s[u][:], pr.identb[:], pr.causalb[:].rearrange("p t g s -> p (t g s)"),
                                  start=True, stop=False, skip_group_check=True)
                        after(pe, act_did["q"], k, u)
                        after(pe, pool_did["kv"], k, u)
                        for t in range(TG):
                            ins = t_.matmul(ps_s[u][:, t * P:(t + 1) * P], qg[u][:, t].rearrange("p j s -> p (j s)"),
                                            kvd[u][0:KV1, t].rearrange("p g s -> p (g s)"),
                                            start=False, stop=True, skip_group_check=True)
                        ins.then_inc(pe_did["score"], 1)
                if has(k - 3):
                    for u in places:
                        after(pe, act_did["nT"], k - 3, u)
                        for c in range(DC):
                            ins = t_.matmul(ps_h[u][:, 256:256 + E], nT[u][:, c, :], pr.wroute[:, c, :],
                                            start=(c == 0), stop=(c == DC - 1))
                        ins.then_inc(pe_did["logit"], 1)
                if has(k - 1):
                    for u in places:
                        after(pe, act_did["wT"], k - 1, u)
                        after(pe, act_did["v"], k - 1, u)
                        for jp in range(2):
                            for t in range(TG):
                                out = ps_v[u][jp * KV1:(jp + 1) * KV1, 256:512].rearrange(
                                    "p (h t s) -> p h t s", h=2, t=TG)
                                ins = t_.matmul(out[:, :, t, :], vb[u][:, t, :], pwT[u][:, t, jp::2, :],
                                                start=True, stop=True, skip_group_check=True)
                        ins.then_inc(pe_did["av"], 1)
                if has(k):
                    for u in places:
                        after(pe, act_did["ao"], k - 1, u)
                        pe.sem_inc(pr.passed, 1)
                        for t in range(TG):
                            ins = t_.transpose(ps_v[u][:, t * KV1:(t + 1) * KV1],
                                       kvd[u][KV1:P, t].rearrange("p g s -> p (g s)"),
                                       pr.cst[KV1:P, C_ID + KV1:C_ID + P])
                        ins.then_inc(pe_did["vT"], 1)

            pipeline(pe, step)

        @block.scalar
        def _(act):
            a = nc.scalar
            a.activation(tmp[:, 0, 0:1], pr.cst[:, 0:1], ACT.Exp).then_inc(links, 1)

            def step(k, has):
                if has(k - 1):
                    for u in places:
                        after(act, pe_did["wT"], k - 1, u)
                        a.copy(pwT[u][:].rearrange("p t j s -> p (t j s)"), ps_w[u][:]
                               ).then_inc(act_did["wT"], 1)
                if has(k - 3):
                    for u in places:
                        after(act, pe_did["nT"], k - 3, u)
                        for c in range(DC):
                            ins = a.activation(nT[u][:, c, :], ps_h[u][:, 256 + c * P:256 + (c + 1) * P],
                                               ACT.Identity, scale=pr.ln2[:, 0, c:c + 1],
                                               bias=pr.ln2[:, 1, c:c + 1])
                        ins.then_inc(act_did["nT"], 1)
                if has(k):
                    for u in places:
                        after(act, dve_did["sub"], k, u)
                        a.activation(pw[u][:], pw[u][:], ACT.Exp).then_inc(act_did["exp"], 1)
                if has(k - 1):
                    for u in places:
                        after(act, pe_did["av"], k - 1, u)
                        a.copy(aoT[u][:].rearrange("p h t s -> p (h t s)"), ps_v[u][:, 256:512]
                               ).then_inc(act_did["ao"], 1)
                if has(k):
                    for u in places:
                        after(act, pe_did["vT"], k, u)
                        a.copy(vb[u][:].rearrange("p t n -> p (t n)"), ps_v[u][:, 0:TG * KV1]
                               ).then_inc(act_did["v"], 1)
                if has(k + 1):
                    for u in places:
                        after(act, pe_did["score"], k, u)
                        act.sem_inc(pr.passed, 1)
                        for jp in range(2):
                            ins = a.copy(
                                qg[u][:].rearrange("p t j s -> p j t s")[:, jp::2],
                                pr.q[jp * KV1:(jp + 1) * KV1, :, bass.ds(group(k + 1, u), 1)]
                                .rearrange("p c a t s -> p c (a t) s"))
                        ins.then_inc(act_did["q"], 1)
                if has(k - 2):
                    for u in places:
                        after(act, dve_did["nrm"], k - 2, u)
                        act.sem_inc(pr.passed, 1)
                        a.copy(pr.rows[:, bass.ds(group(k - 2, u), 1), 0:D].rearrange("p a n -> p (a n)"),
                               nrm[u][:]).then_inc(act_did["rows"], 1)

            pipeline(act, step)

        @block.vector
        def _(dve):
            v = nc.vector
            dve.wait_ge(links, 1)

            def step(k, has):
                norm, score, route = has(k - 2), has(k), has(k - 3)
                root = iter(())
                if norm:
                    ch = Chain(dve, links, (k - 2) * LINKS + 1)
                    for u in places:
                        after(dve, pool_did["res"], k - 3, u)
                        after(dve, dve_did["nrm"], k - 3, u)
                        dve.wait_ge(x_in[u], 16 * (k - 1))
                        after(dve, pe_did["h"], k - 2, u)
                        v.tensor_tensor(h1[u][:], ps_h[u][:, 0:D], x12[u][:, 1, :], ALU.add
                                        ).then_inc(dve_did["h1"], 1)
                    for u in places:
                        after(dve, dve_did["h1"], k - 2, u)
                        ch.step(v.bn_stats(stats[:, u, :], h1[u][:]))
                if norm:
                    ch.wait()
                    dve.sem_inc(pr.passed, 1)
                    for u in places:
                        ch.step(v.bn_aggr(mv[:, u, :], stats[:, u, :]))
                    root = inverse_root_steps(nc, ch, mv[:, :, 1], tmp, seed[:])
                if score:
                    for u in places:
                        after(dve, pe_did["score"], k, u)
                        v.tensor_reduce(nmax[:, u, :], ps_s[u][:].rearrange("p (n s) -> p n s", s=S),
                                        AX.X, ALU.max).then_inc(dve_did["max"], 1)
                        next(root, None)
                        after(dve, dve_did["max"], k, u)
                        v.tensor_tensor(pw[u][:], ps_s[u][:].rearrange("p (n s) -> p n s", s=S),
                                        nmax[:, u, :].unsqueeze(2).broadcast_to([P, TG * NKV, S]),
                                        ALU.subtract).then_inc(dve_did["sub"], 1)
                        next(root, None)
                    next(root, None)
                if route:
                    for u in places:
                        after(dve, pe_did["logit"], k - 3, u)
                        v.tensor_scalar(pr.logits[:, bass.ds(group(k - 3, u), 1), :].rearrange("p a n -> p (a n)"),
                                        ps_h[u][:, 256:256 + E], 1.0, None, ALU.mult
                                        ).then_inc(dve_did["logit"], 1)
                if score:
                    for u in places:
                        after(dve, act_did["exp"], k, u)
                        v.tensor_reduce(den[:, u, :], pw[u][:], AX.X, ALU.add).then_inc(dve_did["sum"], 1)
                        next(root, None)
                        after(dve, dve_did["sum"], k, u)
                        v.reciprocal(den[:, u, :], den[:, u, :]).then_inc(dve_did["rden"], 1)
                        next(root, None)
                if norm:
                    for _ in root:
                        pass
                    ch.wait()
                    rstd = tmp[:, 3 - NEWTON % 2]
                    for u in places:
                        after(dve, pe_did["nT"], k - 3, u)
                        after(dve, act_did["rows"], k - 3, u)
                        v.tensor_scalar(nrm[u][:], h1[u][:], mv[:, u, 0:1], rstd[:, u:u + 1],
                                        ALU.subtract, ALU.mult).then_inc(dve_did["nrm"], 1)
                    assert ch.n == LINKS, ch.n

            pipeline(dve, step)


def dispatch(pr):
    nc, d = pr.nc, pr.d
    with ExitStack() as ctx:
        sb = lambda name, shape, dt=F32: ctx.enter_context(nc.sbuf_tensor(name, shape, dt))
        sem = pr.sem
        ph = [ctx.enter_context(nc.psum_tensor(f"ph{f}", [P, G * E], F32)) for f in range(2)]
        L2, eq, S1, excl = (sb(n, [P, G, E]) for n in ("L2", "eq", "S1", "excl"))
        hot = sb("hot", [P, K, G, E])
        best, top = sb("best", [P, K, G]), sb("top", [P, G])
        ratio, prob = sb("ratio", [P, G]), sb("prob", [P, K, G])
        slotf, slot = sb("slotf", [P, K, G]), sb("slot", [P, K, G], I32)
        chosen = sb("chosen", [P, G, E], BF16)
        total, totalb = sb("total", [P, E]), sb("totalb", [P, E], BF16)
        order = sb("order", [P, 3, P], BF16)
        tiles = sb("tiles", [P, E, G])
        scan = sb("scan", [P, E, G])
        links, ratio_in, ratio_did, ranked = sem("links3"), sem("ratio_in"), sem("ratio_did"), sem("ranked")
        chosen_did, routed, dispatched = sem("chosen_did"), sem("routed"), sem("dispatched")
        grow = lambda a: a.unsqueeze(2).broadcast_to([P, G, E])
        row_e = lambda c0: pr.cst[:, c0:c0 + E].unsqueeze(1).broadcast_to([P, G, E])

        block = ctx.enter_context(nc.Block())

        @block.gpsimd
        def _(pool):
            g = nc.gpsimd
            pool.wait_ge(pr.emptied, 16 * EMPTYING)
            pool.wait_ge(routed, 1)
            for j in range(G):
                for k in range(K):
                    g.indirect_dma_start(
                        out=pr.slots, out_offset=bass.IndirectOffsetOnAxis(ap=slot[:, k, j:j + 1], axis=0),
                        in_=pr.rows[:, j, :], in_offset=None, bounds_check=E * CAP - 1, oob_is_err=False,
                    ).then_inc(dispatched, 16)
            pool.wait_ge(dispatched, 16 * K * G)

        @block.tensor
        def _(pe):
            t_ = nc.tensor
            flat = lambda a: a.rearrange("p g e -> p (g e)")
            pe.wait_ge(chosen_did, 1)
            t_.matmul(ph[0][:], order[:, 2, :], flat(chosen[:]), start=True, stop=False)
            t_.matmul(ph[0][:], order[:, 0, :], totalb[:].unsqueeze(1).broadcast_to([P, G, E]),
                      start=False, stop=True)
            t_.matmul(ph[1][:], order[:, 1, :], flat(chosen[:]), start=True, stop=True).then_inc(ranked, 1)

        @block.scalar
        def _(act):
            a = nc.scalar
            act.wait_ge(ratio_in, 1)
            a.activation(ratio[:], ratio[:], ACT.Exp).then_inc(ratio_did, 1)

        @block.vector
        def _(dve):
            v = nc.vector
            ch = Chain(dve, links)
            ch.step(v.tensor_copy(order[:].rearrange("p k n -> p (k n)"), pr.cst[:, C_ORDER:C_ORDER + 3 * P]))
            source = pr.logits
            for k in range(K):
                ch.link(v.tensor_reduce(best[:, k, :], source[:], AX.X, ALU.max))
                ch.link(v.tensor_tensor(eq[:], source[:], grow(best[:, k, :]), ALU.is_equal))
                ch.link(v.tensor_tensor(eq[:], eq[:], row_e(C_TIE), ALU.mult))
                ch.link(v.tensor_reduce(top[:], eq[:], AX.X, ALU.max))
                ch.link(v.tensor_tensor(hot[:, k], eq[:], grow(top[:]), ALU.is_equal))
                if k == 0:
                    ch.link(v.scalar_tensor_tensor(L2[:].rearrange("p g e -> p (g e)"),
                                                   hot[:, 0].rearrange("p g e -> p (g e)"), NEG,
                                                   pr.logits[:].rearrange("p g e -> p (g e)"),
                                                   ALU.mult, ALU.add))
                    source = L2
            v.tensor_tensor(ratio[:], best[:, 1, :], best[:, 0, :], ALU.subtract).then_inc(ratio_in, 1)
            ch.link(v.tensor_tensor(chosen[:], hot[:, 0], hot[:, 1], ALU.add))
            ch.link(v.tensor_reduce(total[:], chosen[:].rearrange("p g e -> p e g"), AX.X, ALU.add))
            v.tensor_copy(totalb[:], total[:]).then_inc(chosen_did, 1)
            dve.wait_ge(ratio_did, 1)
            ch.link(v.tensor_scalar(prob[:, 1, :], ratio[:], 1.0, None, ALU.add))
            ch.link(v.reciprocal(prob[:, 0, :], prob[:, 1, :]))
            ch.link(v.tensor_tensor(prob[:, 1, :], ratio[:], prob[:, 0, :], ALU.mult))
            for k, out in ((0, eq), (1, L2)):
                ch.link(v.tensor_tensor(out[:], hot[:, k], grow(prob[:, k, :]), ALU.mult))
            ch.step(v.tensor_tensor(pr.rows[:, :, D + 1:ROW], eq[:], L2[:], ALU.add))
            ch.step(v.tensor_copy(pr.rows[:, :, D:D + 1].bitcast(I32), pr.tok[:].unsqueeze(2)))
            dve.wait_ge(ranked, 1)
            ch.link(v.tensor_copy(tiles[:], ph[1][:].rearrange("p (g e) -> p e g", e=E)))
            ch.link(v.tensor_tensor_scan(scan[:].rearrange("p e g -> p (e g)"),
                                         pr.cst[:, C_RESET:C_RESET + E * G],
                                         tiles[:].rearrange("p e g -> p (e g)"), 0.0, ALU.mult, ALU.add))
            ch.link(v.tensor_tensor(excl[:].rearrange("p g e -> p e g"), scan[:], tiles[:], ALU.subtract))
            ch.link(v.tensor_tensor(excl[:], ph[0][:].rearrange("p (g e) -> p g e", e=E), excl[:], ALU.add))
            ch.link(v.tensor_tensor(S1[:], excl[:], row_e(C_BASE), ALU.add))
            ch.link(v.tensor_scalar(excl[:], excl[:], float(CAP), float(NO_ROW), ALU.is_ge, ALU.mult))
            ch.link(v.tensor_tensor(S1[:], S1[:], excl[:], ALU.add))
            for k in range(K):
                ch.link(v.tensor_tensor(eq[:], hot[:, k], S1[:], ALU.mult))
                ch.link(v.tensor_reduce(slotf[:, k, :], eq[:], AX.X, ALU.add))
            v.tensor_copy(slot[:], slotf[:]).then_inc(routed, 1)


def experts(pr):
    nc, d = pr.nc, pr.d
    with ExitStack() as ctx:
        sb = lambda name, shape, dt=F32: ctx.enter_context(nc.sbuf_tensor(name, shape, dt))
        sem = pr.sem
        ph = [ctx.enter_context(nc.psum_tensor(f"ph_{f}", [P, BT], F32)) for f in range(FC)]
        pt = [ctx.enter_context(nc.psum_tensor(f"pt_{c}", [P, BT], F32)) for c in range(DC)]
        py = [ctx.enter_context(nc.psum_tensor(f"py_{c}", [P, 2, D], F32)) for c in range(TB // 2)]
        w1, w2 = sb("w1e", [P, DC, F]), sb("w2e", [P, FC, D])
        w1h, w1l = ([sb(f"{n}{k}", [P, DC, F], F32R) for k in range(2)] for n in ("w1h", "w1l"))
        w2h, w2l = ([sb(f"{n}{k}", [P, FC, D], F32R) for k in range(2)] for n in ("w2h", "w2l"))
        xr = [sb(f"xr{k}", [P, TB, ROW]) for k in range(NX)]
        xT = sb("xTe", [P, DC, BT])
        xh, xl = sb("xh", [P, DC, BT], F32R), sb("xl", [P, DC, BT], F32R)
        h = [sb(f"h{k}", [P, FC, BT]) for k in range(2)]
        hh, hl = ([sb(f"{n}{k}", [P, FC, BT], F32R) for k in range(2)] for n in ("hh", "hl"))
        y = [sb(f"y{k}", [P, TB, D]) for k in range(2)]

        w_in, w_split = sem("w_in"), sem("w_split")
        x_in = [sem(f"xr_in{k}") for k in range(NX)]
        added, settled = sem("added"), sem("settled")
        turned, xh_did, xl_did = sem("turned"), sem("xh_did"), sem("xl_did")
        fc1_did, gelu_did, hl_did = sem("fc1_did"), sem("gelu_did"), sem("hl_did")
        fc2_did, y_did = sem("fc2_did"), sem("y_did")
        STEPS = 2 * NB
        PAIRS = E // 2
        number = lambda ep, n: ep * STEPS + n
        pieces = [(w1, w1h, w1l, 0), (w1, w1h, w1l, 1), (w2, w2h, w2l, 0), (w2, w2h, w2l, 1)]

        block = ctx.enter_context(nc.Block())

        @block.sync
        def _(sp):
            src = pr.slots.rearrange("(n t p) c -> n p t c", t=TB, p=P)
            w1_d = d["L0_ffn_moe_w1"].rearrange("e (c p) f -> e p c f", p=P)
            w2_d = d["L0_ffn_moe_w2"].rearrange("e (c p) n -> e p c n", p=P)

            def load_w(e):
                for dst, w in ((w1, w1_d), (w2, w2_d)):
                    sp.dma_start(dst[:], w[bass.ds(e, 1)].rearrange("a p c f -> p (a c) f")).then_inc(w_in, 16)

            def load_x(m, buf):
                sp.wait_ge(settled, m + 1)
                sp.sem_inc(pr.passed, 1)
                sp.dma_start(xr[buf][:], src[bass.ds(m, 1)].rearrange("a p t c -> p (a t) c")
                             ).then_inc(x_in[buf], 16)

            load_w(0)
            sp.sem_inc(settled, NX)
            with sp.Fori(0, PAIRS) as ep:
                for n in range(STEPS):
                    if n % NB == W_AT:
                        sp.wait_ge(w_split, (ep * 2 + n // NB + 1) * 2 * len(pieces))
                        sp.sem_inc(pr.passed, 1)
                        load_w(ep * 2 + n // NB + 1)
                    load_x(number(ep, n), n % NX)
            for m in range(PAIRS * STEPS, PAIRS * STEPS + AHEAD):
                load_x(m, m % NX)
            for m in range(PAIRS * STEPS, PAIRS * STEPS + AHEAD):
                sp.wait_ge(x_in[m % NX], 16 * (m // NX + 1))

        @block.gpsimd
        def _(pool):
            g = nc.gpsimd
            out = d["out"].rearrange("t s n -> (t s) n")
            with pool.Fori(0, PAIRS) as ep:
                for n in range(STEPS):
                    pool.wait_ge(y_did, number(ep, n) + 2)
                    pool.sem_inc(pr.passed, 1)
                    for t in range(TB):
                        g.indirect_dma_start(
                            out=out, out_offset=bass.IndirectOffsetOnAxis(
                                ap=xr[n % NX][:, t, D:D + 1].bitcast(I32), axis=0),
                            in_=y[n % 2][:, t, :], in_offset=None, bounds_check=N - 1, oob_is_err=False,
                            compute_op=ALU.add).then_inc(added, 16)
                    pool.wait_ge(added, 16 * TB * (number(ep, n) + 1))
                    pool.sem_inc(settled, 1)

        @block.tensor
        def _(pe):
            t_ = nc.tensor

            def turn(m, buf):
                pe.wait_ge(x_in[buf], 16 * (m + 1))
                for c in range(DC):
                    for t in range(TB):
                        ins = t_.transpose(pt[c][:, t * P:(t + 1) * P].bitcast(F32R),
                                           xr[buf][:, t, c * P:(c + 1) * P].bitcast(F32R), pr.identr[:])
                ins.then_inc(turned, 1)

            def three(out, a, b, at_a, at_b, first, last):
                (ah, al), (bh, bl) = a, b
                t_.matmul(out, at_a(ah), at_b(bh), start=first, stop=False)
                t_.matmul(out, at_a(ah), at_b(bl), start=False, stop=False)
                return t_.matmul(out, at_a(al), at_b(bh), start=False, stop=last)

            def layer1(m, k, free=True):
                pe.wait_ge(xl_did, m + 1)
                for f in range(FC):
                    if free:
                        pe.wait_ge(gelu_did, (m - 1) * FC + f + 1)
                    for c in range(DC):
                        ins = three(ph[f][:], (w1h[k], w1l[k]), (xh, xl), lambda w: w[:, c, f * P:(f + 1) * P],
                                    lambda x: x[:, c, :], c == 0, c == DC - 1)
                    ins.then_inc(fc1_did, 1)

            def layer2(m, n, k):
                pe.wait_ge(hl_did, (m + 1) * FC)
                pe.wait_ge(y_did, m + 1)
                for t in range(TB):
                    for f in range(FC):
                        ins = three(py[t // 2][:, t % 2, :], (hh[n % 2], hl[n % 2]), (w2h[k], w2l[k]),
                                    lambda x: x[:, f, t * P:(t + 1) * P], lambda w: w[:, f, :],
                                    f == 0, f == FC - 1)
                    if t % 2:
                        ins.then_inc(fc2_did, 1)

            pe.sem_inc(y_did, 1)
            turn_count = lambda ep, n: ep * (STEPS // NX) + n // NX
            turn(0, 0)
            pe.wait_ge(w_split, 4)
            layer1(0, 0, free=False)
            turn(0, 1)
            with pe.Fori(0, PAIRS) as ep:
                for n in range(STEPS):
                    e = ep * 2 + n // NB
                    if n % NB == NB - 1:
                        pe.wait_ge(w_split, (e + 1) * 8 + 4)
                    layer1(number(ep, n) + 1, (n + 1) // NB % 2)
                    turn(turn_count(ep, n + 2), (n + 2) % NX)
                    if n % NB == 0:
                        pe.wait_ge(w_split, (e + 1) * 8)
                    layer2(number(ep, n), n, n // NB)

        @block.scalar
        def _(act):
            a = nc.scalar

            def features(m):
                act.wait_ge(turned, m + 1)
                for out in (xh, xT):
                    for c in range(DC):
                        ins = a.activation(out[:, c, :], pt[c][:], ACT.Identity,
                                           scale=pr.ln2[:, 0, c:c + 1], bias=pr.ln2[:, 1, c:c + 1])
                ins.then_inc(xh_did, 1)

            def gelu(m, n):
                for f in range(FC):
                    act.wait_ge(fc1_did, m * FC + f + 1)
                    a.activation(hh[n % 2][:, f, :], ph[f][:], ACT.Gelu_apprx_tanh)
                    a.activation(h[n % 2][:, f, :], ph[f][:], ACT.Gelu_apprx_tanh).then_inc(gelu_did, 1)

            features(0)
            gelu(0, 0)
            features(1)
            with act.Fori(0, PAIRS) as ep:
                for n in range(STEPS):
                    gelu(number(ep, n) + 1, n + 1)
                    features(number(ep, n) + 2)

        @block.vector
        def _(dve):
            v = nc.vector

            def split(e, k, piece):
                src, high, low, half = pieces[piece]
                cols = lambda a: a[:].rearrange("p c n -> p (c n)")[:, half * 512:(half + 1) * 512]
                v.tensor_copy(cols(high[k]), cols(src)).then_inc(w_split, 1)
                dve.wait_ge(w_split, (e * len(pieces) + piece) * 2 + 1)
                v.tensor_tensor(cols(low[k]), cols(src), cols(high[k]).bitcast(F32), ALU.subtract
                                ).then_inc(w_split, 1)

            def x_rest(m):
                dve.wait_ge(xh_did, m + 1)
                v.tensor_tensor(xl[:], xT[:], xh[:].bitcast(F32), ALU.subtract).then_inc(xl_did, 1)

            def h_rest(m, n):
                for f in range(FC):
                    dve.wait_ge(gelu_did, m * FC + f + 1)
                    v.tensor_tensor(hl[n % 2][:, f, :], h[n % 2][:, f, :], hh[n % 2][:, f, :].bitcast(F32),
                                    ALU.subtract).then_inc(hl_did, 1)

            dve.wait_ge(w_in, 32)
            for piece in (0, 1):
                split(0, 0, piece)
            x_rest(0)
            for piece in (2, 3):
                split(0, 0, piece)
            h_rest(0, 0)
            x_rest(1)
            with dve.Fori(0, PAIRS) as ep:
                for n in range(STEPS):
                    m = number(ep, n)
                    h_rest(m + 1, n + 1)
                    x_rest(m + 2)
                    dve.wait_ge(settled, m + NX - 1)
                    for half in range(TB // 2):
                        dve.wait_ge(fc2_did, m * 2 + half + 1)
                        dve.sem_inc(pr.passed, 1)
                        for t in (2 * half, 2 * half + 1):
                            ins = v.tensor_scalar(
                                y[n % 2][:, t, :], py[half][:, t % 2, :],
                                xr[n % NX][:, t, bass.ds(ep * 2 + (D + 1 + n // NB), 1)], None, ALU.mult)
                    ins.then_inc(y_did, 1)
                    if n % NB > 0:
                        if n % NB == 1:
                            dve.wait_ge(w_in, 32 * (ep * 2 + n // NB + 2))
                        split(ep * 2 + n // NB + 1, (n // NB + 1) % 2, n % NB - 1)


_INS = ["x", "cond_1024", "L0_cond_W1", "L0_cond_b1", "L0_cond_W2", "L0_cond_b2", "L0_attn_Wq", "L0_attn_Wk",
        "L0_attn_Wv", "L0_attn_Wo", "L0_cond2_base_layer", "L0_cond2_w1", "L0_cond2_b1", "L0_cond2_w2",
        "L0_cond2_b2", "L0_cond2_ln_g", "L0_cond2_ln_b", "L0_ffn_ln1_weight", "L0_ffn_ln1_bias",
        "L0_ffn_ln2_weight", "L0_ffn_ln2_bias", "L0_ffn_qkv_weight", "L0_ffn_proj_weight",
        "L0_ffn_router_weight", "L0_ffn_moe_w1", "L0_ffn_moe_w2"]


def program(nc, dram):
    with ExitStack() as ctx:
        pr = Program(nc, ctx, dram)
        setup(pr)
        with ExitStack() as inner:
            kept = inner.enter_context(nc.sbuf_tensor("kept", [P, G, (DC + 1) * P], F32))
            pr.q = kept[:, :, 0:DC * P].rearrange("p g (c t s) -> p c g t s", c=DC, t=TG)
            pr.kv = kept[:, :, DC * P:].rearrange("p g (t s) -> p g t s", t=TG)
            pr.rows = kept[:, :, 0:ROW]
            pr.logits = inner.enter_context(nc.sbuf_tensor("logits", [P, G, E], F32))
            sequences(pr)
            positions(pr)
            dispatch(pr)
        experts(pr)


def kernel(**inputs):
    import concourse.bacc as bacc
    from concourse.bass_utils import run_bass_kernel_spmd

    nc = bacc.Bacc("TRN2", target_bir_lowering=False, num_devices=1)
    table, tok = constants()
    arrays = {name: np.ascontiguousarray(inputs[name]) for name in _INS}
    for name, a in arrays.items():
        if a.shape == (D,):
            arrays[name] = np.ascontiguousarray(a.reshape(DC, P).transpose(1, 0))
    by_rows = lambda a: np.ascontiguousarray(a.reshape(DC, P, -1).transpose(1, 0, 2))
    for name in ("L0_cond_W1", "L0_cond_W2", "L0_attn_Wo"):
        arrays[name] = by_rows(arrays[name].T)
    arrays["condT"] = by_rows(arrays["cond_1024"].T)
    arrays["xT"] = np.ascontiguousarray(arrays["x"].transpose(0, 2, 1).reshape(S, DC, P, T).transpose(0, 2, 1, 3))
    proj = arrays["L0_ffn_proj_weight"].reshape(D, NKV, JQ // 2, 2, HD)
    arrays["L0_ffn_proj_weight"] = np.ascontiguousarray(proj.transpose(3, 1, 4, 2, 0).reshape(P, DC, D))
    qkv = arrays["L0_ffn_qkv_weight"].reshape(NKV, JQ + 2, HD, DC, P)
    arrays["L0_ffn_qkv_weight"] = np.ascontiguousarray(qkv.transpose(4, 3, 1, 0, 2).reshape(P, DC, QKV))
    for name in ("L0_ffn_moe_w1", "L0_ffn_moe_w2"):
        arrays[name] = np.concatenate([arrays[name], arrays[name][:1]])
    b2 = arrays["L0_cond2_b2"].reshape(2, DC, P, RANK)
    arrays["L0_cond2_b2"] = np.ascontiguousarray(b2.transpose(2, 0, 1, 3))
    arrays["cst"], arrays["tok"] = table, tok
    dram = {name: nc.dram_tensor(f"in_{name}", a.shape, mybir.dt.from_np(a.dtype), kind="ExternalInput").ap()
            for name, a in arrays.items()}
    dram["out"] = nc.dram_tensor("out_rows", (T, S, D), F32, kind="ExternalOutput").ap()
    program(nc, dram)
    arrays = {f"in_{name}": a for name, a in arrays.items()}
    r = run_bass_kernel_spmd(nc, [arrays], core_ids=[0])
    return np.ascontiguousarray(r.results[0]["out_rows"].transpose(1, 0, 2))
```

```python
from contextlib import ExitStack

import numpy as np
import concourse.bass as bass
from concourse import mybir

F32 = mybir.dt.float32
F32R = mybir.dt.float32r
BF16 = mybir.dt.bfloat16
I32 = mybir.dt.int32
ALU = mybir.AluOpType
ACT = mybir.ActivationFunctionType
AX = mybir.AxisListType

P = 128
S, T, D = 32, 256, 256
DC = D // P
TC = T // P
RANK = 8
NH, NKV, HD = 16, 4, 16
JQ = NH // NKV
QKV = NKV * (JQ + 2) * HD
E, K, F = 8, 2, 512
FC = F // P
N = S * T
CAP = -(-N * K * 5 // (E * 4))
U1 = 2
I1 = S // U1
TG = P // S
G = T // TG
U2 = 2
I2 = G // U2
DEPTH = 3
BT = 512
NB = CAP // BT
TB = BT // P
NX = 5
AHEAD = 2
W_AT = 3
ROW = D + 1 + E
LN_EPS = 1e-5
NEG = -1e30
NO_ROW = 1 << 20
RSQRT_MAGIC = float(0x5F3759DF)
NEWTON = 3
EMPTYING = 14

C_ID, C_TRI, C_ORDER, C_SAME, C_WITHIN = 0, P, 2 * P, 3 * P, 4 * P
C_CAUSAL = 5 * P
C_HEAD = C_CAUSAL + S
C_SEL = C_HEAD + NKV
C_TIE = C_SEL + P // RANK
C_BASE = C_TIE + E
C_RESET = C_BASE + E
C_N = C_RESET + E * G


def constants():
    p = np.arange(P)
    s, t = p % S, p // S
    c = np.zeros((P, C_N), np.float32)
    c[:, C_ID:C_ID + P] = np.eye(P)
    c[:, C_TRI:C_TRI + P] = np.where(p[None, :] > p[:, None], NEG, 0)
    c[:, C_ORDER:C_ORDER + P] = s[:, None] < s[None, :]
    c[:, C_SAME:C_SAME + P] = s[:, None] == s[None, :]
    c[:, C_WITHIN:C_WITHIN + P] = (s[:, None] == s[None, :]) & (t[:, None] < t[None, :])
    c[:, C_CAUSAL:C_CAUSAL + S] = np.where(np.arange(S)[None, :] > s[:, None], NEG, 0)
    c[:, C_HEAD:C_HEAD + NKV] = (p[:, None] % (NKV * HD)) // HD == np.arange(NKV)
    c[:, C_SEL:C_SEL + P // RANK] = p[:, None] // RANK == np.arange(P // RANK)
    c[:, C_TIE:C_TIE + E] = E - np.arange(E)
    c[:, C_BASE:C_BASE + E] = np.arange(E) * CAP
    c[:, C_RESET:C_RESET + E * G] = np.tile(np.arange(G) > 0, E)
    tok = (p[:, None] + np.arange(G)[None, :] * P).astype(np.int32)
    return c, tok


class Chain:

    def __init__(self, eng, sem, base=0):
        self.eng, self.sem, self.base, self.n = eng, sem, base, 0

    def step(self, ins):
        ins.then_inc(self.sem, 1)
        self.n += 1

    def wait(self):
        self.eng.wait_ge(self.sem, self.base + self.n)

    def link(self, ins):
        self.step(ins)
        self.wait()


def inverse_root_steps(nc, chain, var, tmp, seed):
    v, a, y0, y1 = (tmp[:, k] for k in range(4))
    chain.wait()
    chain.step(nc.vector.tensor_scalar(v, var, LN_EPS, None, ALU.add))
    yield
    chain.wait()
    chain.step(nc.vector.tensor_single_scalar(seed, v.bitcast(I32), 1, ALU.logical_shift_right))
    yield
    chain.wait()
    chain.step(nc.vector.tensor_scalar(y1.bitcast(I32), seed, -1.0, RSQRT_MAGIC, ALU.mult, ALU.add))
    yield
    old, new = y1, y0
    for _ in range(NEWTON):
        chain.wait()
        chain.step(nc.vector.tensor_tensor(a, old, old, ALU.mult))
        yield
        chain.wait()
        chain.step(nc.vector.scalar_tensor_tensor(a, a, -0.5, v, ALU.mult, ALU.mult))
        yield
        chain.wait()
        chain.step(nc.vector.scalar_tensor_tensor(new, a, 1.5, old, ALU.add, ALU.mult))
        yield
        old, new = new, old


def inverse_root(nc, chain, var, tmp, seed):
    for _ in inverse_root_steps(nc, chain, var, tmp, seed):
        pass
    chain.wait()
    return tmp[:, 3 - NEWTON % 2]


def after(eng, sem, j, u):
    if not (isinstance(j, int) and j < 0):
        eng.wait_ge(sem, j * 2 + (u + 1))


def three(nc, out, a, b, at_a, at_b, first, last):
    (ah, al), (bh, bl) = a, b
    nc.tensor.matmul(out, at_a(ah), at_b(bh), start=first, stop=False, skip_group_check=True)
    nc.tensor.matmul(out, at_a(ah), at_b(bl), start=False, stop=False, skip_group_check=True)
    return nc.tensor.matmul(out, at_a(al), at_b(bh), start=False, stop=last, skip_group_check=True)


def turn(nc, pr, out, src):
    return nc.tensor.transpose(out.bitcast(F32R), src.bitcast(F32R), pr.identr[:])


class Program:

    def __init__(self, nc, ctx, dram):
        self.nc, self.ctx, self.d = nc, ctx, dram
        sb = lambda name, shape, dt=F32: ctx.enter_context(nc.sbuf_tensor(name, shape, dt))
        self.cst = sb("cst", [P, C_N])
        self.ident = self.cst[:, C_ID:C_ID + P]
        self.identb = sb("identb", [P, P], BF16)
        self.identr = sb("identr", [P, P], F32R)
        self.trib = sb("trib", [P, P], BF16)
        self.causalb = sb("causalb", [P, TG, NKV, S], BF16)
        self.gate = sb("gate", [P, DC, S])
        parts = lambda name, shape: tuple(sb(f"{name}_{part}", shape, F32R) for part in ("high", "low"))
        self.Wa = parts("Wa", [P, DC, D])
        self.Wc = parts("Wc", [P, DC, D])
        self.base = parts("base", [P, DC, D])
        self.xa = parts("xa", [P, DC, 2, P])
        self.xb = parts("xb", [P, 2, D])
        self.wqkv = parts("wqkv", [P, DC, QKV])
        self.wproj = sb("wproj", [P, DC, D])
        self.wroute = sb("wroute", [P, DC, E])
        self.ln1 = sb("ln1", [P, 2, DC])
        self.ln2 = sb("ln2", [P, 2, DC])
        self.tok = sb("tok", [P, G], I32)
        self.empty = sb("empty", [P, ROW])
        self.sem = lambda name: ctx.enter_context(nc.semaphore(name))
        self.passed = self.sem("passed")
        self.emptied = self.sem("emptied")
        self.x12 = nc.dram_tensor("x12_rows", (T, S, 2, D), F32, kind="Internal").ap()
        self.slots = nc.dram_tensor("slot_rows", (E * CAP + AHEAD * BT, ROW), F32, kind="Internal").ap()


def setup(pr):
    nc, d = pr.nc, pr.d
    with ExitStack() as ctx:
        sb = lambda name, shape, dt=F32: ctx.enter_context(nc.sbuf_tensor(name, shape, dt))
        sem = pr.sem
        ps = [ctx.enter_context(nc.psum_tensor(f"setup_ps{k}", [P, 512], F32)) for k in range(8)]
        cond = sb("cond", [S, D])
        condn = sb("condn", [S, D])
        w = {k: sb(f"s_{k}", [P, DC, D]) for k in ("Wq", "Wk", "Wv", "w1")}
        W1T, W2T, WoT = (sb(n, [P, DC, D]) for n in ("W1T", "W2T", "WoT"))
        w2 = sb("w2", [P, DC, 2 * D * RANK])
        vec = {k: sb(f"s_{k}", [P, DC]) for k in ("b1", "b2", "c2b1", "lng", "lnb")}
        b2c = sb("b2c", [P, 2, DC, RANK])
        condT, aeT, z, ez, hs, h2 = (sb(n, [P, DC, S]) for n in ("condT", "aeT", "z", "ez", "hs", "h2"))
        Wa, Wc, base = (sb(n, [P, DC, D]) for n in ("Wa", "Wc", "base"))
        xa, xbT, xb = sb("xa", [P, DC, 2, P]), sb("xbT", [P, DC, 2, P]), sb("xb", [P, 2, D])
        wqkv = sb("wqkv", [P, DC, QKV])
        stats = sb("stats", [S, 6])
        mv = sb("mv", [S, 2])
        tmp = sb("tmp", [S, 4, 1])
        seed = sb("seed", [S, 1], I32)
        dve = sem("setup_dve")
        events = {}

        def event(name):
            if name not in events:
                events[name] = sem(f"done_{name}")
            return events[name]

        chunked = lambda a: a.rearrange("(c p) n -> p c n", p=P)
        block = ctx.enter_context(nc.Block())

        half = D * RANK
        loads = {
            "cond": [(cond[:], d["cond_1024"]), (pr.cst[:], d["cst"]), (condT[:], d["condT"]),
                     (W1T[:], d["L0_cond_W1"]), (W2T[:], d["L0_cond_W2"]), (w["w1"][:], chunked(d["L0_cond2_w1"])),
                     (vec["b1"][:], d["L0_cond_b1"]), (vec["b2"][:], d["L0_cond_b2"]),
                     (vec["c2b1"][:], d["L0_cond2_b1"]), (vec["lng"][:], d["L0_cond2_ln_g"]),
                     (vec["lnb"][:], d["L0_cond2_ln_b"]), (b2c[:], d["L0_cond2_b2"])],
            "left": [(w2[:, :, 0:half], chunked(d["L0_cond2_w2"])[:, :, 0:half])],
            "right": [(w2[:, :, half:], chunked(d["L0_cond2_w2"])[:, :, half:])],
            "attn": [(w["Wq"][:], chunked(d["L0_attn_Wq"])), (w["Wk"][:], chunked(d["L0_attn_Wk"])),
                     (w["Wv"][:], chunked(d["L0_attn_Wv"])), (WoT[:], d["L0_attn_Wo"])],
            "rest": [(wqkv[:], d["L0_ffn_qkv_weight"]), (base[:], chunked(d["L0_cond2_base_layer"])),
                     (pr.ln1[:, 0, :], d["L0_ffn_ln1_weight"]), (pr.ln1[:, 1, :], d["L0_ffn_ln1_bias"]),
                     (pr.ln2[:, 0, :], d["L0_ffn_ln2_weight"]), (pr.ln2[:, 1, :], d["L0_ffn_ln2_bias"]),
                     (pr.wproj[:], d["L0_ffn_proj_weight"]),
                     (pr.wroute[:], chunked(d["L0_ffn_router_weight"])), (pr.tok[:], d["tok"])],
        }
        loaded = {name: sem(f"loaded_{name}") for name in loads}

        def wait_loads(eng, name):
            eng.wait_ge(loaded[name], 16 * len(loads[name]))

        @block.sync
        def _(sp):
            for name, pairs in loads.items():
                for dst, src in pairs:
                    sp.dma_start(dst, src).then_inc(loaded[name], 16)
            for name in loads:
                wait_loads(sp, name)

        @block.vector
        def _(dve_eng):
            ch = Chain(dve_eng, dve)
            v = nc.vector
            ch.link(v.memset(pr.empty[:], 0.0))
            ch.step(v.memset(pr.empty[:, D:D + 1].bitcast(I32), NO_ROW))
            wait_loads(dve_eng, "cond")
            ch.step(v.tensor_copy(pr.identb[:], pr.ident))
            ch.step(v.tensor_copy(pr.identr[:], pr.ident))
            ch.step(v.tensor_copy(pr.trib[:], pr.cst[:, C_TRI:C_TRI + P]))
            ch.step(v.tensor_copy(pr.causalb[:].rearrange("p t g s -> p (t g) s"),
                                  pr.cst[:, None, C_CAUSAL:C_CAUSAL + S].broadcast_to([P, TG * NKV, S])))
            ch.link(v.bn_stats(stats[:], cond[:]))
            ch.link(v.bn_aggr(mv[:], stats[:]))
            rstd = inverse_root(nc, ch, mv[:, 1:2], tmp, seed[:])
            v.tensor_scalar(condn[:], cond[:], mv[:, 0:1], rstd, ALU.subtract, ALU.mult).then_inc(event("condn"), 1)
            dve_eng.wait_ge(event("ps_condnT"), 1)
            for c in range(DC):
                ins = (v.tensor_scalar(aeT[:, c, :], ps[1][:, c * S:(c + 1) * S], vec["lng"][:, c:c + 1],
                                        vec["lnb"][:, c:c + 1], ALU.mult, ALU.add))
            ins.then_inc(event("aeT"), 1)
            dve_eng.wait_ge(event("ps_h"), 1)
            for c in range(DC):
                ins = (v.tensor_scalar(z[:, c, :], ps[4][:, c * S:(c + 1) * S], vec["b1"][:, c:c + 1],
                                        None, ALU.add))
            ins.then_inc(event("z1"), 1)
            dve_eng.wait_ge(event("exp1"), 1)
            ch.link(v.tensor_scalar(ez[:], ez[:], 1.0, None, ALU.add))
            ch.link(v.reciprocal(ez[:], ez[:]))
            v.tensor_tensor(hs[:], z[:], ez[:], ALU.mult).then_inc(event("hs"), 1)
            dve_eng.wait_ge(event("ps_gate"), 1)
            for c in range(DC):
                ins = (v.tensor_scalar(z[:, c, :], ps[5][:, c * S:(c + 1) * S], vec["b2"][:, c:c + 1],
                                        None, ALU.add))
            ins.then_inc(event("z2"), 1)
            dve_eng.wait_ge(event("exp2"), 1)
            ch.link(v.tensor_scalar(ez[:], ez[:], 1.0, None, ALU.add))
            ch.link(v.reciprocal(ez[:], ez[:]))
            ch.step(v.tensor_scalar(pr.gate[:], ez[:], 1.0, None, ALU.add))
            for a, dst in ((0, xa), (1, xbT)):
                dve_eng.wait_ge(event(f"ps_x{a}"), 1)
                for c in range(DC):
                    src = ps[a][:, c * RANK * S:(c + 1) * RANK * S].rearrange("p (r b) -> p b r", r=RANK)
                    ins = (v.tensor_tensor(
                        dst[:, c].rearrange("p h n -> p (h n)").rearrange("p (b r) -> p b r", r=RANK),
                        src, b2c[:, a, c, :].unsqueeze(1).broadcast_to([P, S, RANK]), ALU.add))
            ins.then_inc(event("xbT"), 1)
            dve_eng.wait_ge(event("ps_Wa"), 1)
            ch.step(v.tensor_scalar(Wa[:].rearrange("p c n -> p (c n)"), ps[2][:], D ** -0.5, None, ALU.mult))
            dve_eng.wait_ge(event("ps_Wc"), 1)
            ch.step(v.tensor_copy(Wc[:].rearrange("p c n -> p (c n)"), ps[3][:]))
            wait_loads(dve_eng, "rest")
            ch.step(v.tensor_scalar(wqkv[:, :, 0:D], wqkv[:, :, 0:D], HD ** -0.5, None, ALU.mult))
            dve_eng.wait_ge(event("ps_xb"), 1)
            ch.link(v.tensor_copy(xb[:].rearrange("p h n -> p (h n)"), ps[7][:]))
            split = ((Wa, pr.Wa), (Wc, pr.Wc), (base, pr.base), (xa, pr.xa), (xb, pr.xb), (wqkv, pr.wqkv))
            for full, (high, low) in split:
                ch.step(v.tensor_copy(high[:], full[:]))
            ch.wait()
            for full, (high, low) in split:
                ch.step(v.tensor_tensor(low[:], full[:], high[:].bitcast(F32), ALU.subtract))
            ch.wait()

        @block.tensor
        def _(pe):
            t = nc.tensor
            wait_loads(pe, "cond")
            pe.wait_ge(event("condn"), 1)
            for c in range(DC):
                ins = t.transpose(ps[1][:, c * S:(c + 1) * S], condn[:, c * P:(c + 1) * P], pr.ident[0:S, 0:S])
            ins.then_inc(event("ps_condnT"), 1)

            def product(name, out, lhs, rhs, after=None):
                if after:
                    pe.wait_ge(event(after), 1)
                width = rhs.shape[2]
                for mc in range(DC):
                    for kc in range(DC):
                        ins = t.matmul(out[:, mc * width:(mc + 1) * width], lhs[:, kc, mc * P:(mc + 1) * P],
                                       rhs[:, kc, :], start=(kc == 0), stop=(kc == DC - 1))
                ins.then_inc(event(f"ps_{name}"), 1)

            product("h", ps[4], W1T, condT)
            product("h2", ps[6], w["w1"], aeT, after="aeT")
            product("gate", ps[5], W2T, hs, after="hs")
            pe.wait_ge(event("gelu"), 1)
            for a in range(2):
                wait_loads(pe, ("left", "right")[a])
                for c in range(DC):
                    for r in range(RANK):
                        at = (c * RANK + r) * S
                        for ic in range(DC):
                            cols = w2[:, ic, a * D * RANK:(a + 1) * D * RANK].rearrange("p (k r) -> p r k", r=RANK)
                            ins = t.matmul(ps[a][:, at:at + S], cols[:, r, c * P:(c + 1) * P], h2[:, ic, :],
                                           start=(ic == 0), stop=(ic == DC - 1))
                ins.then_inc(event(f"ps_x{a}"), 1)
            wait_loads(pe, "attn")
            product("Wa", ps[2], w["Wq"], w["Wk"])
            product("Wc", ps[3], w["Wv"], WoT)
            pe.wait_ge(event("xbT"), 1)
            for h in range(2):
                for c in range(DC):
                    ins = t.transpose(ps[7][:, h * D + c * P:h * D + (c + 1) * P], xbT[:, c, h, :], pr.ident)
            ins.then_inc(event("ps_xb"), 1)

        @block.scalar
        def _(act):
            act.wait_ge(event("z1"), 1)
            nc.scalar.activation(ez[:], z[:], ACT.Exp, scale=-1.0).then_inc(event("exp1"), 1)
            act.wait_ge(event("z2"), 1)
            nc.scalar.activation(ez[:], z[:], ACT.Exp, scale=-1.0).then_inc(event("exp2"), 1)
            act.wait_ge(event("ps_h2"), 1)
            for c in range(DC):
                ins = nc.scalar.activation(h2[:, c, :], ps[6][:, c * S:(c + 1) * S], ACT.Gelu,
                                           bias=vec["c2b1"][:, c:c + 1])
            ins.then_inc(event("gelu"), 1)


def sequences(pr):
    nc, d = pr.nc, pr.d
    with ExitStack() as ctx:
        sb = lambda name, shape, dt=F32: ctx.enter_context(nc.sbuf_tensor(name, shape, dt))
        sem = pr.sem
        sems = lambda name: [sem(f"{name}{u}") for u in range(U1)]
        places = range(U1)
        bank = lambda name: [ctx.enter_context(nc.psum_tensor(f"{name}{u}", [P, 512], F32)) for u in places]
        pa, pb, pc, pd = (bank(n) for n in ("pa", "pb", "pc", "pd"))
        bufs = lambda name, shape: [sb(f"{name}{u}", shape) for u in places]
        x = bufs("x", [P, TC, D])
        xT = [bufs(f"xT{par}_", [P, DC, T]) for par in range(2)]
        parts = lambda name, shape: [tuple(sb(f"{name}{u}_{part}", shape, F32R) for part in ("high", "low"))
                                     for u in places]
        uT = parts("uT", [P, DC, T])
        qT = parts("qT", [P, DC, T])
        pz = bufs("pz", [P, T + P])
        pT = bufs("pT", [P, T + P])
        x1T = bufs("x1T", [P, DC, T])
        x1p = parts("x1p", [P, DC, T])
        lr = parts("lr", [P, T])
        x12 = bufs("x12_", [P, TC, 2, D])
        nrm = bufs("nrm1_", [P, TC, D])
        nT = parts("nT1_", [P, DC, T])
        nmax, den, rden = (sb(n, [P, U1, TC]) for n in ("nmax", "den", "rden"))
        col = [sb(f"col{par}", [P, U1, DC + 1]) for par in range(2)]
        stats = sb("stats1", [P, U1, TC, 6])
        mv = sb("mv1", [P, U1, TC, 2])
        tmp = sb("tmp1", [P, 4, U1 * TC])
        seed = sb("seed1", [P, U1 * TC], I32)
        flat = lambda a: a[:].rearrange("p c n -> p (c n)")

        x_in, xT_in = sems("x_in"), sems("xT_in")
        pe_did = {n: sem(f"pe_{n}_") for n in "qT score pT z y low out x1 nT kv q".split()}
        dve_did = {n: sem(f"dve_{n}_") for n in "col uh u qT max rden soft pT x1T x1p lr x12 z nrm kv".split()}
        act_did = {n: sem(f"act_{n}_") for n in "qT exp z lr x1 x1p nT q".split()}
        pool_did = {n: sem(f"pool_{n}_") for n in ["nT"]}
        stored = sems("stored")
        links = sem("links1")
        LINKS = U1 * 2 * TC + 3 + 3 * NEWTON

        def pipeline(eng, step):
            has = lambda j: 0 <= j < I1
            first, last = 2, I1 - 3
            for k in range(-2, first):
                step(k, k % 2, has)
            with eng.Fori(0, (last + 1 - first) // 2) as i:
                for par in range(2):
                    step(i * 2 + (first + par), par, lambda j: True)
            for k in range(last + 1, I1 + 2):
                step(k, k % 2, has)

        block = ctx.enter_context(nc.Block())

        @block.sync
        def _(sp):
            src = d["x"].rearrange("s (c p) n -> s p c n", p=P)
            dst = pr.x12.rearrange("(c p) s k n -> s p c (k n)", p=P)

            rows = pr.slots.rearrange("(k p a) c -> k p a c", k=EMPTYING, p=P)

            def step(k, par, has):
                if not isinstance(k, int) or 0 <= k < EMPTYING:
                    sp.dma_start(rows[bass.ds(k, 1)].rearrange("a p n c -> (a p) n c"),
                                 pr.empty[:, None, :].broadcast_to([P, rows.shape[2], ROW])).then_inc(pr.emptied, 16)
                if has(k - 1):
                    for u in places:
                        after(sp, dve_did["x12"], k - 1, u)
                        sp.sem_inc(pr.passed, 1)
                        sp.dma_start(dst[bass.ds(k - 1 + I1 * u, 1)].rearrange("a p c n -> p (a c) n"),
                                     x12[u][:].rearrange("p c k n -> p c (k n)")).then_inc(stored[u], 16)
                if has(k + 1):
                    for u in places:
                        after(sp, pe_did["z"], k, u)
                        sp.sem_inc(pr.passed, 1)
                        sp.dma_start(x[u][:], src[bass.ds(k + 1 + I1 * u, 1)].rearrange("a p c n -> p (a c) n")
                                     ).then_inc(x_in[u], 16)
                if has(k + 2):
                    for u in places:
                        after(sp, dve_did["x1T"], k, u)
                        if not isinstance(k, int) or k > -2:
                            sp.wait_ge(xT_in[u], 16 * (k + 2))
                        sp.sem_inc(pr.passed, 1)
                        sp.dma_start(xT[par][u][:], d["xT"][bass.ds(k + 2 + I1 * u, 1)]
                                     .rearrange("a p c n -> p (a c) n")).then_inc(xT_in[u], 16)

            pipeline(sp, step)
            for u in places:
                sp.wait_ge(stored[u], 16 * I1)

        @block.tensor
        def _(pe):
            t = nc.tensor

            def product(out, lhs, rhs):
                for mc in range(DC):
                    for kc in range(DC):
                        ins = three(nc, out[:, mc * T:(mc + 1) * T], lhs, rhs,
                                    lambda a: a[:, kc, mc * P:(mc + 1) * P], lambda b: b[:, kc, :],
                                    mc == 0 and kc == 0, kc == DC - 1)
                return ins

            def transposes(out, src):
                for c in range(DC):
                    for r in range(TC):
                        ins = t.transpose(out[:, c * 256 + r * P:c * 256 + (r + 1) * P],
                                          src[:, r, c * P:(c + 1) * P], pr.ident)
                return ins

            def step(k, par, has):
                if has(k):
                    for u in places:
                        after(pe, dve_did["x1T"], k - 1, u)
                        after(pe, dve_did["u"], k, u)
                        product(pb[u], pr.Wa, uT[u]).then_inc(pe_did["qT"], 1)
                if has(k - 2):
                    for u in places:
                        after(pe, pool_did["nT"], k - 2, u)
                        for name, dst, c0, n in (("kv", pd, 2 * P, 1), ("q", pc, 0, 2)):
                            for m in range(n):
                                for c in range(DC):
                                    ins = three(nc, dst[u][:, m * T:(m + 1) * T], pr.wqkv, nT[u],
                                                lambda a: a[:, c, c0 + m * P:c0 + (m + 1) * P],
                                                lambda b: b[:, c, :], m == 0 and c == 0, c == DC - 1)
                            ins.then_inc(pe_did[name], 1)
                if has(k - 1):
                    for u in places:
                        after(pe, dve_did["kv"], k - 2, u)
                        after(pe, dve_did["x1p"], k - 1, u)
                        for c in range(DC):
                            ins = three(nc, pd[u][:, 0:T], pr.xa, x1p[u], lambda a: a[:, c, u, :],
                                        lambda b: b[:, c, :], c == 0, c == DC - 1)
                        ins.then_inc(pe_did["low"], 1)
                if has(k):
                    for u in places:
                        after(pe, dve_did["qT"], k, u)
                        for r in range(TC):
                            out = pa[u][:, r * P:r * P + (r + 1) * P]
                            for c in range(DC):
                                three(nc, out, qT[u], uT[u], lambda a: a[:, c, r * P:(r + 1) * P],
                                      lambda b: b[:, c, 0:(r + 1) * P], c == 0, False)
                            ins = t.matmul(out[:, r * P:(r + 1) * P], pr.identb[:], pr.trib[:],
                                           start=False, stop=True, skip_group_check=True)
                        ins.then_inc(pe_did["score"], 1)
                if has(k - 1):
                    for u in places:
                        after(pe, dve_did["lr"], k - 1, u)
                        for r in range(TC):
                            for c in range(DC):
                                for part in x1p[u]:
                                    ins = t.matmul(pd[u][:, r * D + c * P:r * D + (c + 1) * P],
                                                   part[:, c, r * P:(r + 1) * P], pr.identr[:],
                                                   start=part is x1p[u][0], stop=part is x1p[u][1],
                                                   skip_group_check=True)
                        ins.then_inc(pe_did["x1"], 1)
                        after(pe, act_did["q"], k - 2, u)
                        for r in range(TC):
                            rows, cols = slice(r * P, (r + 1) * P), slice(r * D, (r + 1) * D)
                            for c in range(DC):
                                three(nc, pc[u][:, cols], x1p[u], pr.base, lambda a: a[:, c, rows],
                                      lambda b: b[:, c, :], r == 0 and c == 0, False)
                            ins = three(nc, pc[u][:, cols], lr[u], pr.xb, lambda a: a[:, rows],
                                        lambda b: b[:, u, :], False, True)
                        ins.then_inc(pe_did["out"], 1)
                if has(k):
                    for u in places:
                        after(pe, dve_did["soft"], k, u)
                        for b in range(3):
                            ins = t.transpose(pb[u][:, b * P:(b + 1) * P], pz[u][:, b * P:(b + 1) * P], pr.ident)
                        ins.then_inc(pe_did["pT"], 1)
                if has(k):
                    for u in places:
                        after(pe, dve_did["pT"], k, u)
                        pe.wait_ge(x_in[u], 16 * (k + 1))
                        for c in range(DC):
                            t.matmul(pa[u][:, c * T:(c + 1) * T], x[u][:, 0, c * P:(c + 1) * P], pT[u][:, 0:T],
                                     start=(c == 0), stop=False, skip_group_check=True)
                            ins = t.matmul(pa[u][:, c * T + P:(c + 1) * T], x[u][:, 1, c * P:(c + 1) * P],
                                           pT[u][:, T:T + P], start=False, stop=True, skip_group_check=True)
                        ins.then_inc(pe_did["z"], 1)
                    for u in places:
                        after(pe, dve_did["z"], k, u)
                        product(pb[u], pr.Wc, qT[u]).then_inc(pe_did["y"], 1)
                if has(k - 1):
                    for u in places:
                        after(pe, dve_did["nrm"], k - 1, u)
                        transposes(pd[u], nrm[u]).then_inc(pe_did["nT"], 1)

            pipeline(pe, step)

        @block.scalar
        def _(act):
            a = nc.scalar

            def step(k, par, has):
                if has(k):
                    for u in places:
                        after(act, pe_did["qT"], k, u)
                        a.copy(flat(qT[u][0]), pb[u][:]).then_inc(act_did["qT"], 1)
                if has(k - 2):
                    for u in places:
                        after(act, pe_did["q"], k - 2, u)
                        act.sem_inc(pr.passed, 1)
                        a.copy(pr.q[:, :, :, :, bass.ds(k - 2 + I1 * u, 1)].rearrange("p c g t a -> p c g (t a)"),
                               pc[u][:].rearrange("p (c g t) -> p c g t", c=DC, g=G)).then_inc(act_did["q"], 1)
                if has(k - 1):
                    for u in places:
                        after(act, pe_did["low"], k - 1, u)
                        a.activation(lr[u][0][:], pd[u][:, 0:T], ACT.Copy, scale=col[1 - par][:, u, DC:DC + 1]
                                     ).then_inc(act_did["lr"], 1)
                if has(k):
                    for u in places:
                        after(act, dve_did["max"], k, u)
                        for r in range(TC):
                            cols = slice(r * P, r * P + (r + 1) * P)
                            ins = a.activation(pz[u][:, cols], pa[u][:, cols], ACT.Exp, bias=nmax[:, u, r:r + 1],
                                               accum_out=den[:, u, r:r + 1])
                        ins.then_inc(act_did["exp"], 1)
                if has(k - 1):
                    for u in places:
                        after(act, pe_did["x1"], k - 1, u)
                        if not isinstance(k, int) or k > 1:
                            act.wait_ge(stored[u], 16 * (k - 1))
                        a.copy(x12[u][:, :, 0, :], pd[u][:].rearrange("p (c n) -> p c n", c=TC)
                               ).then_inc(act_did["x1"], 1)
                if has(k):
                    for u in places:
                        after(act, pe_did["z"], k, u)
                        for c in range(DC):
                            ins = a.activation(qT[u][0][:, c, :], pa[u][:, c * T:(c + 1) * T], ACT.Copy,
                                               scale=col[par][:, u, c:c + 1])
                        ins.then_inc(act_did["z"], 1)
                if has(k - 1):
                    for u in places:
                        after(act, pe_did["nT"], k - 1, u)
                        for out in (nT[u][0], nrm[u]):
                            for c in range(DC):
                                ins = a.activation(out[:, c, :], pd[u][:, c * T:(c + 1) * T], ACT.Identity,
                                                   scale=pr.ln1[:, 0, c:c + 1], bias=pr.ln1[:, 1, c:c + 1])
                        ins.then_inc(act_did["nT"], 1)
                if has(k):
                    for u in places:
                        after(act, dve_did["x1T"], k, u)
                        a.copy(flat(x1p[u][0]), flat(x1T[u])).then_inc(act_did["x1p"], 1)

            pipeline(act, step)

        @block.gpsimd
        def _(pool):
            def step(k, par, has):
                if has(k - 1):
                    for u in places:
                        after(pool, act_did["nT"], k - 1, u)
                        nc.gpsimd.tensor_tensor(flat(nT[u][1]), flat(nrm[u]), flat(nT[u][0]).bitcast(F32),
                                                ALU.subtract).then_inc(pool_did["nT"], 1)

            pipeline(pool, step)

        @block.vector
        def _(dve):
            v = nc.vector

            def rest(out, full, high):
                return v.tensor_tensor(out, full, high.bitcast(F32), ALU.subtract)

            def step(k, par, has):
                if has(k):
                    for u in places:
                        after(dve, act_did["qT"], k, u)
                        rest(flat(qT[u][1]), pb[u][:], flat(qT[u][0])).then_inc(dve_did["qT"], 1)
                if has(k - 2):
                    for u in places:
                        after(dve, pe_did["kv"], k - 2, u)
                        dve.sem_inc(pr.passed, 1)
                        v.tensor_copy(pr.kv[:, :, :, bass.ds(k - 2 + I1 * u, 1)].rearrange("p g t a -> p g (t a)"),
                                      pd[u][:, 0:T].rearrange("p (g t) -> p g t", g=G)).then_inc(dve_did["kv"], 1)
                if has(k - 1):
                    for u in places:
                        after(dve, act_did["lr"], k - 1, u)
                        v.scalar_tensor_tensor(lr[u][1][:], pd[u][:, 0:T], col[1 - par][:, u, DC:DC + 1],
                                               lr[u][0][:].bitcast(F32), ALU.mult, ALU.subtract
                                               ).then_inc(dve_did["lr"], 1)
                if has(k):
                    for u in places:
                        after(dve, pe_did["score"], k, u)
                        for r in range(TC):
                            ins = v.tensor_reduce(nmax[:, u, r:r + 1], pa[u][:, r * P:r * P + (r + 1) * P],
                                                  AX.X, ALU.max, negate=True)
                        ins.then_inc(dve_did["max"], 1)
                    for u in places:
                        after(dve, act_did["exp"], k, u)
                        v.reciprocal(rden[:, u, :], den[:, u, :]).then_inc(dve_did["rden"], 1)
                        after(dve, dve_did["rden"], k, u)
                        for r in range(TC):
                            cols = slice(r * P, r * P + (r + 1) * P)
                            ins = v.tensor_scalar(pz[u][:, cols], pz[u][:, cols], rden[:, u, r:r + 1],
                                                  None, ALU.mult)
                        ins.then_inc(dve_did["soft"], 1)
                if has(k + 1):
                    for u in places:
                        v.tensor_scalar(col[1 - par][:, u, 0:DC], pr.gate[:, :, bass.ds(k + 1 + I1 * u, 1)]
                                        .rearrange("p c a -> p (c a)"), 1.0, None, ALU.mult)
                        v.tensor_scalar(col[1 - par][:, u, DC:DC + 1], pr.cst[:, bass.ds(C_SEL + 1 + k, 1)],
                                        1.0, None, ALU.mult).then_inc(dve_did["col"], 1)
                    for u in places:
                        after(dve, dve_did["col"], k + 1, u)
                        dve.wait_ge(xT_in[u], 16 * (k + 2))
                        for c in range(DC):
                            ins = v.tensor_scalar(uT[u][0][:, c, :], xT[1 - par][u][:, c, :],
                                                  col[1 - par][:, u, c:c + 1], None, ALU.mult)
                        ins.then_inc(dve_did["uh"], 1)
                    for u in places:
                        after(dve, dve_did["uh"], k + 1, u)
                        for c in range(DC):
                            ins = v.scalar_tensor_tensor(uT[u][1][:, c, :], xT[1 - par][u][:, c, :],
                                                         col[1 - par][:, u, c:c + 1],
                                                         uT[u][0][:, c, :].bitcast(F32), ALU.mult, ALU.subtract)
                        ins.then_inc(dve_did["u"], 1)
                if has(k - 1):
                    for u in places:
                        after(dve, pe_did["out"], k - 1, u)
                        after(dve, act_did["x1"], k - 1, u)
                        v.tensor_tensor(x12[u][:, :, 1, :], pc[u][:].rearrange("p (c n) -> p c n", c=TC),
                                        x12[u][:, :, 0, :], ALU.add).then_inc(dve_did["x12"], 1)
                if has(k):
                    for u in places:
                        after(dve, pe_did["pT"], k, u)
                        v.tensor_copy(pT[u][:], pb[u][:, 0:T + P]).then_inc(dve_did["pT"], 1)
                def z_rest(u):
                    if has(k):
                        after(dve, act_did["z"], k, u)
                        for c in range(DC):
                            ins = v.scalar_tensor_tensor(qT[u][1][:, c, :], pa[u][:, c * T:(c + 1) * T],
                                                         col[par][:, u, c:c + 1],
                                                         qT[u][0][:, c, :].bitcast(F32), ALU.mult, ALU.subtract)
                        ins.then_inc(dve_did["z"], 1)
                if has(k - 1):
                    ch = Chain(dve, links, (k - 1) * LINKS)
                    for u in places:
                        after(dve, dve_did["x12"], k - 1, u)
                        for c in range(TC):
                            ch.step(v.bn_stats(stats[:, u, c, :], x12[u][:, c, 1, :]))
                    ch.wait()
                    dve.sem_inc(pr.passed, 1)
                    for u in places:
                        for c in range(TC):
                            ch.step(v.bn_aggr(mv[:, u, c, :], stats[:, u, c, :]))
                    root = inverse_root_steps(nc, ch, mv[:].rearrange("p u c k -> p (u c) k")[:, :, 1],
                                              tmp, seed[:])
                    for _ in range(NEWTON):
                        next(root)
                z_rest(0)
                if has(k - 1):
                    for _ in range(NEWTON):
                        next(root)
                z_rest(1)
                if has(k - 1):
                    for _ in root:
                        pass
                    ch.wait()
                    assert ch.n == LINKS, ch.n
                    rstd = tmp[:, 3 - NEWTON % 2]
                    for u in places:
                        for c in range(TC):
                            r = u * TC + c
                            ins = v.tensor_scalar(nrm[u][:, c, :], x12[u][:, c, 1, :], mv[:, u, c, 0:1],
                                                  rstd[:, r:r + 1], ALU.subtract, ALU.mult)
                        ins.then_inc(dve_did["nrm"], 1)
                if has(k):
                    for u in places:
                        after(dve, pe_did["y"], k, u)
                        v.tensor_tensor(flat(x1T[u]), pb[u][:], flat(xT[par][u]), ALU.add
                                        ).then_inc(dve_did["x1T"], 1)
                    for u in places:
                        after(dve, act_did["x1p"], k, u)
                        rest(flat(x1p[u][1]), flat(x1T[u]), flat(x1p[u][0])).then_inc(dve_did["x1p"], 1)

            pipeline(dve, step)


def positions(pr):
    nc, d = pr.nc, pr.d
    with ExitStack() as ctx:
        sb = lambda name, shape, dt=F32: ctx.enter_context(nc.sbuf_tensor(name, shape, dt))
        sem = pr.sem
        sems = lambda name: [sem(f"{name}{u}") for u in range(U2)]
        bank = lambda name: [ctx.enter_context(nc.psum_tensor(f"{name}{u}", [P, 512], F32)) for u in range(U2)]
        ps_s, ps_w, ps_v, ps_h = (bank(n) for n in ("gs", "gw", "gv", "gh"))
        bufs = lambda name, shape: [sb(f"{name}{u}", shape) for u in range(U2)]
        KV1 = NKV * HD
        qg = bufs("qg", [KV1, TG, JQ, S])
        kvd = bufs("kvd", [P, TG, NKV, S])
        pw = bufs("pw", [P, TG * NKV, S])
        pwT = bufs("pwT", [P, TG, JQ, S])
        vb = bufs("vb", [P, TG, KV1])
        aoT = bufs("aoT", [P, 2, TG, S])
        x12 = bufs("xg", [P, 2, D])
        h1 = bufs("h1", [P, D])
        res = bufs("res", [P, D])
        nrm = bufs("nrm", [P, D])
        nT = bufs("nT", [P, DC, P])
        nmax, den = (sb(n, [P, U2, TG * NKV]) for n in ("gmax", "gden"))
        stats = sb("stats2", [P, U2, 6])
        mv = sb("mv2", [P, U2, 2])
        tmp = sb("tmp2", [P, 4, U2])
        seed = sb("seed2", [P, U2], I32)

        x_in, stored = sems("g_x_in"), sems("g_stored")
        pe_did = {n: sem(f"gpe_{n}_") for n in "score vT wT av h nT logit".split()}
        dve_did = {n: sem(f"gdve_{n}_") for n in "max sub sum rden h1 nrm".split()}
        act_did = {n: sem(f"gact_{n}_") for n in "q exp wT v ao nT logit rows".split()}
        pool_did = {n: sem(f"gpool_{n}_") for n in "kv soft res".split()}
        links = sem("links2")
        LINKS = U2 * 2 + 3 + 3 * NEWTON
        group = lambda j, u: j * U2 + u
        places = range(U2)

        def pipeline(eng, step):
            has = lambda j: 0 <= j < I2
            for k in range(-1, DEPTH + 1):
                step(k, has)
            with eng.Fori(0, I2 - 2 - DEPTH) as i:
                step(i + (DEPTH + 1), lambda j: True)
            for k in range(I2 - 1, I2 + DEPTH):
                step(k, has)

        block = ctx.enter_context(nc.Block())

        @block.sync
        def _(sp):
            src = pr.x12.rearrange("(g t) s k n -> g (t s) (k n)", t=TG)
            dst = pr.d["out"].rearrange("(g t) s n -> g (t s) n", t=TG)

            def load(j, u):
                sp.dma_start(x12[u][:].rearrange("p k n -> p (k n)"),
                             src[bass.ds(group(j, u), 1)].rearrange("a p n -> (a p) n")).then_inc(x_in[u], 16)

            def store(j, u):
                after(sp, pool_did["res"], j, u)
                sp.sem_inc(pr.passed, 1)
                sp.dma_start(dst[bass.ds(group(j, u), 1)].rearrange("a p n -> (a p) n"), res[u][:]
                             ).then_inc(stored[u], 16)

            for u in places:
                load(0, u)
            with sp.Fori(0, I2 - 1) as j:
                for u in places:
                    store(j, u)
                    load(j + 1, u)
            for u in places:
                store(I2 - 1, u)
            for u in places:
                sp.wait_ge(stored[u], 16 * I2)

        @block.gpsimd
        def _(pool):
            g = nc.gpsimd

            def step(k, has):
                if has(k - 2):
                    for u in places:
                        after(pool, dve_did["h1"], k - 2, u)
                        if not isinstance(k, int) or k > 2:
                            pool.wait_ge(stored[u], 16 * (k - 2))
                        g.tensor_tensor(res[u][:], x12[u][:, 0, :], h1[u][:], ALU.add
                                        ).then_inc(pool_did["res"], 1)
                if has(k):
                    for u in places:
                        after(pool, dve_did["rden"], k, u)
                        g.tensor_tensor(pw[u][:], pw[u][:], den[:, u, :].unsqueeze(2)
                                        .broadcast_to([P, TG * NKV, S]), ALU.mult).then_inc(pool_did["soft"], 1)
                if has(k + 1):
                    for u in places:
                        after(pool, pe_did["vT"], k, u)
                        g.tensor_tensor(kvd[u][:],
                                        pr.kv[:, bass.ds(group(k + 1, u), 1)].rearrange("p a t s -> p (a t) s")
                                        .unsqueeze(2).broadcast_to([P, TG, NKV, S]),
                                        pr.cst[:, C_HEAD:C_HEAD + NKV].unsqueeze(1).unsqueeze(3)
                                        .broadcast_to([P, TG, NKV, S]), ALU.mult).then_inc(pool_did["kv"], 1)

            pipeline(pool, step)

        @block.tensor
        def _(pe):
            t_ = nc.tensor

            def step(k, has):
                if has(k - 2):
                    for u in places:
                        after(pe, act_did["logit"], k - 4, u)
                        after(pe, act_did["ao"], k - 2, u)
                        for h in range(2):
                            ins = t_.matmul(ps_h[u][:, 0:D], aoT[u][:, h].rearrange("p t s -> p (t s)"),
                                            pr.wproj[:, h, :], start=(h == 0), stop=(h == 1))
                        ins.then_inc(pe_did["h"], 1)
                if has(k - 1):
                    for u in places:
                        after(pe, pool_did["soft"], k - 1, u)
                        for t in range(TG):
                            ins = t_.transpose(ps_w[u][:, t * P:(t + 1) * P],
                                       pw[u][:, t * NKV:(t + 1) * NKV, :].rearrange("p g s -> p (g s)"), pr.ident)
                        ins.then_inc(pe_did["wT"], 1)
                if has(k - 3):
                    for u in places:
                        if has(k - 2):
                            after(pe, dve_did["h1"], k - 2, u)
                        else:
                            after(pe, act_did["logit"], k - 4, u)
                        after(pe, dve_did["nrm"], k - 3, u)
                        for c in range(DC):
                            ins = t_.transpose(ps_h[u][:, 256 + c * P:256 + (c + 1) * P],
                                       nrm[u][:, c * P:(c + 1) * P], pr.ident)
                        ins.then_inc(pe_did["nT"], 1)
                if has(k):
                    for u in places:
                        t_.matmul(ps_s[u][:], pr.identb[:], pr.causalb[:].rearrange("p t g s -> p (t g s)"),
                                  start=True, stop=False, skip_group_check=True)
                        after(pe, act_did["q"], k, u)
                        after(pe, pool_did["kv"], k, u)
                        for t in range(TG):
                            ins = t_.matmul(ps_s[u][:, t * P:(t + 1) * P], qg[u][:, t].rearrange("p j s -> p (j s)"),
                                            kvd[u][0:KV1, t].rearrange("p g s -> p (g s)"),
                                            start=False, stop=True, skip_group_check=True)
                        ins.then_inc(pe_did["score"], 1)
                if has(k - 1):
                    for u in places:
                        after(pe, act_did["wT"], k - 1, u)
                        after(pe, act_did["v"], k - 1, u)
                        for jp in range(2):
                            for t in range(TG):
                                out = ps_v[u][jp * KV1:(jp + 1) * KV1, 256:512].rearrange(
                                    "p (h t s) -> p h t s", h=2, t=TG)
                                ins = t_.matmul(out[:, :, t, :], vb[u][:, t, :], pwT[u][:, t, jp::2, :],
                                                start=True, stop=True, skip_group_check=True)
                        ins.then_inc(pe_did["av"], 1)
                if has(k - 3):
                    for u in places:
                        after(pe, act_did["nT"], k - 3, u)
                        for c in range(DC):
                            ins = t_.matmul(ps_h[u][:, 256:256 + E], nT[u][:, c, :], pr.wroute[:, c, :],
                                            start=(c == 0), stop=(c == DC - 1))
                        ins.then_inc(pe_did["logit"], 1)
                if has(k):
                    for u in places:
                        after(pe, act_did["ao"], k - 1, u)
                        pe.sem_inc(pr.passed, 1)
                        for t in range(TG):
                            ins = t_.transpose(ps_v[u][:, t * KV1:(t + 1) * KV1],
                                       kvd[u][KV1:P, t].rearrange("p g s -> p (g s)"),
                                       pr.cst[KV1:P, C_ID + KV1:C_ID + P])
                        ins.then_inc(pe_did["vT"], 1)

            pipeline(pe, step)

        @block.scalar
        def _(act):
            a = nc.scalar
            a.activation(tmp[:, 0, 0:1], pr.cst[:, 0:1], ACT.Exp).then_inc(links, 1)

            def step(k, has):
                if has(k - 1):
                    for u in places:
                        after(act, pe_did["wT"], k - 1, u)
                        a.copy(pwT[u][:].rearrange("p t j s -> p (t j s)"), ps_w[u][:]
                               ).then_inc(act_did["wT"], 1)
                if has(k - 3):
                    for u in places:
                        after(act, pe_did["nT"], k - 3, u)
                        for c in range(DC):
                            ins = a.activation(nT[u][:, c, :], ps_h[u][:, 256 + c * P:256 + (c + 1) * P],
                                               ACT.Identity, scale=pr.ln2[:, 0, c:c + 1],
                                               bias=pr.ln2[:, 1, c:c + 1])
                        ins.then_inc(act_did["nT"], 1)
                def exponentials(u):
                    if has(k):
                        after(act, dve_did["sub"], k, u)
                        a.activation(pw[u][:], pw[u][:], ACT.Exp).then_inc(act_did["exp"], 1)

                exponentials(0)
                if has(k - 1):
                    for u in places:
                        after(act, pe_did["av"], k - 1, u)
                        a.copy(aoT[u][:].rearrange("p h t s -> p (h t s)"), ps_v[u][:, 256:512]
                               ).then_inc(act_did["ao"], 1)
                exponentials(1)
                if has(k - 3):
                    for u in places:
                        after(act, pe_did["logit"], k - 3, u)
                        act.sem_inc(pr.passed, 1)
                        a.copy(pr.logits[:, bass.ds(group(k - 3, u), 1), :].rearrange("p a n -> p (a n)"),
                               ps_h[u][:, 256:256 + E]).then_inc(act_did["logit"], 1)
                if has(k):
                    for u in places:
                        after(act, pe_did["vT"], k, u)
                        a.copy(vb[u][:].rearrange("p t n -> p (t n)"), ps_v[u][:, 0:TG * KV1]
                               ).then_inc(act_did["v"], 1)
                if has(k + 1):
                    for u in places:
                        after(act, pe_did["score"], k, u)
                        act.sem_inc(pr.passed, 1)
                        for jp in range(2):
                            ins = a.copy(
                                qg[u][:].rearrange("p t j s -> p j t s")[:, jp::2],
                                pr.q[jp * KV1:(jp + 1) * KV1, :, bass.ds(group(k + 1, u), 1)]
                                .rearrange("p c a t s -> p c (a t) s"))
                        ins.then_inc(act_did["q"], 1)
                if has(k - 2):
                    for u in places:
                        after(act, dve_did["nrm"], k - 2, u)
                        act.sem_inc(pr.passed, 1)
                        a.copy(pr.rows[:, bass.ds(group(k - 2, u), 1), 0:D].rearrange("p a n -> p (a n)"),
                               nrm[u][:]).then_inc(act_did["rows"], 1)

            pipeline(act, step)

        @block.vector
        def _(dve):
            v = nc.vector
            dve.wait_ge(links, 1)

            def step(k, has):
                norm, score = has(k - 2), has(k)
                root = iter(())
                if norm:
                    ch = Chain(dve, links, (k - 2) * LINKS + 1)
                    for u in places:
                        after(dve, pool_did["res"], k - 3, u)
                        after(dve, dve_did["nrm"], k - 3, u)
                        dve.wait_ge(x_in[u], 16 * (k - 1))
                        after(dve, pe_did["h"], k - 2, u)
                        v.tensor_tensor(h1[u][:], ps_h[u][:, 0:D], x12[u][:, 1, :], ALU.add
                                        ).then_inc(dve_did["h1"], 1)
                    for u in places:
                        after(dve, dve_did["h1"], k - 2, u)
                        ch.step(v.bn_stats(stats[:, u, :], h1[u][:]))
                if norm:
                    ch.wait()
                    dve.sem_inc(pr.passed, 1)
                    for u in places:
                        ch.step(v.bn_aggr(mv[:, u, :], stats[:, u, :]))
                    root = inverse_root_steps(nc, ch, mv[:, :, 1], tmp, seed[:])
                if score:
                    for u in places:
                        after(dve, pe_did["score"], k, u)
                        v.tensor_reduce(nmax[:, u, :], ps_s[u][:].rearrange("p (n s) -> p n s", s=S),
                                        AX.X, ALU.max).then_inc(dve_did["max"], 1)
                        next(root, None)
                        after(dve, dve_did["max"], k, u)
                        v.tensor_tensor(pw[u][:], ps_s[u][:].rearrange("p (n s) -> p n s", s=S),
                                        nmax[:, u, :].unsqueeze(2).broadcast_to([P, TG * NKV, S]),
                                        ALU.subtract).then_inc(dve_did["sub"], 1)
                        next(root, None)
                    next(root, None)
                    for u in places:
                        after(dve, act_did["exp"], k, u)
                        v.tensor_reduce(den[:, u, :], pw[u][:], AX.X, ALU.add).then_inc(dve_did["sum"], 1)
                        next(root, None)
                        after(dve, dve_did["sum"], k, u)
                        v.reciprocal(den[:, u, :], den[:, u, :]).then_inc(dve_did["rden"], 1)
                        next(root, None)
                if norm:
                    for _ in root:
                        pass
                    ch.wait()
                    rstd = tmp[:, 3 - NEWTON % 2]
                    for u in places:
                        after(dve, pe_did["nT"], k - 3, u)
                        after(dve, act_did["rows"], k - 3, u)
                        v.tensor_scalar(nrm[u][:], h1[u][:], mv[:, u, 0:1], rstd[:, u:u + 1],
                                        ALU.subtract, ALU.mult).then_inc(dve_did["nrm"], 1)
                    assert ch.n == LINKS, ch.n

            pipeline(dve, step)


def dispatch(pr):
    nc, d = pr.nc, pr.d
    with ExitStack() as ctx:
        sb = lambda name, shape, dt=F32: ctx.enter_context(nc.sbuf_tensor(name, shape, dt))
        sem = pr.sem
        ph = [ctx.enter_context(nc.psum_tensor(f"ph{f}", [P, G * E], F32)) for f in range(2)]
        L2, eq, S1, excl = (sb(n, [P, G, E]) for n in ("L2", "eq", "S1", "excl"))
        hot = sb("hot", [P, K, G, E])
        best, top = sb("best", [P, K, G]), sb("top", [P, G])
        ratio, prob = sb("ratio", [P, G]), sb("prob", [P, K, G])
        slotf, slot = sb("slotf", [P, K, G]), sb("slot", [P, K, G], I32)
        chosen = sb("chosen", [P, G, E], BF16)
        total, totalb = sb("total", [P, E]), sb("totalb", [P, E], BF16)
        order = sb("order", [P, 3, P], BF16)
        tiles = sb("tiles", [P, E, G])
        scan = sb("scan", [P, E, G])
        links, ratio_in, ratio_did, ranked = sem("links3"), sem("ratio_in"), sem("ratio_did"), sem("ranked")
        chosen_did, routed, dispatched = sem("chosen_did"), sem("routed"), sem("dispatched")
        grow = lambda a: a.unsqueeze(2).broadcast_to([P, G, E])
        row_e = lambda c0: pr.cst[:, c0:c0 + E].unsqueeze(1).broadcast_to([P, G, E])

        block = ctx.enter_context(nc.Block())

        @block.gpsimd
        def _(pool):
            g = nc.gpsimd
            pool.wait_ge(pr.emptied, 16 * EMPTYING)
            pool.wait_ge(routed, 1)
            for j in range(G):
                for k in range(K):
                    g.indirect_dma_start(
                        out=pr.slots, out_offset=bass.IndirectOffsetOnAxis(ap=slot[:, k, j:j + 1], axis=0),
                        in_=pr.rows[:, j, :], in_offset=None, bounds_check=E * CAP - 1, oob_is_err=False,
                    ).then_inc(dispatched, 16)
            pool.wait_ge(dispatched, 16 * K * G)

        @block.tensor
        def _(pe):
            t_ = nc.tensor
            flat = lambda a: a.rearrange("p g e -> p (g e)")
            pe.wait_ge(chosen_did, 1)
            t_.matmul(ph[0][:], order[:, 2, :], flat(chosen[:]), start=True, stop=False)
            t_.matmul(ph[0][:], order[:, 0, :], totalb[:].unsqueeze(1).broadcast_to([P, G, E]),
                      start=False, stop=True)
            t_.matmul(ph[1][:], order[:, 1, :], flat(chosen[:]), start=True, stop=True).then_inc(ranked, 1)

        @block.scalar
        def _(act):
            a = nc.scalar
            act.wait_ge(ratio_in, 1)
            a.activation(ratio[:], ratio[:], ACT.Exp).then_inc(ratio_did, 1)

        @block.vector
        def _(dve):
            v = nc.vector
            ch = Chain(dve, links)
            ch.step(v.tensor_copy(order[:].rearrange("p k n -> p (k n)"), pr.cst[:, C_ORDER:C_ORDER + 3 * P]))
            source = pr.logits
            for k in range(K):
                ch.link(v.tensor_reduce(best[:, k, :], source[:], AX.X, ALU.max))
                ch.link(v.tensor_tensor(eq[:], source[:], grow(best[:, k, :]), ALU.is_equal))
                ch.link(v.tensor_tensor(eq[:], eq[:], row_e(C_TIE), ALU.mult))
                ch.link(v.tensor_reduce(top[:], eq[:], AX.X, ALU.max))
                ch.link(v.tensor_tensor(hot[:, k], eq[:], grow(top[:]), ALU.is_equal))
                if k == 0:
                    ch.link(v.scalar_tensor_tensor(L2[:].rearrange("p g e -> p (g e)"),
                                                   hot[:, 0].rearrange("p g e -> p (g e)"), NEG,
                                                   pr.logits[:].rearrange("p g e -> p (g e)"),
                                                   ALU.mult, ALU.add))
                    source = L2
            v.tensor_tensor(ratio[:], best[:, 1, :], best[:, 0, :], ALU.subtract).then_inc(ratio_in, 1)
            ch.link(v.tensor_tensor(chosen[:], hot[:, 0], hot[:, 1], ALU.add))
            ch.link(v.tensor_reduce(total[:], chosen[:].rearrange("p g e -> p e g"), AX.X, ALU.add))
            v.tensor_copy(totalb[:], total[:]).then_inc(chosen_did, 1)
            dve.wait_ge(ratio_did, 1)
            ch.link(v.tensor_scalar(prob[:, 1, :], ratio[:], 1.0, None, ALU.add))
            ch.link(v.reciprocal(prob[:, 0, :], prob[:, 1, :]))
            ch.link(v.tensor_tensor(prob[:, 1, :], ratio[:], prob[:, 0, :], ALU.mult))
            for k, out in ((0, eq), (1, L2)):
                ch.link(v.tensor_tensor(out[:], hot[:, k], grow(prob[:, k, :]), ALU.mult))
            ch.step(v.tensor_tensor(pr.rows[:, :, D + 1:ROW], eq[:], L2[:], ALU.add))
            ch.step(v.tensor_copy(pr.rows[:, :, D:D + 1].bitcast(I32), pr.tok[:].unsqueeze(2)))
            dve.wait_ge(ranked, 1)
            ch.link(v.tensor_copy(tiles[:], ph[1][:].rearrange("p (g e) -> p e g", e=E)))
            ch.link(v.tensor_tensor_scan(scan[:].rearrange("p e g -> p (e g)"),
                                         pr.cst[:, C_RESET:C_RESET + E * G],
                                         tiles[:].rearrange("p e g -> p (e g)"), 0.0, ALU.mult, ALU.add))
            ch.link(v.tensor_tensor(excl[:].rearrange("p g e -> p e g"), scan[:], tiles[:], ALU.subtract))
            ch.link(v.tensor_tensor(excl[:], ph[0][:].rearrange("p (g e) -> p g e", e=E), excl[:], ALU.add))
            ch.link(v.tensor_tensor(S1[:], excl[:], row_e(C_BASE), ALU.add))
            ch.link(v.tensor_scalar(excl[:], excl[:], float(CAP), float(NO_ROW), ALU.is_ge, ALU.mult))
            ch.link(v.tensor_tensor(S1[:], S1[:], excl[:], ALU.add))
            for k in range(K):
                ch.link(v.tensor_tensor(eq[:], hot[:, k], S1[:], ALU.mult))
                ch.link(v.tensor_reduce(slotf[:, k, :], eq[:], AX.X, ALU.add))
            v.tensor_copy(slot[:], slotf[:]).then_inc(routed, 1)


def experts(pr):
    nc, d = pr.nc, pr.d
    with ExitStack() as ctx:
        sb = lambda name, shape, dt=F32: ctx.enter_context(nc.sbuf_tensor(name, shape, dt))
        sem = pr.sem
        ph = [ctx.enter_context(nc.psum_tensor(f"ph_{f}", [P, BT], F32)) for f in range(FC)]
        pt = [ctx.enter_context(nc.psum_tensor(f"pt_{c}", [P, BT], F32)) for c in range(DC)]
        py = [ctx.enter_context(nc.psum_tensor(f"py_{c}", [P, 2, D], F32)) for c in range(TB // 2)]
        w1, w2 = sb("w1e", [P, DC, F]), sb("w2e", [P, FC, D])
        w1h, w1l = ([sb(f"{n}{k}", [P, DC, F], F32R) for k in range(2)] for n in ("w1h", "w1l"))
        w2h, w2l = ([sb(f"{n}{k}", [P, FC, D], F32R) for k in range(2)] for n in ("w2h", "w2l"))
        xr = [sb(f"xr{k}", [P, TB, ROW]) for k in range(NX)]
        xT = sb("xTe", [P, DC, BT])
        xh, xl = sb("xh", [P, DC, BT], F32R), sb("xl", [P, DC, BT], F32R)
        h = [sb(f"h{k}", [P, FC, BT]) for k in range(2)]
        hh, hl = ([sb(f"{n}{k}", [P, FC, BT], F32R) for k in range(2)] for n in ("hh", "hl"))
        y = [sb(f"y{k}", [P, TB, D]) for k in range(2)]

        w_in, w_split = sem("w_in"), sem("w_split")
        x_in = [sem(f"xr_in{k}") for k in range(NX)]
        added, settled = sem("added"), sem("settled")
        turned, xh_did, xl_did = sem("turned"), sem("xh_did"), sem("xl_did")
        fc1_did, gelu_did, hl_did = sem("fc1_did"), sem("gelu_did"), sem("hl_did")
        fc2_did, y_did = sem("fc2_did"), sem("y_did")
        STEPS = 2 * NB
        PAIRS = E // 2
        number = lambda ep, n: ep * STEPS + n
        pieces = [(w1, w1h, w1l, 0), (w1, w1h, w1l, 1), (w2, w2h, w2l, 0), (w2, w2h, w2l, 1)]

        block = ctx.enter_context(nc.Block())

        @block.sync
        def _(sp):
            src = pr.slots.rearrange("(n t p) c -> n p t c", t=TB, p=P)
            w1_d = d["L0_ffn_moe_w1"].rearrange("e (c p) f -> e p c f", p=P)
            w2_d = d["L0_ffn_moe_w2"].rearrange("e (c p) n -> e p c n", p=P)

            def load_w(e):
                for dst, w in ((w1, w1_d), (w2, w2_d)):
                    sp.dma_start(dst[:], w[bass.ds(e, 1)].rearrange("a p c f -> p (a c) f")).then_inc(w_in, 16)

            def load_x(m, buf):
                sp.wait_ge(settled, m + 1)
                sp.sem_inc(pr.passed, 1)
                sp.dma_start(xr[buf][:], src[bass.ds(m, 1)].rearrange("a p t c -> p (a t) c")
                             ).then_inc(x_in[buf], 16)

            load_w(0)
            sp.sem_inc(settled, NX)
            with sp.Fori(0, PAIRS) as ep:
                for n in range(STEPS):
                    if n % NB == W_AT:
                        sp.wait_ge(w_split, (ep * 2 + n // NB + 1) * 2 * len(pieces))
                        sp.sem_inc(pr.passed, 1)
                        load_w(ep * 2 + n // NB + 1)
                    load_x(number(ep, n), n % NX)
            for m in range(PAIRS * STEPS, PAIRS * STEPS + AHEAD):
                load_x(m, m % NX)
            for m in range(PAIRS * STEPS, PAIRS * STEPS + AHEAD):
                sp.wait_ge(x_in[m % NX], 16 * (m // NX + 1))

        @block.gpsimd
        def _(pool):
            g = nc.gpsimd
            out = d["out"].rearrange("t s n -> (t s) n")
            with pool.Fori(0, PAIRS) as ep:
                for n in range(STEPS):
                    pool.wait_ge(y_did, number(ep, n) + 2)
                    pool.sem_inc(pr.passed, 1)
                    for t in range(TB):
                        g.indirect_dma_start(
                            out=out, out_offset=bass.IndirectOffsetOnAxis(
                                ap=xr[n % NX][:, t, D:D + 1].bitcast(I32), axis=0),
                            in_=y[n % 2][:, t, :], in_offset=None, bounds_check=N - 1, oob_is_err=False,
                            compute_op=ALU.add).then_inc(added, 16)
                    pool.wait_ge(added, 16 * TB * (number(ep, n) + 1))
                    pool.sem_inc(settled, 1)

        @block.tensor
        def _(pe):
            t_ = nc.tensor

            def turn_block(m, buf):
                pe.wait_ge(x_in[buf], 16 * (m + 1))
                for c in range(DC):
                    for t in range(TB):
                        ins = turn(nc, pr, pt[c][:, t * P:(t + 1) * P], xr[buf][:, t, c * P:(c + 1) * P])
                ins.then_inc(turned, 1)

            def layer1(m, k, free=True):
                pe.wait_ge(xl_did, m + 1)
                for f in range(FC):
                    if free:
                        pe.wait_ge(gelu_did, (m - 1) * FC + f + 1)
                    for c in range(DC):
                        ins = three(nc, ph[f][:], (w1h[k], w1l[k]), (xh, xl), lambda w: w[:, c, f * P:(f + 1) * P],
                                    lambda x: x[:, c, :], c == 0, c == DC - 1)
                    ins.then_inc(fc1_did, 1)

            def layer2(m, n, k):
                pe.wait_ge(hl_did, (m + 1) * FC)
                pe.wait_ge(y_did, m + 1)
                for t in range(TB):
                    for f in range(FC):
                        ins = three(nc, py[t // 2][:, t % 2, :], (hh[n % 2], hl[n % 2]), (w2h[k], w2l[k]),
                                    lambda x: x[:, f, t * P:(t + 1) * P], lambda w: w[:, f, :],
                                    f == 0, f == FC - 1)
                    if t % 2:
                        ins.then_inc(fc2_did, 1)

            pe.sem_inc(y_did, 1)
            turn_count = lambda ep, n: ep * (STEPS // NX) + n // NX
            turn_block(0, 0)
            pe.wait_ge(w_split, 4)
            layer1(0, 0, free=False)
            turn_block(0, 1)
            with pe.Fori(0, PAIRS) as ep:
                for n in range(STEPS):
                    e = ep * 2 + n // NB
                    if n % NB == NB - 1:
                        pe.wait_ge(w_split, (e + 1) * 8 + 4)
                    layer1(number(ep, n) + 1, (n + 1) // NB % 2)
                    turn_block(turn_count(ep, n + 2), (n + 2) % NX)
                    if n % NB == 0:
                        pe.wait_ge(w_split, (e + 1) * 8)
                    layer2(number(ep, n), n, n // NB)

        @block.scalar
        def _(act):
            a = nc.scalar

            def features(m):
                act.wait_ge(turned, m + 1)
                for out in (xh, xT):
                    for c in range(DC):
                        ins = a.activation(out[:, c, :], pt[c][:], ACT.Identity,
                                           scale=pr.ln2[:, 0, c:c + 1], bias=pr.ln2[:, 1, c:c + 1])
                ins.then_inc(xh_did, 1)

            def gelu(m, n):
                for f in range(FC):
                    act.wait_ge(fc1_did, m * FC + f + 1)
                    a.activation(hh[n % 2][:, f, :], ph[f][:], ACT.Gelu_apprx_tanh)
                    a.activation(h[n % 2][:, f, :], ph[f][:], ACT.Gelu_apprx_tanh).then_inc(gelu_did, 1)

            features(0)
            gelu(0, 0)
            features(1)
            with act.Fori(0, PAIRS) as ep:
                for n in range(STEPS):
                    gelu(number(ep, n) + 1, n + 1)
                    features(number(ep, n) + 2)

        @block.vector
        def _(dve):
            v = nc.vector

            def split(e, k, piece):
                src, high, low, half = pieces[piece]
                cols = lambda a: a[:].rearrange("p c n -> p (c n)")[:, half * 512:(half + 1) * 512]
                v.tensor_copy(cols(high[k]), cols(src)).then_inc(w_split, 1)
                dve.wait_ge(w_split, (e * len(pieces) + piece) * 2 + 1)
                v.tensor_tensor(cols(low[k]), cols(src), cols(high[k]).bitcast(F32), ALU.subtract
                                ).then_inc(w_split, 1)

            def x_rest(m):
                dve.wait_ge(xh_did, m + 1)
                v.tensor_tensor(xl[:], xT[:], xh[:].bitcast(F32), ALU.subtract).then_inc(xl_did, 1)

            def h_rest(m, n):
                for f in range(FC):
                    dve.wait_ge(gelu_did, m * FC + f + 1)
                    v.tensor_tensor(hl[n % 2][:, f, :], h[n % 2][:, f, :], hh[n % 2][:, f, :].bitcast(F32),
                                    ALU.subtract).then_inc(hl_did, 1)

            dve.wait_ge(w_in, 32)
            for piece in (0, 1):
                split(0, 0, piece)
            x_rest(0)
            for piece in (2, 3):
                split(0, 0, piece)
            h_rest(0, 0)
            x_rest(1)
            with dve.Fori(0, PAIRS) as ep:
                for n in range(STEPS):
                    m = number(ep, n)
                    h_rest(m + 1, n + 1)
                    x_rest(m + 2)
                    dve.wait_ge(settled, m + NX - 1)
                    for half in range(TB // 2):
                        dve.wait_ge(fc2_did, m * 2 + half + 1)
                        dve.sem_inc(pr.passed, 1)
                        for t in (2 * half, 2 * half + 1):
                            ins = v.tensor_scalar(
                                y[n % 2][:, t, :], py[half][:, t % 2, :],
                                xr[n % NX][:, t, bass.ds(ep * 2 + (D + 1 + n // NB), 1)], None, ALU.mult)
                    ins.then_inc(y_did, 1)
                    if n % NB > 0:
                        if n % NB == 1:
                            dve.wait_ge(w_in, 32 * (ep * 2 + n // NB + 2))
                        split(ep * 2 + n // NB + 1, (n // NB + 1) % 2, n % NB - 1)


_INS = ["x", "cond_1024", "L0_cond_W1", "L0_cond_b1", "L0_cond_W2", "L0_cond_b2", "L0_attn_Wq", "L0_attn_Wk",
        "L0_attn_Wv", "L0_attn_Wo", "L0_cond2_base_layer", "L0_cond2_w1", "L0_cond2_b1", "L0_cond2_w2",
        "L0_cond2_b2", "L0_cond2_ln_g", "L0_cond2_ln_b", "L0_ffn_ln1_weight", "L0_ffn_ln1_bias",
        "L0_ffn_ln2_weight", "L0_ffn_ln2_bias", "L0_ffn_qkv_weight", "L0_ffn_proj_weight",
        "L0_ffn_router_weight", "L0_ffn_moe_w1", "L0_ffn_moe_w2"]


def program(nc, dram):
    with ExitStack() as ctx:
        pr = Program(nc, ctx, dram)
        setup(pr)
        with ExitStack() as inner:
            kept = inner.enter_context(nc.sbuf_tensor("kept", [P, G, (DC + 1) * P], F32))
            pr.q = kept[:, :, 0:DC * P].rearrange("p g (c t s) -> p c g t s", c=DC, t=TG)
            pr.kv = kept[:, :, DC * P:].rearrange("p g (t s) -> p g t s", t=TG)
            pr.rows = kept[:, :, 0:ROW]
            pr.logits = inner.enter_context(nc.sbuf_tensor("logits", [P, G, E], F32))
            sequences(pr)
            positions(pr)
            dispatch(pr)
        experts(pr)


def kernel(**inputs):
    import concourse.bacc as bacc
    from concourse.bass_utils import run_bass_kernel_spmd

    nc = bacc.Bacc("TRN2", target_bir_lowering=False, num_devices=1)
    table, tok = constants()
    arrays = {name: np.ascontiguousarray(inputs[name]) for name in _INS}
    for name, a in arrays.items():
        if a.shape == (D,):
            arrays[name] = np.ascontiguousarray(a.reshape(DC, P).transpose(1, 0))
    by_rows = lambda a: np.ascontiguousarray(a.reshape(DC, P, -1).transpose(1, 0, 2))
    for name in ("L0_cond_W1", "L0_cond_W2", "L0_attn_Wo"):
        arrays[name] = by_rows(arrays[name].T)
    arrays["condT"] = by_rows(arrays["cond_1024"].T)
    arrays["xT"] = np.ascontiguousarray(arrays["x"].transpose(0, 2, 1).reshape(S, DC, P, T).transpose(0, 2, 1, 3))
    proj = arrays["L0_ffn_proj_weight"].reshape(D, NKV, JQ // 2, 2, HD)
    arrays["L0_ffn_proj_weight"] = np.ascontiguousarray(proj.transpose(3, 1, 4, 2, 0).reshape(P, DC, D))
    qkv = arrays["L0_ffn_qkv_weight"].reshape(NKV, JQ + 2, HD, DC, P)
    arrays["L0_ffn_qkv_weight"] = np.ascontiguousarray(qkv.transpose(4, 3, 1, 0, 2).reshape(P, DC, QKV))
    for name in ("L0_ffn_moe_w1", "L0_ffn_moe_w2"):
        arrays[name] = np.concatenate([arrays[name], arrays[name][:1]])
    b2 = arrays["L0_cond2_b2"].reshape(2, DC, P, RANK)
    arrays["L0_cond2_b2"] = np.ascontiguousarray(b2.transpose(2, 0, 1, 3))
    arrays["cst"], arrays["tok"] = table, tok
    dram = {name: nc.dram_tensor(f"in_{name}", a.shape, mybir.dt.from_np(a.dtype), kind="ExternalInput").ap()
            for name, a in arrays.items()}
    dram["out"] = nc.dram_tensor("out_rows", (T, S, D), F32, kind="ExternalOutput").ap()
    program(nc, dram)
    arrays = {f"in_{name}": a for name, a in arrays.items()}
    r = run_bass_kernel_spmd(nc, [arrays], core_ids=[0])
    return np.ascontiguousarray(r.results[0]["out_rows"].transpose(1, 0, 2))
```
